# Optimizing a Trainium2 kernel written in Bass

```python
import numpy as np
import jax
import jax.numpy as jnp

def _softmax(x, axis=-1):
    return jax.nn.softmax(x, axis=axis)

def _gelu(x):
    return jax.nn.gelu(x, approximate=True)

def _silu(x):
    return jax.nn.silu(x)

def _sigmoid(x):
    return jax.nn.sigmoid(x)

def _layernorm(x, axis=-1, eps=1e-05):
    m = jnp.mean(x, axis=axis, keepdims=True)
    v = jnp.var(x, axis=axis, keepdims=True)
    return (x - m) / jnp.sqrt(v + eps)

def _scatter_add(tgt, idx, src, axis=0):
    return tgt.at[idx].add(src)

def _segment_sum(src, seg, n):
    return jax.ops.segment_sum(src, seg, n)
kernel_name = 'mk_perceiver_d1_seqx_r2_3bd1bc'

def setup_inputs(seed: int=0):
    np.random.seed(seed)
    _w = jnp.asarray

    def _rec_inputs():
        import jax
        import jax.numpy as jnp
        _rk = jax.random.key(seed)
        x = -0.0002928 + 1 * jax.random.normal(jax.random.fold_in(_rk, 1), (4, 128, 512), jnp.float32)
        _lenS = 128 - jax.random.randint(jax.random.fold_in(_rk, 7), (4,), 0, max(1, 128 // 4) + 1, jnp.int32)
        _lenS2 = 2048 - jax.random.randint(jax.random.fold_in(_rk, 8), (4,), 0, max(1, 2048 // 4) + 1, jnp.int32)
        _ctx_1024P = jax.random.normal(jax.random.fold_in(_rk, 11), (4, 16, 512), jnp.float32)
        _ctx_1024c = jax.random.dirichlet(jax.random.fold_in(_rk, 511), 0.3 * jnp.ones((16,), jnp.float32), (4, 2048))
        _ctx_1024t = jnp.einsum('bsk,bkd->bsd', _ctx_1024c, _ctx_1024P)
        _ctx_1024t = _ctx_1024t * jax.lax.rsqrt(jnp.mean(jnp.square(_ctx_1024t)) + 1e-12) * 0.953939
        ctx_1024 = -1.39393e-06 + 0.999914 * (_ctx_1024t + 0.3 * jax.random.normal(jax.random.fold_in(_rk, 611), (4, 2048, 512), jnp.float32))
        _validS = jnp.arange(128)[None, :] < _lenS[:, None]
        _validS2 = jnp.arange(2048)[None, :] < _lenS2[:, None]
        _causal = jnp.tril(jnp.ones((128, 128), dtype=bool))
        mask_1x1xSxS2_ik0 = jnp.where(jnp.broadcast_to(_validS2[0:1, None, None, :], (1, 1, 128, 2048)), 0, 1).astype(jnp.int32)
        return (x, ctx_1024, mask_1x1xSxS2_ik0)
    x, ctx_1024, mask_1x1xSxS2_ik0 = _rec_inputs()

    def _L0_xattn_setup():
        import jax, jax.numpy as jnp
        import numpy as np
        B, N, DIM, H = (2, 1024, 512, 16)
        HD = DIM // H
        SCALE = HD ** (-0.5)

        def _split_heads(x):
            b, n, _ = x.shape
            return x.reshape(b, n, H, HD).transpose(0, 2, 1, 3)
        key = jax.random.key(seed)
        ks = jax.random.split(key, 11)
        std = DIM ** (-0.5)
        inp = {'q': jax.random.normal(ks[0], (B, N, DIM), jnp.float32), 'k': jax.random.normal(ks[1], (B, N, DIM), jnp.float32), 'v': jax.random.normal(ks[2], (B, N, DIM), jnp.float32), 'mask': jnp.tril(jnp.ones((N, N), jnp.int32))[None, None], 'Wq': jax.random.normal(ks[3], (DIM, DIM), jnp.float32) * std, 'bq': jnp.zeros((DIM,), jnp.float32), 'Wk': jax.random.normal(ks[4], (DIM, DIM), jnp.float32) * std, 'bk': jnp.zeros((DIM,), jnp.float32), 'Wv': jax.random.normal(ks[5], (DIM, DIM), jnp.float32) * std, 'bv': jnp.zeros((DIM,), jnp.float32), 'Wo': jax.random.normal(ks[6], (DIM, DIM), jnp.float32) * std, 'bo': jnp.zeros((DIM,), jnp.float32)}
        return inp
    _L0_xattn_all = _L0_xattn_setup()
    _L0_xattn_in = {k: v for k, v in _L0_xattn_all.items() if k in ('Wq', 'bq', 'Wk', 'bk', 'Wv', 'bv', 'Wo', 'bo')}
    del _L0_xattn_all

    def _L0_attn_setup():
        import jax, jax.numpy as jnp
        import numpy as np
        NUM_HEADS = 16
        LN_EPS = 1e-05
        key = jax.random.key(seed)
        ks = jax.random.split(key, 5)
        B, S, E = (4, 512, 512)
        x = jax.random.normal(ks[0], (B, S, E), dtype=jnp.float32)
        Wq = jax.random.normal(ks[1], (E, E), dtype=jnp.float32) * E ** (-0.5)
        Wk = jax.random.normal(ks[2], (E, E), dtype=jnp.float32) * E ** (-0.5)
        Wv = jax.random.normal(ks[3], (E, E), dtype=jnp.float32) * E ** (-0.5)
        Wo = jax.random.normal(ks[4], (E, E), dtype=jnp.float32) * E ** (-0.5)
        gamma = jnp.ones((E,), dtype=jnp.float32)
        beta = jnp.zeros((E,), dtype=jnp.float32)
        return {'x': x, 'Wq': Wq, 'Wk': Wk, 'Wv': Wv, 'Wo': Wo, 'gamma': gamma, 'beta': beta}
    _L0_attn_all = _L0_attn_setup()
    _L0_attn_in = {k: v for k, v in _L0_attn_all.items() if k in ('Wq', 'Wk', 'Wv', 'Wo', 'gamma', 'beta')}
    del _L0_attn_all

    def _L0_ffn_setup():
        import jax, jax.numpy as jnp
        import numpy as np
        GROUP = 16
        EPS = 1e-05

        def _dequant(q, scale):
            w = q.astype(jnp.float32) / 7.5 - 1.0
            return w * jnp.repeat(scale, GROUP, axis=1)

        def _qlora_linear(x, q, scale, bias, la, lb):
            w = _dequant(q, scale)
            base = jnp.einsum('btd,od->bto', x, w) + bias
            lora = jnp.einsum('btr,or->bto', jnp.einsum('btd,rd->btr', x, la), lb)
            return base + lora

        def _layernorm(x, g, b):
            mu = jnp.mean(x, axis=-1, keepdims=True)
            var = jnp.mean(jnp.square(x - mu), axis=-1, keepdims=True)
            return (x - mu) * jax.lax.rsqrt(var + EPS) * g + b
        key = jax.random.key(seed)
        ks = jax.random.split(key, 6)
        D, R, B, T = (512, 32, 8, 2048)
        x = jax.random.normal(ks[0], (B, T, D), dtype=jnp.float32)
        qweights = jax.random.randint(ks[1], (6, D, D), 0, 16, dtype=jnp.int32)
        scales = jax.random.uniform(ks[2], (6, D, D // GROUP), dtype=jnp.float32)
        biases = jax.random.normal(ks[3], (6, D), dtype=jnp.float32) * 0.02
        lora_a = jax.random.normal(ks[4], (6, R, D), dtype=jnp.float32) * 0.02
        lora_b = jax.random.normal(ks[5], (6, D, R), dtype=jnp.float32) * 0.02
        ln_gamma = jnp.ones((3, D), dtype=jnp.float32)
        ln_beta = jnp.zeros((3, D), dtype=jnp.float32)
        return {'x': x, 'qweights': qweights, 'scales': scales, 'biases': biases, 'lora_a': lora_a, 'lora_b': lora_b, 'ln_gamma': ln_gamma, 'ln_beta': ln_beta}
    _L0_ffn_all = _L0_ffn_setup()
    _L0_ffn_in = {k: v for k, v in _L0_ffn_all.items() if k in ('qweights', 'scales', 'biases', 'lora_a', 'lora_b', 'ln_gamma', 'ln_beta')}
    del _L0_ffn_all
    return {'x': x, 'ctx_1024': ctx_1024, 'mask_1x1xSxS2_ik0': mask_1x1xSxS2_ik0, 'L0_xattn_Wq': _L0_xattn_in['Wq'], 'L0_xattn_bq': _L0_xattn_in['bq'], 'L0_xattn_Wk': _L0_xattn_in['Wk'], 'L0_xattn_bk': _L0_xattn_in['bk'], 'L0_xattn_Wv': _L0_xattn_in['Wv'], 'L0_xattn_bv': _L0_xattn_in['bv'], 'L0_xattn_Wo': _L0_xattn_in['Wo'], 'L0_xattn_bo': _L0_xattn_in['bo'], 'L0_attn_Wq': _L0_attn_in['Wq'], 'L0_attn_Wk': _L0_attn_in['Wk'], 'L0_attn_Wv': _L0_attn_in['Wv'], 'L0_attn_Wo': _L0_attn_in['Wo'], 'L0_attn_gamma': _L0_attn_in['gamma'], 'L0_attn_beta': _L0_attn_in['beta'], 'L0_ffn_qweights': _L0_ffn_in['qweights'], 'L0_ffn_scales': _L0_ffn_in['scales'], 'L0_ffn_biases': _L0_ffn_in['biases'], 'L0_ffn_lora_a': _L0_ffn_in['lora_a'], 'L0_ffn_lora_b': _L0_ffn_in['lora_b'], 'L0_ffn_ln_gamma': _L0_ffn_in['ln_gamma'], 'L0_ffn_ln_beta': _L0_ffn_in['ln_beta']}

def reference(x, ctx_1024, mask_1x1xSxS2_ik0, L0_xattn_Wq, L0_xattn_bq, L0_xattn_Wk, L0_xattn_bk, L0_xattn_Wv, L0_xattn_bv, L0_xattn_Wo, L0_xattn_bo, L0_attn_Wq, L0_attn_Wk, L0_attn_Wv, L0_attn_Wo, L0_attn_gamma, L0_attn_beta, L0_ffn_qweights, L0_ffn_scales, L0_ffn_biases, L0_ffn_lora_a, L0_ffn_lora_b, L0_ffn_ln_gamma, L0_ffn_ln_beta):
    import jax
    import jax.numpy as jnp

    def _L0_xattn_ref(q, k, v, mask, Wq, bq, Wk, bk, Wv, bv, Wo, bo):
        import jax, jax.numpy as jnp
        import numpy as np
        B, N, DIM, H = (2, 1024, 512, 16)
        HD = DIM // H
        SCALE = HD ** (-0.5)

        def _split_heads(x):
            b, n, _ = x.shape
            return x.reshape(b, n, H, HD).transpose(0, 2, 1, 3)
        qh = _split_heads(q @ Wq.T + bq)
        kh = _split_heads(k @ Wk.T + bk)
        vh = _split_heads(v @ Wv.T + bv)
        attn = jnp.einsum('bhqc,bhkc->bhqk', qh, kh) * SCALE
        attn = jnp.where(mask == 0, -jnp.inf, attn)
        attn = jax.nn.softmax(attn, axis=-1)
        out = jnp.einsum('bhqk,bhkc->bhqc', attn, vh)
        b, h, n, c = out.shape
        out = out.transpose(0, 2, 1, 3).reshape(b, n, h * c)
        return out @ Wo.T + bo

    def _L0_attn_ref(x, Wq, Wk, Wv, Wo, gamma, beta):
        import jax, jax.numpy as jnp
        import numpy as np
        NUM_HEADS = 16
        LN_EPS = 1e-05
        B, S, E = x.shape
        H = NUM_HEADS
        D = E // H
        scale = 1.0 / D ** 0.5
        q = x @ Wq.T
        k = x @ Wk.T * scale
        v = x @ Wv.T
        qh = q.reshape(B, S, H, D)
        kh = k.reshape(B, S, H, D)
        qk = jnp.einsum('bthd,bshd->bhts', qh, kh)
        causal = jnp.tril(jnp.ones((S, S), dtype=bool))
        qk = jnp.where(causal, qk, -jnp.inf)
        attn = jax.nn.softmax(qk, axis=-1)
        vh = v.reshape(B, S, D, H)
        qkv = jnp.einsum('bsdh,bhts->bthd', vh, attn)
        qkv = qkv.reshape(B, S, E)
        mu = jnp.mean(qkv, axis=-1, keepdims=True)
        var = jnp.mean(jnp.square(qkv - mu), axis=-1, keepdims=True)
        ln = (qkv - mu) * jax.lax.rsqrt(var + LN_EPS) * gamma + beta
        return ln @ Wo.T

    def _L0_ffn_ref(x, qweights, scales, biases, lora_a, lora_b, ln_gamma, ln_beta):
        import jax, jax.numpy as jnp
        import numpy as np
        GROUP = 16
        EPS = 1e-05

        def _dequant(q, scale):
            w = q.astype(jnp.float32) / 7.5 - 1.0
            return w * jnp.repeat(scale, GROUP, axis=1)

        def _qlora_linear(x, q, scale, bias, la, lb):
            w = _dequant(q, scale)
            base = jnp.einsum('btd,od->bto', x, w) + bias
            lora = jnp.einsum('btr,or->bto', jnp.einsum('btd,rd->btr', x, la), lb)
            return base + lora

        def _layernorm(x, g, b):
            mu = jnp.mean(x, axis=-1, keepdims=True)
            var = jnp.mean(jnp.square(x - mu), axis=-1, keepdims=True)
            return (x - mu) * jax.lax.rsqrt(var + EPS) * g + b
        h = x
        for blk in range(3):
            i0, i1 = (2 * blk, 2 * blk + 1)
            y = _qlora_linear(h, qweights[i0], scales[i0], biases[i0], lora_a[i0], lora_b[i0])
            y = _layernorm(y, ln_gamma[blk], ln_beta[blk])
            y = jax.nn.gelu(y, approximate=False)
            y = _qlora_linear(y, qweights[i1], scales[i1], biases[i1], lora_a[i1], lora_b[i1])
            h = y + h
        return h
    x = x + _L0_xattn_ref(_layernorm(x, axis=-1), ctx_1024, ctx_1024, mask_1x1xSxS2_ik0, L0_xattn_Wq, L0_xattn_bq, L0_xattn_Wk, L0_xattn_bk, L0_xattn_Wv, L0_xattn_bv, L0_xattn_Wo, L0_xattn_bo)
    x = x + _L0_attn_ref(_layernorm(x, axis=-1), L0_attn_Wq, L0_attn_Wk, L0_attn_Wv, L0_attn_Wo, L0_attn_gamma, L0_attn_beta)
    x = x + _L0_ffn_ref(_layernorm(x, axis=-1), L0_ffn_qweights, L0_ffn_scales, L0_ffn_biases, L0_ffn_lora_a, L0_ffn_lora_b, L0_ffn_ln_gamma, L0_ffn_ln_beta)
    return x

_drawn_inputs = setup_inputs


def setup_inputs(seed=0):
    import zlib

    import numpy as np

    out = dict(_drawn_inputs(seed))
    spreads = {'L0_xattn_bq': (0.0, 0.287),
     'L0_xattn_bk': (0.0, 0.8),
     'L0_xattn_bv': (0.0, 0.1),
     'L0_xattn_bo': (0.0, 0.1),
     'L0_attn_gamma': (1.0, 0.2),
     'L0_attn_beta': (0.0, 0.1),
     'L0_ffn_ln_gamma': (1.0, 0.2),
     'L0_ffn_ln_beta': (0.0, 0.1)}
    factors = {'L0_ffn_biases': 8.0, 'L0_ffn_lora_a': 4.937, 'L0_ffn_lora_b': 4.879}
    for name, (base, spread) in spreads.items():
        noise = np.random.default_rng([zlib.crc32(name.encode()), seed]).standard_normal(out[name].shape)
        drawn = base * np.exp(spread * noise) if base else spread * noise
        out[name] = jnp.asarray(drawn.astype(out[name].dtype))
    for name, factor in factors.items():
        out[name] = (out[name] * factor).astype(out[name].dtype)
    return out
```

```python
from contextlib import ExitStack
import math

import numpy as np

import concourse.bass as bass
from concourse import mybir

ALU = mybir.AluOpType
ACT = mybir.ActivationFunctionType
AX = mybir.AxisListType
F32 = mybir.dt.float32
F32R = mybir.dt.float32r
F16 = mybir.dt.float16
BF16 = mybir.dt.bfloat16
I32 = mybir.dt.int32

P = 128
B = 4
D = 512
KD = D // P
H = 16
HD = D // H
S2 = 2048
NKC = S2 // 512
NI = 2 * B
HI = H // 2
VW = 3 * HD + 2
SCALE = HD ** -0.5
NEG = -1.0e30
LN_EPS = 1e-5
PSHIFT = math.log(4096.0)
LEAD = 6
LAG = 2
NG = HI * NKC
PTR = 4
NBLK = 3
NU = B * H // 4
FFN_STEPS = 33
DEQ = 1.0 / 7.5
WXO, WQ, WK, WV, WAO = range(5)
SLOT = [0, 1, 2, 0, 1]
SLOT0, SLOT1 = 2, 0


def wait(eng, sem, value):
    if not (isinstance(value, int) and value <= 0):
        eng.wait_ge(sem, value)


def wait_apart(eng, sem, value, passed):
    if not (isinstance(value, int) and value <= 0):
        eng.wait_ge(sem, value)
        eng.sem_inc(passed, 1)


class Steps:

    def __init__(self, eng, sem, base):
        self.eng, self.sem, self.base, self.n = eng, sem, base, 0

    def mark(self, ins):
        self.n += 1
        ins.then_inc(self.sem, 1)
        return self.base + self.n

    def need(self, value):
        self.eng.wait_ge(self.sem, value)


def build(nc, x, ctxT, mask, wqT, wkT, wvT, woT, bq, bk, bv, bo,
          aqT, akT, avT, aoT, a_gamma, a_beta, fqT, fsT, f_bias, f_la, f_lbT, f_gamma, f_beta, out):
    ctx = ExitStack()
    with ctx:
        def sb(name, shape, dt, st=ctx):
            return st.enter_context(nc.sbuf_tensor(name, shape, dt))

        def sem(name):
            return ctx.enter_context(nc.semaphore(name))

        ps = ctx.enter_context(nc.psum_tensor("ps", [P, 8, 512], F32))

        ident = sb("ident", [P, P], F32)
        causal = sb("causal", [P, P], F32)
        rowmask = sb("rowmask", [P, 4], F32)
        x_sb = sb("x_sb", [P, B, D], F32)
        o_tok = sb("o_tok", [P, B, D], F32)
        b_q = sb("b_q", [P, KD], F32)
        b_k = sb("b_k", [P, 2, KD], F32)
        b_kf = b_k[:].rearrange("p a m -> p (a m)")
        b_kn = sb("b_kn", [P, 2], F32)
        b_v = sb("b_v", [P, KD], F32)
        g_a = sb("g_a", [P, KD], F32)
        be_a = sb("be_a", [P, KD], F32)
        g_f = sb("g_f", [P, NBLK, KD], F32)
        be_f = sb("be_f", [P, NBLK, KD], F32)
        bo_bc = sb("bo_bc", [P, D], F32)
        stats = sb("stats", [P, B, 6], F32)
        mv = sb("mv", [P, B, 2], F32)
        ve = sb("ve", [P, B], F32)
        rs = sb("rs", [P, B], F32)
        rt = sb("rt", [P, B], F32)
        nanfix = sb("nanfix", [P, 4], F32)
        mx = sb("mx", [P, 2, 2], F32)
        nb = sb("nb", [P, 2, 4], F32)
        rc = sb("rc", [P, 4], F32)
        osum = sb("osum", [P, 4, HD], F32)
        mx2 = sb("mx2", [P, 4], F32)

        st1 = ExitStack()
        craw = sb("craw", [P, 2, KD, 512], F32, st1)
        chi = sb("chi", [P, 2, KD, 512], F32R, st1)
        clo = sb("clo", [P, 2, KD, 512], F32R, st1)
        wraw = sb("wraw", [P, 2, KD, 256], F32, st1)
        whi = sb("whi", [P, 2, KD, 256], F32R, st1)
        wlo = sb("wlo", [P, 2, KD, 256], F32R, st1)
        khi = sb("khi", [P, 2, S2], F32R, st1)
        klo = sb("klo", [P, 2, S2], F32R, st1)
        qthi = sb("qthi", [P, KD, D], F32R, st1)
        qtlo = sb("qtlo", [P, KD, D], F32R, st1)
        qzhi = sb("qzhi", [P, HI, P], F32R, st1)
        qzlo = sb("qzlo", [P, HI, P], F32R, st1)
        vh = sb("vh", [P, S2 // P, HI, VW], BF16, st1)
        vrest = sb("vrest", [P, 2, 512], F32, st1)
        sm = sb("sm", [P, 2, S2], F32, st1)
        pthi = sb("pthi", [P, PTR, 4, P], F16, st1)
        ptlo = sb("ptlo", [P, PTR, 4, P], F16, st1)
        mbias = sb("mbias", [P, S2], BF16, st1)
        xnT_hi = khi[:, 0, :].rearrange("p (k t) -> p k t", k=KD)
        xnT_lo = klo[:, 0, :].rearrange("p (k t) -> p k t", k=KD)
        xn0 = sm[:, 0, :].rearrange("p (b d) -> p b d", b=B)
        mraw = sm[:, 1, :].bitcast(I32)
        st1.close()

        st2 = ExitStack()
        raw = sb("raw", [P, 2, KD, 512], F32, st2)
        Whi = sb("Whi", [P, 3, KD, 512], F32R, st2)
        Wlo = sb("Wlo", [P, 3, KD, 512], F32R, st2)
        aThi = sb("aThi", [P, KD, D], F32R, st2)
        aTlo = sb("aTlo", [P, KD, D], F32R, st2)
        tok = sb("tok", [P, B, D], F32, st2)
        g32 = sb("g32", [P, KD, D], F32, st2)
        dq_scale = sb("dq_scale", [P, KD, 512], F32, st2)
        dq_w = sb("dq_w", [P, KD, 512], F32, st2)
        la_sb = sb("la_sb", [32, D], F32, st2)
        lb_sb = sb("lb_sb", [32, D], F32, st2)
        st3 = ExitStack()
        qz2 = sb("qz2", [P, KD, 4, D], F32, st3)
        kT2 = sb("kT2", [P, KD, D], F32, st3)
        vh2 = sb("vh2", [P, B, H, VW], BF16, st3)
        vrest2 = sb("vrest2", [P, 2, 512], F32, st3)
        sm2 = sb("sm2", [P, 2, 4, P], F32, st3)
        pthi2 = sb("pthi2", [P, 2, 4, P], F16, st3)
        ptlo2 = sb("ptlo2", [P, 2, 4, P], F16, st3)
        st3.close()
        st4 = ExitStack()
        h_tok = sb("h_tok", [P, B, D], F32, st4)
        f_bc = sb("f_bc", [P, 2 * NBLK, D], F32, st4)
        st4.close()
        st2.close()

        s_x, s_m, s_wq, s_cst = sem("x_loaded"), sem("mask_loaded"), sem("wq_loaded"), sem("bias_loaded")
        s_id = sem("identity_ready")
        s_vec = sem("vector_chain")
        s_xn = sem("xn_ready")
        s_t0 = sem("xn_transposed")
        s_t0h = sem("xnT_hi_ready")
        s_t0l = sem("xnT_lo_ready")
        s_wq_hi, s_wq_lo = sem("wq_hi_ready"), sem("wq_lo_ready")
        s_q = sem("q_mm_done")
        s_qh, s_ql = sem("q_hi_ready"), sem("q_lo_ready")
        s_w = sem("kv_weights_loaded")
        s_w_hi, s_w_lo = sem("kv_weights_hi"), sem("kv_weights_lo")
        s_c = [sem("ctx_loaded0"), sem("ctx_loaded1")]
        s_c_hi, s_c_lo = sem("ctx_hi"), sem("ctx_lo")
        kv_mm = sem("kv_mm_done")
        kv_hi = sem("kv_hi_ready")
        kv_lo = sem("kv_lo_ready")
        v_mid = sem("v_mid_ready")
        v_all = sem("v_parts_ready")
        q_slots = sem("q_slots_ready")
        scores = sem("scores_done")
        masked = sem("scores_masked")
        nbias = sem("neg_max_ready")
        exps = sem("exp_done")
        tps = sem("weights_transposed")
        pt_hi, pt_lo = sem("weights_hi_ready"), sem("weights_lo_ready")
        pv = sem("pv_done")
        o_ready = sem("attn_out_ready")
        bk_now = sem("k_bias_in_place")
        passed_sp, passed_dve = sem("passed_sp"), sem("passed_dve")
        s_raw = [sem("raw_loaded0"), sem("raw_loaded1")]
        s_Whi, s_Wlo = sem("W_hi_ready"), sem("W_lo_ready")
        s_lin = sem("linear_done")
        s_T = sem("act_transposed")
        s_g = sem("act_full_ready")
        s_ah, s_al = sem("act_hi_ready"), sem("act_lo_ready")
        s_res = sem("residual_ready")
        s_tok = sem("tokens_ready")
        s_xb = sem("residual_bias_added")
        s_k2 = sem("self_k_ready")
        s_q2 = sem("self_q_ready")
        s_v1, s_vr, s_v2, s_v3 = sem("self_v_hi"), sem("self_v_rest"), sem("self_v_mid"), sem("self_v_low")
        u_s, u_m, u_nb, u_e = sem("self_scores"), sem("self_masked"), sem("self_neg_max"), sem("self_exp")
        u_t, u_h, u_l, u_pv, u_o = (sem("self_transposed"), sem("self_w_hi"), sem("self_w_lo"),
                                    sem("self_pv"), sem("self_out"))
        s_pre, s_ffn = sem("vector_steps"), sem("vector_ffn_steps")
        s_ones2, s_h, s_fadd = sem("self_v_ones"), sem("h_ready"), sem("lora_added")
        passed_act, passed_pool = sem("passed_act"), sem("passed_pool")
        s_fq = [sem("ffn_levels0"), sem("ffn_levels1")]
        s_fs, s_fl, s_fb = sem("ffn_scale_loaded"), sem("ffn_lora_loaded"), sem("ffn_bias_loaded")
        s_dq1, s_dq2 = sem("dequant_levels"), sem("dequant_scaled")
        s_lora, s_fw = sem("lora_product"), sem("ffn_weight_full")
        s_fhi = sem("ffn_weight_hi")
        s_flo = sem("ffn_weight_lo")
        s_hb = sem("h_bias_added")
        s_out, s_fin = sem("out_stored"), sem("out_ready")

        block = ctx.enter_context(nc.Block())

        ctxT_v = ctxT.rearrange("(k p) t -> p k t", p=P)

        def wview(w):
            return w.rearrange("(k p) o -> p k o", p=P)

        @block.sync
        def _(sp):
            sp.dma_start(x_sb[:], x.rearrange("(b p) d -> p b d", p=P)).then_inc(s_x, 16)
            sp.dma_start(mraw, mask).then_inc(s_m, 16)
            sp.dma_start(craw[:, 1], wview(wqT)).then_inc(s_wq, 16)
            sp.dma_start(craw[:, 0], ctxT_v[:, :, 0:512]).then_inc(s_c[0], 16)

            def load_kv_weights(p):
                wait(sp, s_w_lo, p)
                sp.dma_start(wraw[:, 0], wview(wkT)[:, :, 256 * p:256 * p + 256]).then_inc(s_w, 16)
                sp.dma_start(wraw[:, 1], wview(wvT)[:, :, 256 * p:256 * p + 256]).then_inc(s_w, 16)

            load_kv_weights(0)
            sp.wait_ge(s_wq_lo, 1)
            sp.dma_start(craw[:, 1], ctxT_v[:, :, 512:1024]).then_inc(s_c[1], 16)

            def ctx_load(i, kc):
                wait_apart(sp, s_c_lo, i * 4 + (kc - 1), passed_sp)
                sp.dma_start(craw[:, kc % 2], ctxT_v[:, :, bass.ds((i & 3) * S2 + kc * 512, 512)]
                             ).then_inc(s_c[kc % 2], 16)

            ctx_load(0, 2)
            ctx_load(0, 3)
            load_kv_weights(1)
            with sp.Fori(1, NI) as i:
                for kc in range(NKC):
                    ctx_load(i, kc)
            for n, w in enumerate((woT, aqT, akT, avT, aoT)):
                if n < 2:
                    sp.wait_ge(s_c_lo, NKC * NI)
                else:
                    sp.wait_ge(s_Wlo, n - 1)
                sp.dma_start(raw[:, n % 2], wview(w)).then_inc(s_raw[n % 2], 16)

            def ffn_levels(blk, a):
                if not isinstance(blk, int):
                    wait_apart(sp, s_dq1, 2 * blk + (a - 1), passed_sp)
                sp.dma_start(raw[:, 1 - a].bitcast(I32),
                             fqT[bass.ds(2 * blk + a, 1)].rearrange("one (k p) o -> p (one k) o", p=P)
                             ).then_inc(s_fq[a], 16)

            def ffn_scales(blk, a):
                if a == 1 or not isinstance(blk, int):
                    wait_apart(sp, s_dq2, 2 * blk + a, passed_sp)
                sp.dma_start(dq_scale[:], fsT[bass.ds(2 * blk + a, 1)].rearrange("one (k p) o -> p (one k) o", p=P)
                             ).then_inc(s_fs, 16)

            def ffn_lora(blk, a):
                if a == 1 or not isinstance(blk, int):
                    wait_apart(sp, s_lora, 4 * (2 * blk + a), passed_sp)
                f = bass.ds(2 * blk + a, 1)
                sp.dma_start(la_sb[:], f_la[f].rearrange("one r d -> r (one d)")).then_inc(s_fl, 16)
                sp.dma_start(lb_sb[:], f_lbT[f].rearrange("one r d -> r (one d)")).then_inc(s_fl, 16)

            sp.wait_ge(s_Wlo, 4)
            ffn_levels(0, 0)
            sp.wait_ge(o_ready, 6 * NI)
            ffn_scales(0, 0)
            ffn_lora(0, 0)
            sp.wait_ge(s_Wlo, 5)
            ffn_levels(0, 1)
            ffn_scales(0, 1)
            sp.wait_ge(u_s, NU)
            sp.dma_start(f_bc[:].rearrange("p f d -> p (f d)"),
                         f_bias.rearrange("f d -> (f d)").partition_broadcast(P)).then_inc(s_fb, 16)
            ffn_lora(0, 1)
            with sp.Fori(1, NBLK) as blk:
                for a in range(2):
                    ffn_levels(blk, a)
                    ffn_scales(blk, a)
                    ffn_lora(blk, a)
            out_v = out.rearrange("(b p) d -> p b d", p=P)
            for b in range(B):
                sp.wait_ge(s_fin, b + 1)
                sp.dma_start(out_v[:, b], h_tok[:, b]).then_inc(s_out, 16)
            sp.wait_ge(s_out, 16 * B)

        @block.gpsimd
        def _(pool):
            nc.gpsimd.memset(ident[:], 0.0).then_inc(s_id, 1)
            nc.gpsimd.memset(causal[:], 0.0).then_inc(s_id, 1)
            nc.gpsimd.memset(rowmask[:], 1.0).then_inc(s_id, 1)
            nc.gpsimd.memset(vh[:, :, :, 3 * HD:VW], 1.0).then_inc(s_id, 1)
            nc.gpsimd.memset(qzhi[:].bitcast(F32), 0.0).then_inc(s_id, 1)
            nc.gpsimd.memset(qzlo[:].bitcast(F32), 0.0).then_inc(s_id, 1)
            pool.wait_ge(s_id, 6)
            nc.gpsimd.affine_select(out=ident[:], in_=ident[:], compare_op=ALU.not_equal, fill=1.0, base=0,
                                    pattern=[[-1, P]], channel_multiplier=1).then_inc(s_id, 1)
            nc.gpsimd.affine_select(out=causal[:], in_=causal[:], compare_op=ALU.is_ge, fill=NEG, base=0,
                                    pattern=[[-1, P]], channel_multiplier=1).then_inc(s_id, 1)
            nc.gpsimd.affine_select(out=rowmask[:], in_=rowmask[:], compare_op=ALU.is_ge, fill=0.0, base=0,
                                    pattern=[[-HD, 4]], channel_multiplier=1).then_inc(s_id, 1)
            pool.wait_ge(s_id, 9)
            nc.gpsimd.affine_select(out=rowmask[:], in_=rowmask[:], compare_op=ALU.is_ge, fill=0.0, base=HD - 1,
                                    pattern=[[HD, 4]], channel_multiplier=-1).then_inc(s_id, 1)
            pool.dma_start(b_q[:], bq).then_inc(s_cst, 16)
            pool.dma_start(b_k[:, :, 0:2], bk.rearrange("p (a m) -> p a m", a=2)).then_inc(s_cst, 16)
            pool.dma_start(b_v[:], bv).then_inc(s_cst, 16)
            pool.dma_start(g_a[:], a_gamma).then_inc(s_cst, 16)
            pool.dma_start(be_a[:], a_beta).then_inc(s_cst, 16)
            pool.dma_start(g_f[:], f_gamma).then_inc(s_cst, 16)
            pool.dma_start(be_f[:], f_beta).then_inc(s_cst, 16)
            pool.dma_start(bo_bc[:], bo.partition_broadcast(P)).then_inc(s_cst, 16)

            pool.wait_ge(s_wq_hi, 1)
            nc.gpsimd.tensor_tensor(clo[:, 1], craw[:, 1], chi[:, 1].bitcast(F32), ALU.subtract).then_inc(s_wq_lo, 1)

            def kv_weights_lo(p):
                pool.wait_ge(s_w_hi, p + 1)
                nc.gpsimd.tensor_tensor(wlo[:], wraw[:], whi[:].bitcast(F32), ALU.subtract).then_inc(s_w_lo, 1)

            def ctx_lo(i, kc):
                pool.wait_ge(s_c_hi, 4 * i + (kc + 1))
                nc.gpsimd.tensor_tensor(clo[:, kc % 2], craw[:, kc % 2], chi[:, kc % 2].bitcast(F32),
                                        ALU.subtract).then_inc(s_c_lo, 1)

            def v_low(i, n):
                pool.wait_ge(v_mid, 8 * i + (n + 1))
                v = vh[:, 2 * n:2 * n + 2]
                nc.gpsimd.tensor_tensor(v[:, :, :, 2 * HD:3 * HD],
                                        vrest[:, n % 2].rearrange("p (a h c) -> p a h c", a=2, c=HD),
                                        v[:, :, :, HD:2 * HD], ALU.subtract).then_inc(v_all, 1)

            def iteration(i, prefetch, weights=None):
                for kc in range(NKC):
                    if kc + 2 < NKC:
                        ctx_lo(i, kc + 2)
                    v_low(i, 2 * kc)
                    v_low(i, 2 * kc + 1)
                if weights is not None:
                    kv_weights_lo(weights)
                if prefetch:
                    ctx_lo(i + 1, 0)
                    ctx_lo(i + 1, 1)

            kv_weights_lo(0)
            ctx_lo(0, 0)
            ctx_lo(0, 1)
            pool.wait_ge(s_cst, 16 * 8)
            pool.wait_ge(s_x, 16)
            pool.wait_ge(s_xn, 1)
            for b in range(B):
                nc.gpsimd.tensor_tensor(x_sb[:, b], x_sb[:, b], bo_bc[:], ALU.add).then_inc(s_xb, 1)
            with pool.Fori(0, 3) as i:
                iteration(i, True)
            iteration(3, True, weights=1)
            with pool.Fori(4, NI - 1) as i:
                iteration(i, True)
            iteration(NI - 1, False)

            def weight_lo(n):
                pool.wait_ge(s_Whi, n + 1)
                nc.gpsimd.tensor_tensor(Wlo[:, SLOT[n]], raw[:, n % 2], Whi[:, SLOT[n]].bitcast(F32),
                                        ALU.subtract).then_inc(s_Wlo, 1)

            def dequantise(blk, a):
                f = 2 * blk + a
                if not (isinstance(f, int) and f == 0):
                    wait_apart(pool, s_fw, f, passed_pool)
                wait_apart(pool, s_fq[a], 16 * (blk + 1), passed_pool)
                nc.gpsimd.tensor_scalar(dq_w[:], raw[:, 1 - a].bitcast(I32), DEQ, -1.0, ALU.mult, ALU.add).then_inc(s_dq1, 1)
                pool.wait_ge(s_fs, 16 * (f + 1))
                pool.wait_ge(s_dq1, f + 1)
                nc.gpsimd.tensor_tensor(dq_w[:], dq_w[:], dq_scale[:], ALU.mult).then_inc(s_dq2, 1)

            for n in (WXO, WQ, WK):
                weight_lo(n)
            pool.wait_ge(o_ready, 6 * NI)
            nc.gpsimd.memset(vh2[:, :, :, 3 * HD:VW], 1.0).then_inc(s_ones2, 1)
            weight_lo(WV)
            weight_lo(WAO)
            for b in range(B):
                pool.wait_ge(s_v2, b + 1)
                nc.gpsimd.tensor_tensor(vh2[:, b, :, 2 * HD:3 * HD],
                                        vrest2[:, b % 2].rearrange("p (h c) -> p h c", c=HD),
                                        vh2[:, b, :, HD:2 * HD], ALU.subtract).then_inc(s_v3, 1)
            dequantise(0, 0)
            dequantise(0, 1)

            def ffn_block(blk, last):
                pool.wait_ge(s_T, 16 + 8 * blk)
                for b in range(B):
                    nc.gpsimd.tensor_tensor(h_tok[:, b], h_tok[:, b],
                                            f_bc[:, bass.ds(2 * blk + 1, 1)].rearrange("p one d -> p (one d)"),
                                            ALU.add).then_inc(s_hb, 1)
                if last:
                    for b in range(B):
                        pool.wait_ge(s_hb, 4 * blk + b + 1)
                        nc.gpsimd.tensor_tensor(h_tok[:, b], h_tok[:, b], x_sb[:, b], ALU.add).then_inc(s_hb, 1)
                else:
                    dequantise(blk + 1, 0)
                    dequantise(blk + 1, 1)

            pool.wait_ge(s_fb, 16)
            with pool.Fori(0, NBLK - 1) as blk:
                ffn_block(blk, False)
            ffn_block(NBLK - 1, True)

        def split_product(out_ap, pairs, last_sem=None):
            n = len(pairs)
            for k, (lh, ll, rh, rl) in enumerate(pairs):
                nc.tensor.matmul(out_ap, lh, rh, start=(k == 0), stop=False)
                nc.tensor.matmul(out_ap, lh, rl, start=False, stop=False)
                mm = nc.tensor.matmul(out_ap, ll, rh, start=False, stop=(k == n - 1))
            if last_sem is not None:
                mm.then_inc(last_sem, 1)

        def ksl(m):
            return slice(P * m, P * m + P)

        @block.tensor
        def _(pe):
            pe.wait_ge(s_id, 7)
            pe.wait_ge(s_xn, 1)
            for k in range(KD):
                for b in range(B):
                    mm = nc.tensor.transpose(ps[:, k, ksl(b)], xn0[:, b, ksl(k)], ident[:])
                mm.then_inc(s_t0, 1)
            pe.wait_ge(s_wq_lo, 1)
            pe.wait_ge(s_t0l, KD)
            for m in range(KD):
                split_product(ps[:, 4 + m], [(chi[:, 1, k, ksl(m)], clo[:, 1, k, ksl(m)], xnT_hi[:, k], xnT_lo[:, k])
                                             for k in range(KD)], s_q)
            pe.wait_ge(s_ql, KD)

            with pe.Fori(0, NI) as i:
                pe.wait_ge(s_w_lo, (i >> 2) + 1)
                for kc in range(NKC):
                    pe.wait_ge(s_c_lo, 4 * i + (kc + 1))
                    c = kc % 2
                    for t in range(4):
                        n = 4 * kc + t
                        if n >= 4:
                            pe.wait_ge(kv_lo, 16 * i + (n - 3))
                        if t < 2:
                            split_product(ps[:, t], [(whi[:, 0, k, ksl(t)], wlo[:, 0, k, ksl(t)], chi[:, c, k], clo[:, c, k])
                                                     for k in range(KD)], kv_mm)
                        else:
                            for a in range(2):
                                q = 2 * (t - 2) + a
                                split_product(ps[:, t, 256 * a:256 * a + 256],
                                              [(chi[:, c, k, ksl(q)], clo[:, c, k, ksl(q)], whi[:, 1, k], wlo[:, 1, k])
                                               for k in range(KD)], kv_mm if a else None)
                pe.wait_ge(kv_lo, 16 * (i + 1))
                pe.wait_ge(q_slots, i + 1)

                def score(m):
                    h, c = m // NKC, m % NKC
                    if m >= 4 and c % 2 == 0:
                        pe.wait_ge(masked, 16 * i + (2 * (h - 1) + c // 2 + 1))
                    ks = slice(512 * c, 512 * c + 512)
                    split_product(ps[:, c], [(qzhi[:, h], qzlo[:, h], khi[:, h // 4, ks], klo[:, h // 4, ks])],
                                  scores if c % 2 else None)

                def transposes(n):
                    h, t = n // NKC, n % NKC
                    if t % 2 == 0:
                        pe.wait_ge(exps, 16 * i + (2 * h + t // 2 + 1))
                    if n >= 2:
                        pe.wait_ge(pt_lo, 32 * i + (n - 1))
                    for y in range(4):
                        mm = nc.tensor.transpose(ps[:, 4 + n % 2, ksl(y)], sm[:, h % 2, ksl(4 * t + y)], ident[:])
                    mm.then_inc(tps, 1)

                def weighted(n):
                    h, t = n // NKC, n % NKC
                    pe.wait_ge(pt_lo, 32 * i + (n + 1))
                    if n == 0:
                        pe.wait_ge(v_all, 8 * (i + 1))
                    acc = ps[:, 6 + h // 4, VW * (h % 4):VW * (h % 4) + VW]
                    for y in range(4):
                        v = vh[:, 4 * t + y, h, :]
                        nc.tensor.matmul(acc, pthi[:, n % PTR, y], v, start=(t == 0 and y == 0), stop=False)
                        mm = nc.tensor.matmul(acc, ptlo[:, n % PTR, y], v, start=False, stop=(t == 3 and y == 3))
                    mm.then_inc(pv, 1)

                for n in range(-LEAD, NG + LAG):
                    if 0 <= n + LEAD < NG:
                        score(n + LEAD)
                    if 0 <= n < NG:
                        transposes(n)
                    if 0 <= n - LAG < NG:
                        weighted(n - LAG)
            def transpose_tokens(src, base, free_sem, free_base):
                for k in range(KD):
                    if k >= 2:
                        pe.wait_ge(free_sem, free_base + (k - 1))
                    for b in range(B):
                        mm = nc.tensor.transpose(ps[:, k % 2, ksl(b)], src[:, b, ksl(k)], ident[:])
                    mm.then_inc(s_T, 1)

            def lora_product(f, k):
                if k == 0:
                    pe.wait_ge(s_fl, 32 * (f + 1))
                if k >= 2:
                    pe.wait_ge(s_fadd, 4 * f + (k - 1))
                nc.tensor.matmul(ps[:, 2 + k % 2], la_sb[:, ksl(k)], lb_sb[:], start=True, stop=True).then_inc(s_lora, 1)

            def token_linear(slot, f=None):
                if f is not None:
                    lora_product(f, 0)
                    lora_product(f, 1)
                for b in range(B):
                    split_product(ps[:, 4 + b], [(aThi[:, k, ksl(b)], aTlo[:, k, ksl(b)], Whi[:, slot, k], Wlo[:, slot, k])
                                                 for k in range(KD)], s_lin)
                    if f is not None and b < 2:
                        lora_product(f, b + 2)

            def feature_linear(slot, free_sem):
                for m in range(KD):
                    if free_sem is not None:
                        pe.wait_ge(free_sem, m + 1)
                    split_product(ps[:, 4 + m], [(Whi[:, slot, k, ksl(m)], Wlo[:, slot, k, ksl(m)], aThi[:, k], aTlo[:, k])
                                                 for k in range(KD)], s_lin)

            pe.wait_ge(o_ready, 6 * NI)
            transpose_tokens(o_tok, 0, s_al, 0)
            pe.wait_ge(s_Wlo, 1)
            pe.wait_ge(s_al, 4)
            token_linear(SLOT[WXO])
            pe.wait_ge(s_tok, 1)
            transpose_tokens(tok, 4, s_al, 4)
            pe.wait_ge(s_Wlo, 2)
            pe.wait_ge(s_al, 8)
            feature_linear(SLOT[WQ], None)
            pe.wait_ge(s_Wlo, 3)
            feature_linear(SLOT[WK], s_q2)
            pe.wait_ge(s_Wlo, 4)
            for b in range(B):
                pe.wait_ge(s_k2, b + 1)
                split_product(ps[:, 4 + b], [(aThi[:, k, ksl(b)], aTlo[:, k, ksl(b)], Whi[:, SLOT[WV], k], Wlo[:, SLOT[WV], k])
                                             for k in range(KD)], s_lin)
            pe.wait_ge(s_v3, B)
            pe.wait_ge(s_ones2, 1)
            for n in range(NU + 3):
                if n < NU:
                    b, g = n // 4, n % 4
                    wait(pe, u_m, n - 1)
                    for j in range(4):
                        mm = nc.tensor.matmul(ps[:, 2 + n % 2, ksl(j)], qz2[:, g, j, ksl(b)], kT2[:, g, ksl(b)],
                                              start=True, stop=True)
                    mm.then_inc(u_s, 1)
                if 0 <= n - 2 < NU:
                    u = n - 2
                    pe.wait_ge(u_e, u + 1)
                    wait(pe, u_l, u - 1)
                    for j in range(4):
                        mm = nc.tensor.transpose(ps[:, u % 2, ksl(j)], sm2[:, u % 2, j], ident[:])
                    mm.then_inc(u_t, 1)
                if 0 <= n - 3 < NU:
                    u = n - 3
                    b, g = u // 4, u % 4
                    pe.wait_ge(u_l, u + 1)
                    wait(pe, u_o, u - 1)
                    for j in range(4):
                        acc = ps[:, 6 + u % 2, VW * j:VW * j + VW]
                        nc.tensor.matmul(acc, pthi2[:, u % 2, j], vh2[:, b, 4 * g + j], start=True, stop=False)
                        mm = nc.tensor.matmul(acc, ptlo2[:, u % 2, j], vh2[:, b, 4 * g + j], start=False, stop=True)
                    mm.then_inc(u_pv, 1)
            pe.wait_ge(s_tok, 2)
            transpose_tokens(tok, 8, s_g, 0)
            pe.wait_ge(s_Wlo, 5)
            pe.wait_ge(s_al, 12)
            token_linear(SLOT[WAO], 0)

            def ffn_block(blk, last):
                pe.wait_ge(s_h, blk + 1)
                transpose_tokens(h_tok, None, s_al, 12 + 8 * blk)
                pe.wait_ge(s_al, 16 + 8 * blk)
                pe.wait_ge(s_fw, 2 * blk + 1)
                token_linear(SLOT0, 2 * blk + 1)
                pe.wait_ge(s_tok, 3 + blk)
                transpose_tokens(tok, None, s_g, 4 + 4 * blk)
                pe.wait_ge(s_al, 20 + 8 * blk)
                pe.wait_ge(s_fw, 2 * blk + 2)
                token_linear(SLOT1, None if last else 2 * blk + 2)

            with pe.Fori(0, NBLK - 1) as blk:
                ffn_block(blk, False)
            ffn_block(NBLK - 1, True)

        @block.scalar
        def _(act):
            def ident_bias(out_ap, in_ap, bias_ap):
                return nc.scalar.activation(out_ap, in_ap, ACT.Identity, bias=bias_ap)

            for k in range(KD):
                act.wait_ge(s_t0, k + 1)
                nc.scalar.copy(xnT_hi[:, k], ps[:, k]).then_inc(s_t0h, 1)
            act.wait_ge(s_cst, 16 * 8)
            for m in range(KD):
                act.wait_ge(s_q, m + 1)
                ident_bias(qthi[:, m], ps[:, 4 + m], b_q[:, m:m + 1]).then_inc(s_qh, 1)

            with act.Fori(0, NI) as i:
                def v_mid_part(n):
                    act.wait_ge(kv_lo, 16 * i + (4 * (n // 2) + 2 + n % 2 + 1))
                    nc.scalar.copy(vh[:, 2 * n:2 * n + 2, :, HD:2 * HD],
                                   vrest[:, n % 2].rearrange("p (a h c) -> p a h c", a=2, c=HD)).then_inc(v_mid, 1)

                act.wait_ge(bk_now, i + 1)
                for n in range(16):
                    kc, t = n // 4, n % 4
                    act.wait_ge(kv_mm, 16 * i + (n + 1))
                    if t < 2:
                        ident_bias(khi[:, t, 512 * kc:512 * kc + 512], ps[:, t],
                                   b_kn[:, t:t + 1]).then_inc(kv_hi, 1)
                    else:
                        v = 2 * kc + t - 2
                        nc.scalar.copy(vh[:, 2 * v:2 * v + 2, :, 0:HD],
                                       ps[:, t].rearrange("p (a h c) -> p a h c", a=2, c=HD)).then_inc(kv_hi, 1)
                        if v >= 1:
                            v_mid_part(v - 1)
                v_mid_part(7)

                def exp_half(h, half):
                    act.wait_ge(nbias, 8 * i + (h + 1))
                    s = sm[:, h % 2, 1024 * half:1024 * half + 1024]
                    nc.scalar.activation(s, s, ACT.Exp, bias=nb[:, h % 2, 0:1], scale=SCALE).then_inc(exps, 1)

                def weights_hi(n):
                    act.wait_ge(tps, 32 * i + (n + 1))
                    if n >= PTR:
                        act.wait_ge(pv, 32 * i + (n - PTR + 1))
                    nc.scalar.copy(pthi[:, n % PTR], ps[:, 4 + n % 2].rearrange("p (y q) -> p y q", y=4)).then_inc(pt_hi, 1)

                for n in range(-2, NG):
                    h, t = (n + 2) // NKC, (n + 2) % NKC
                    if h < HI and t % 2 == 0:
                        exp_half(h, t // 2)
                    if n >= 0:
                        weights_hi(n)
            def head_view(ap):
                return ap.rearrange("p (h c) -> p h c", c=HD)

            for k in range(KD):
                act.wait_ge(s_T, k + 1)
                ident_bias(aThi[:, k], ps[:, k % 2], b_v[:, k:k + 1]).then_inc(s_ah, 1)
            for k in range(KD):
                act.wait_ge(s_T, 4 + k + 1)
                nc.scalar.copy(aThi[:, k], ps[:, k % 2]).then_inc(s_ah, 1)
            for m in range(KD):
                act.wait_ge(s_lin, 4 + m + 1)
                for j in range(4):
                    ins = nc.scalar.activation(qz2[:, m, j], ps[:, 4 + m], ACT.Copy, scale=rowmask[:, j:j + 1])
                ins.then_inc(s_q2, 1)
            for b in range(B + 1):
                if b < B:
                    act.wait_ge(s_lin, 12 + b + 1)
                    nc.scalar.copy(vh2[:, b, :, 0:HD], head_view(ps[:, 4 + b])).then_inc(s_v1, 1)
                if b >= 1:
                    act.wait_ge(s_vr, b)
                    nc.scalar.copy(vh2[:, b - 1, :, HD:2 * HD], head_view(vrest2[:, (b - 1) % 2])).then_inc(s_v2, 1)
            for n in range(NU + 2):
                if n < NU:
                    act.wait_ge(u_nb, n + 1)
                    for j in range(4):
                        ins = nc.scalar.activation(sm2[:, n % 2, j], sm2[:, n % 2, j], ACT.Exp, bias=nb[:, n % 2, j:j + 1])
                    ins.then_inc(u_e, 1)
                if n >= 2:
                    u = n - 2
                    act.wait_ge(u_t, u + 1)
                    wait(act, u_pv, u - 1)
                    nc.scalar.copy(pthi2[:, u % 2], ps[:, u % 2].rearrange("p (j q) -> p j q", j=4)).then_inc(u_h, 1)
            for k in range(KD):
                act.wait_ge(s_T, 8 + k + 1)
                nc.scalar.activation(g32[:, k], ps[:, k % 2], ACT.Identity, scale=g_a[:, k:k + 1],
                                     bias=be_a[:, k:k + 1]).then_inc(s_g, 1)

            g_ff = g_f[:].rearrange("p f k -> p (f k)")
            be_ff = be_f[:].rearrange("p f k -> p (f k)")
            with act.Fori(0, NBLK) as blk:
                for k in range(KD):
                    act.wait_ge(s_T, 12 + 8 * blk + (k + 1))
                    nc.scalar.copy(aThi[:, k], ps[:, k % 2]).then_inc(s_ah, 1)
                for k in range(KD):
                    wait_apart(act, s_T, 16 + 8 * blk + (k + 1), passed_act)
                    nc.scalar.activation(g32[:, k], ps[:, k % 2], ACT.Gelu, scale=g_ff[:, bass.ds(4 * blk + k, 1)],
                                         bias=be_ff[:, bass.ds(4 * blk + k, 1)]).then_inc(s_g, 1)

        @block.vector
        def _(dve):
            chain = [0]

            def link(ins, n=None):
                chain[0] += 1
                ins.then_inc(s_vec, 1)
                dve.wait_ge(s_vec, chain[0])

            def kv_weights_hi(p):
                dve.wait_ge(s_w, 32 * (p + 1))
                wait(dve, kv_mm, 16 * 4 * p)
                nc.vector.tensor_copy(whi[:], wraw[:]).then_inc(s_w_hi, 1)

            def ctx_hi(i, kc):
                dve.wait_ge(s_c[kc % 2], 32 * i + 16 * (kc // 2 + 1))
                wait(dve, kv_mm, 16 * i + 4 * (kc - 1))
                nc.vector.tensor_copy(chi[:, kc % 2], craw[:, kc % 2]).then_inc(s_c_hi, 1)

            def rstd(link):
                link(nc.vector.tensor_scalar(ve[:], mv[:, :, 1], LN_EPS, None, ALU.add))
                link(nc.vector.tensor_scalar(rt[:].bitcast(I32), ve[:].bitcast(I32), 1, None, ALU.logical_shift_right))
                link(nc.vector.tensor_scalar(rs[:].bitcast(I32), rt[:].bitcast(I32), -1.0, float(0x5F3759DF),
                                             ALU.mult, ALU.add))
                for _ in range(4):
                    link(nc.vector.tensor_tensor(rt[:], rs[:], rs[:], ALU.mult))
                    link(nc.vector.scalar_tensor_tensor(out=rt[:], in0=rt[:], scalar=-0.5, in1=ve[:],
                                                        op0=ALU.mult, op1=ALU.mult))
                    link(nc.vector.scalar_tensor_tensor(out=rs[:], in0=rt[:], scalar=1.5, in1=rs[:],
                                                        op0=ALU.add, op1=ALU.mult))

            def weight_hi(n):
                dve.wait_ge(s_raw[n % 2], 16 * (n // 2 + 1))
                if n <= WK:
                    dve.wait_ge(kv_mm, 16 * NI)
                else:
                    dve.wait_ge(s_lin, 4 if n == WV else 8)
                nc.vector.tensor_copy(Whi[:, SLOT[n]], raw[:, n % 2]).then_inc(s_Whi, 1)

            dve.wait_ge(s_wq, 16)
            nc.vector.tensor_copy(chi[:, 1], craw[:, 1]).then_inc(s_wq_hi, 1)
            dve.wait_ge(s_x, 16)
            for b in range(B):
                link(nc.vector.bn_stats(stats[:, b], x_sb[:, b]))
                link(nc.vector.bn_aggr(mv[:, b], stats[:, b]))
            rstd(link)
            for b in range(B):
                ins = nc.vector.tensor_scalar(xn0[:, b], x_sb[:, b], mv[:, b, 0:1], rs[:, b:b + 1],
                                              ALU.subtract, ALU.mult)
            ins.then_inc(s_xn, 1)
            kv_weights_hi(0)
            ctx_hi(0, 0)
            for k in range(KD):
                dve.wait_ge(s_t0h, k + 1)
                nc.vector.tensor_tensor(xnT_lo[:, k], ps[:, k], xnT_hi[:, k].bitcast(F32), ALU.subtract).then_inc(s_t0l, 1)
            dve.wait_ge(s_m, 16)
            link(nc.vector.tensor_scalar(mbias[:], mraw, 0.0, NEG, ALU.is_equal, ALU.mult))
            link(nc.vector.tensor_reduce(nanfix[:, 0:1], mbias[:], AX.X, ALU.max))
            link(nc.vector.tensor_scalar(nanfix[:, 1:2], nanfix[:, 0:1], 0.1 * NEG, None, ALU.is_gt))
            link(nc.vector.reciprocal(nanfix[:, 2:3], nanfix[:, 1:2]))
            link(nc.vector.tensor_tensor(nanfix[:, 3:4], nanfix[:, 1:2], nanfix[:, 2:3], ALU.mult))
            for m in range(KD):
                dve.wait_ge(s_qh, m + 1)
                nc.vector.scalar_tensor_tensor(out=qtlo[:, m], in0=ps[:, 4 + m], scalar=b_q[:, m:m + 1],
                                               in1=qthi[:, m].bitcast(F32), op0=ALU.add, op1=ALU.subtract).then_inc(s_ql, 1)
            dve.wait_ge(s_q, KD)
            dve.wait_ge(s_ql, KD)
            ctx_hi(0, 1)
            pool_init = 6
            dve.wait_ge(s_id, pool_init)

            def iteration(i, prefetch, weights=None):
                def kv_rest(n):
                    kc, t = n // 4, n % 4
                    dve.wait_ge(kv_hi, 16 * i + (n + 1))
                    if t < 2:
                        ks = slice(512 * kc, 512 * kc + 512)
                        nc.vector.scalar_tensor_tensor(out=klo[:, t, ks], in0=ps[:, t],
                                                       scalar=b_kn[:, t:t + 1],
                                                       in1=khi[:, t, ks].bitcast(F32), op0=ALU.add,
                                                       op1=ALU.subtract).then_inc(kv_lo, 1)
                    else:
                        v = 2 * kc + t - 2
                        if v >= 2:
                            dve.wait_ge(v_all, 8 * i + (v - 1))
                        nc.vector.tensor_tensor(vrest[:, v % 2].rearrange("p (a h c) -> p a h c", a=2, c=HD),
                                                ps[:, t].rearrange("p (a h c) -> p a h c", a=2, c=HD),
                                                vh[:, 2 * v:2 * v + 2, :, 0:HD], ALU.subtract).then_inc(kv_lo, 1)

                nc.vector.tensor_copy(b_kn[:], b_kf[:, bass.ds(i & 4, 2)]).then_inc(bk_now, 1)
                for j in range(4):
                    rows = slice(32 * j, 32 * j + 32)
                    for dst, src in ((qzhi, qthi), (qzlo, qtlo)):
                        s = src[rows].rearrange("p m t -> p (m t)")
                        for g in range(2):
                            ins = nc.vector.tensor_copy(dst[rows, 4 * g + j],
                                                        s[:, bass.ds((i & 4) * 256 + (i & 3) * P + 512 * g, P)])
                ins.then_inc(q_slots, 1)
                dve.wait_ge(bk_now, i + 1)
                for n in range(16):
                    kv_rest(n)
                    if n in (4, 8):
                        ctx_hi(i, 2 + n // 8)

                def mask_half(h, half):
                    if h >= 2:
                        dve.wait_ge(tps, 32 * i + (4 * (h - 2) + 2 * half + 2))
                    if half:
                        dve.wait_ge(masked, 16 * i + (2 * h + 1))
                    wait_apart(dve, scores, 16 * i + (2 * h + half + 1), passed_dve)
                    s = slice(1024 * half, 1024 * half + 1024)
                    nc.vector.tensor_tensor_reduce(
                        sm[:, h % 2, s], ps[:, 2 * half:2 * half + 2].rearrange("p c t -> p (c t)"), mbias[:, s],
                        1.0, mx[:, h % 2, 0:1] if half else 3.0 * NEG, ALU.add, ALU.max,
                        mx[:, h % 2, half:half + 1]).then_inc(masked, 1)
                    if half:
                        dve.wait_ge(masked, 16 * i + (2 * h + 2))
                        nc.vector.tensor_scalar(nb[:, h % 2, 0:1], mx[:, h % 2, 1:2], -SCALE, PSHIFT,
                                                ALU.mult, ALU.add).then_inc(nbias, 1)

                def weights_lo(n):
                    dve.wait_ge(pt_hi, 32 * i + (n + 1))
                    nc.vector.tensor_tensor(ptlo[:, n % PTR], ps[:, 4 + n % 2].rearrange("p (y q) -> p y q", y=4),
                                            pthi[:, n % PTR], ALU.subtract).then_inc(pt_lo, 1)

                def normalise(g):
                    dve.wait_ge(pv, 32 * i + 16 * (g + 1))
                    acc = ps[:, 6 + g, 0:4 * VW].rearrange("p (h w) -> p h w", h=4)
                    nc.vector.reciprocal(rc[:], acc[:, :, 3 * HD]).then_inc(o_ready, 1)
                    nc.vector.tensor_reduce(osum[:], acc[:, :, 0:3 * HD].rearrange("p h (s c) -> p h c s", s=3),
                                            AX.X, ALU.add).then_inc(o_ready, 1)
                    dve.wait_ge(o_ready, 6 * i + (3 * g + 2))
                    dst = o_tok[:].rearrange("p b d -> p (b d)")[:, bass.ds((i & 3) * D + (i & 4) * 64 + P * g, P)]
                    nc.vector.scalar_tensor_tensor(out=dst, in0=osum[:].rearrange("p h c -> p (h c)"),
                                                   scalar=nanfix[:, 3:4],
                                                   in1=rc[:].unsqueeze(2).broadcast_to([P, 4, HD]),
                                                   op0=ALU.mult, op1=ALU.mult).then_inc(o_ready, 1)

                for n in range(-5, NG):
                    m = n + LEAD
                    if m % 2 == 1 and m < NG:
                        mask_half(m // NKC, (m % NKC) // 2)
                    if n == 18:
                        normalise(0)
                    if n == 4 and weights is not None:
                        kv_weights_hi(weights)
                    if n in (8, 12) and prefetch:
                        ctx_hi(i + 1, (n - 8) // 4)
                    if n in (8, 16, 24) and not prefetch:
                        weight_hi(n // 8 - 1)
                    if n >= 0:
                        weights_lo(n)
                normalise(1)

            with dve.Fori(0, 3) as i:
                iteration(i, True)
            iteration(3, True, weights=1)
            with dve.Fori(4, NI - 1) as i:
                iteration(i, True)
            iteration(NI - 1, False)
            def low_parts(base, bias=None):
                for k in range(KD):
                    dve.wait_ge(s_ah, base + (k + 1))
                    hi = aThi[:, k].bitcast(F32)
                    if bias is None:
                        ins = nc.vector.tensor_tensor(aTlo[:, k], ps[:, k % 2], hi, ALU.subtract)
                    else:
                        ins = nc.vector.scalar_tensor_tensor(out=aTlo[:, k], in0=ps[:, k % 2], scalar=bias[:, k:k + 1],
                                                             in1=hi, op0=ALU.add, op1=ALU.subtract)
                    ins.then_inc(s_al, 1)

            def both_parts(steps, base):
                for k in range(KD):
                    dve.wait_ge(s_g, base + (k + 1))
                    steps.need(steps.mark(nc.vector.tensor_copy(aThi[:, k], g32[:, k])))
                    nc.vector.tensor_tensor(aTlo[:, k], g32[:, k], aThi[:, k].bitcast(F32), ALU.subtract).then_inc(s_al, 1)

            def lora_add(f, k):
                dve.wait_ge(s_lora, 4 * f + (k + 1))
                if k == 0:
                    dve.wait_ge(s_dq2, f + 1)
                nc.vector.tensor_tensor(dq_w[:, k], dq_w[:, k], ps[:, 2 + k % 2], ALU.add).then_inc(s_fadd, 1)

            def ffn_weight_parts(steps, f, slot):
                dve.wait_ge(s_fadd, 4 * (f + 1))
                steps.need(steps.mark(nc.vector.tensor_copy(Whi[:, slot], dq_w[:])))
                nc.vector.tensor_tensor(Wlo[:, slot], dq_w[:], Whi[:, slot].bitcast(F32), ALU.subtract).then_inc(s_fw, 1)

            def with_lora(steps, produce, f, slot):
                def step(b):
                    if f is not None and b == 0:
                        lora_add(f, 0)
                        lora_add(f, 1)
                    ins = produce(b)
                    if f is not None and b < 2:
                        return ins, lambda: lora_add(f, b + 2)
                    if f is not None and b == 2:
                        return ins, lambda: ffn_weight_parts(steps, f, slot)
                    return ins, lambda: None
                return step

            def normalise_tiles(steps, step, src, dst):
                made, seen = [None] * B, [None] * B
                for b in range(B + 1):
                    if b < B and step is not None:
                        ins, after = step(b)
                        made[b] = steps.mark(ins)
                        after()
                    if b >= 1:
                        if made[b - 1] is not None:
                            steps.need(made[b - 1])
                        seen[b - 1] = steps.mark(nc.vector.bn_stats(stats[:, b - 1], src[:, b - 1]))
                for b in range(B):
                    wait_apart(dve, steps.sem, seen[b], passed_dve)
                    last = steps.mark(nc.vector.bn_aggr(mv[:, b], stats[:, b]))
                steps.need(last)
                rstd(lambda ins: steps.need(steps.mark(ins)))
                for b in range(B):
                    ins = nc.vector.tensor_scalar(dst[:, b], src[:, b], mv[:, b, 0:1], rs[:, b:b + 1],
                                                  ALU.subtract, ALU.mult)
                return ins

            steps = Steps(dve, s_pre, 0)
            low_parts(0, b_v)

            def residual_tile(base, need_bias=False):
                def step(b):
                    if need_bias:
                        dve.wait_ge(s_xb, b + 1)
                    dve.wait_ge(s_lin, base + b + 1)
                    return nc.vector.tensor_tensor(x_sb[:, b], ps[:, 4 + b], x_sb[:, b], ALU.add)
                return step

            normalise_tiles(steps, with_lora(steps, residual_tile(0, True), None, None), x_sb, tok).then_inc(s_tok, 1)
            low_parts(4)
            weight_hi(WV)
            for m in range(KD):
                dve.wait_ge(s_lin, 8 + m + 1)
                nc.vector.tensor_scalar(kT2[:, m], ps[:, 4 + m], SCALE, None, ALU.mult).then_inc(s_k2, 1)
                if m == 0:
                    weight_hi(WAO)
            for b in range(B):
                dve.wait_ge(s_v1, b + 1)
                if b >= 2:
                    dve.wait_ge(s_v3, b - 1)
                nc.vector.tensor_tensor(vrest2[:, b % 2].rearrange("p (h c) -> p h c", c=HD),
                                        ps[:, 4 + b].rearrange("p (h c) -> p h c", c=HD),
                                        vh2[:, b, :, 0:HD], ALU.subtract).then_inc(s_vr, 1)
            for n in range(NU + 4):
                if n < NU:
                    dve.wait_ge(u_s, n + 1)
                    wait(dve, u_t, n - 1)
                    nc.vector.tensor_tensor(sm2[:, n % 2], ps[:, 2 + n % 2].rearrange("p (j q) -> p j q", j=4),
                                            causal[:].unsqueeze(1).broadcast_to([P, 4, P]), ALU.add).then_inc(u_m, 1)
                    dve.wait_ge(u_m, n + 1)
                    steps.need(steps.mark(nc.vector.tensor_reduce(mx2[:], sm2[:, n % 2], AX.X, ALU.max)))
                    nc.vector.tensor_scalar(nb[:, n % 2], mx2[:], -1.0, PSHIFT, ALU.mult, ALU.add).then_inc(u_nb, 1)
                if 0 <= n - 2 < NU:
                    u = n - 2
                    dve.wait_ge(u_h, u + 1)
                    nc.vector.tensor_tensor(ptlo2[:, u % 2], ps[:, u % 2].rearrange("p (j q) -> p j q", j=4),
                                            pthi2[:, u % 2], ALU.subtract).then_inc(u_l, 1)
                if 0 <= n - 4 < NU:
                    u = n - 4
                    dve.wait_ge(u_pv, u + 1)
                    wait(dve, u_o, u)
                    acc = ps[:, 6 + u % 2, 0:4 * VW].rearrange("p (h w) -> p h w", h=4)
                    steps.mark(nc.vector.reciprocal(rc[:], acc[:, :, 3 * HD]))
                    steps.need(steps.mark(nc.vector.tensor_reduce(
                        osum[:], acc[:, :, 0:3 * HD].rearrange("p h (s c) -> p h c s", s=3), AX.X, ALU.add)))
                    nc.vector.tensor_tensor(o_tok[:, u // 4, P * (u % 4):P * (u % 4) + P].rearrange("p (h c) -> p h c", c=HD),
                                            osum[:], rc[:].unsqueeze(2).broadcast_to([P, 4, HD]), ALU.mult).then_inc(u_o, 1)
            dve.wait_ge(u_o, NU)
            normalise_tiles(steps, None, o_tok, tok).then_inc(s_tok, 1)
            both_parts(steps, 0)
            normalise_tiles(steps, with_lora(steps, residual_tile(16), 0, SLOT0), x_sb, h_tok).then_inc(s_h, 1)

            def ffn_block(blk, last):
                steps = Steps(dve, s_ffn, FFN_STEPS * blk)
                low_parts(8 + 4 * blk)

                def first(b):
                    if b == 0:
                        dve.wait_ge(s_fb, 16)
                    dve.wait_ge(s_lin, 20 + 8 * blk + (b + 1))
                    return nc.vector.tensor_tensor(tok[:, b], ps[:, 4 + b],
                                                   f_bc[:, bass.ds(2 * blk, 1)].rearrange("p one d -> p (one d)"), ALU.add)

                normalise_tiles(steps, with_lora(steps, first, 2 * blk + 1, SLOT1), tok, tok).then_inc(s_tok, 1)
                both_parts(steps, 4 + 4 * blk)

                def second(b):
                    dve.wait_ge(s_hb, 4 * blk + (b + 1) + (B if last else 0))
                    dve.wait_ge(s_lin, 24 + 8 * blk + (b + 1))
                    return nc.vector.tensor_tensor(h_tok[:, b], ps[:, 4 + b], h_tok[:, b], ALU.add)

                step = with_lora(steps, second, None if last else 2 * blk + 2, SLOT0)
                for b in range(B):
                    ins, after = step(b)
                    if last:
                        ins.then_inc(s_fin, 1)
                    elif b == B - 1:
                        ins.then_inc(s_h, 1)
                    after()
                if not last:
                    assert steps.n == FFN_STEPS, steps.n

            with dve.Fori(0, NBLK - 1) as blk:
                ffn_block(blk, False)
            ffn_block(NBLK - 1, True)




def kernel(**inputs):
    import concourse.bacc as bacc
    from concourse.bass_utils import run_bass_kernel_spmd

    nc = bacc.Bacc("TRN2", target_bir_lowering=False, num_devices=1)
    g = {k: np.asarray(v) for k, v in inputs.items()}

    def cols(v):
        return v.reshape(KD, P).T

    av = g["L0_attn_Wv"].reshape(HD, H, D).transpose(1, 0, 2).reshape(D, D)
    fq = g["L0_ffn_qweights"]
    data = {
        "x": g["x"].reshape(B * P, D),
        "ctxT": g["ctx_1024"].reshape(B * S2, D).T,
        "mask": g["mask_1x1xSxS2_ik0"].reshape(P, S2),
        "wqT": g["L0_xattn_Wq"].T, "wkT": g["L0_xattn_Wk"].T, "wvT": g["L0_xattn_Wv"].T, "woT": g["L0_xattn_Wo"].T,
        "bq": cols(g["L0_xattn_bq"]), "bk": cols(g["L0_xattn_bk"]), "bv": cols(g["L0_xattn_bv"]),
        "bo": g["L0_xattn_bo"],
        "aqT": g["L0_attn_Wq"].T, "akT": g["L0_attn_Wk"].T, "avT": av.T, "aoT": g["L0_attn_Wo"].T,
        "a_gamma": cols(g["L0_attn_gamma"]), "a_beta": cols(g["L0_attn_beta"]),
        "fqT": fq.transpose(0, 2, 1), "fsT": np.repeat(g["L0_ffn_scales"].transpose(0, 2, 1), 16, axis=1),
        "f_bias": g["L0_ffn_biases"],
        "f_la": g["L0_ffn_lora_a"], "f_lbT": g["L0_ffn_lora_b"].transpose(0, 2, 1),
        "f_gamma": g["L0_ffn_ln_gamma"].reshape(NBLK, KD, P).transpose(2, 0, 1),
        "f_beta": g["L0_ffn_ln_beta"].reshape(NBLK, KD, P).transpose(2, 0, 1),
    }
    arrays, args = {}, {}
    for name, a in data.items():
        a = np.ascontiguousarray(a)
        arrays["in_" + name] = a
        args[name] = nc.dram_tensor("in_" + name, a.shape, mybir.dt.from_np(a.dtype), kind="ExternalInput").ap()
    args["out"] = nc.dram_tensor("out", (B * P, D), F32, kind="ExternalOutput").ap()
    build(nc, **args)
    r = run_bass_kernel_spmd(nc, [arrays], core_ids=[0])
    return r.results[0]["out"].reshape(B, P, D)
```

```python
from contextlib import ExitStack
import math

import numpy as np

import concourse.bass as bass
from concourse import mybir

ALU = mybir.AluOpType
ACT = mybir.ActivationFunctionType
AX = mybir.AxisListType
F32 = mybir.dt.float32
F32R = mybir.dt.float32r
F16 = mybir.dt.float16
BF16 = mybir.dt.bfloat16
I32 = mybir.dt.int32

P = 128
B = 4
D = 512
KD = D // P
H = 16
HD = D // H
S2 = 2048
NKC = S2 // 512
NI = 2 * B
HI = H // 2
VW = 3 * HD + 2
SCALE = HD ** -0.5
NEG = -1.0e30
LN_EPS = 1e-5
PSHIFT = math.log(4096.0)
LEAD = 7
LAG = 3
NG = HI * NKC
PTR = 4
TB = 2
NBLK = 3
NU = B * H // 4
FFN_STEPS = 52
DEQ = 1.0 / 7.5
WXO, WQ, WK, WV, WAO = range(5)
SLOT = [0, 1, 2, 0, 1]
SLOT0, SLOT1 = 2, 0


def wait(eng, sem, value):
    if not (isinstance(value, int) and value <= 0):
        eng.wait_ge(sem, value)


def wait_apart(eng, sem, value, passed):
    if not (isinstance(value, int) and value <= 0):
        eng.wait_ge(sem, value)
        eng.sem_inc(passed, 1)


class Steps:

    def __init__(self, eng, sem, base):
        self.eng, self.sem, self.base, self.n = eng, sem, base, 0

    def mark(self, ins):
        self.n += 1
        ins.then_inc(self.sem, 1)
        return self.base + self.n

    def need(self, value):
        self.eng.wait_ge(self.sem, value)


def build(nc, x, ctxT, mask, wqT, wkT, wvT, woT, bq, bk, bv, bo,
          aqT, akT, avT, aoT, a_gamma, a_beta, fqT, fsT, f_bias, f_la, f_lbT, f_gamma, f_beta, out):
    ctx = ExitStack()
    with ctx:
        def sb(name, shape, dt, st=ctx):
            return st.enter_context(nc.sbuf_tensor(name, shape, dt))

        def sem(name):
            return ctx.enter_context(nc.semaphore(name))

        ps = ctx.enter_context(nc.psum_tensor("ps", [P, 8, 512], F32))

        ident = sb("ident", [P, P], F32)
        causal = sb("causal", [P, P], F32)
        rowmask = sb("rowmask", [P, 4], F32)
        x_sb = sb("x_sb", [P, B, D], F32)
        o_tok = sb("o_tok", [P, B, D], F32)
        b_q = sb("b_q", [P, KD], F32)
        b_k = sb("b_k", [P, 2, KD], F32)
        b_kf = b_k[:].rearrange("p a m -> p (a m)")
        b_kn = sb("b_kn", [P, 2], F32)
        b_v = sb("b_v", [P, KD], F32)
        g_a = sb("g_a", [P, KD], F32)
        be_a = sb("be_a", [P, KD], F32)
        g_f = sb("g_f", [P, NBLK, KD], F32)
        be_f = sb("be_f", [P, NBLK, KD], F32)
        bo_bc = sb("bo_bc", [P, D], F32)
        stats = sb("stats", [P, B, 6], F32)
        mv = sb("mv", [P, B, 2], F32)
        ve = sb("ve", [P, B], F32)
        rs = sb("rs", [P, B], F32)
        rt = sb("rt", [P, B], F32)
        nh = sb("nh", [P, B], F32)
        nanfix = sb("nanfix", [P, 4], F32)
        mx = sb("mx", [P, 2, 2], F32)
        nb = sb("nb", [P, 2, 4], F32)
        rc = sb("rc", [P, 4], F32)
        osum = sb("osum", [P, 4, HD], F32)
        mx2 = sb("mx2", [P, 2, 4], F32)
        rc2 = sb("rc2", [P, 2, 4], F32)
        osum2 = sb("osum2", [P, 2, 4, HD], F32)
        is_low = sb("is_low", [P, 2], F32)
        gelu_tab = sb("gelu_tab", [P, 1], F32)

        st1 = ExitStack()
        craw = sb("craw", [P, 2, KD, 512], F32, st1)
        chi = sb("chi", [P, 2, KD, 512], F32R, st1)
        clo = sb("clo", [P, 2, KD, 512], F32R, st1)
        wraw = sb("wraw", [P, 2, KD, 256], F32, st1)
        whi = sb("whi", [P, 2, KD, 256], F32R, st1)
        wlo = sb("wlo", [P, 2, KD, 256], F32R, st1)
        khi = sb("khi", [P, 2, S2], F32R, st1)
        klo = sb("klo", [P, 2, S2], F32R, st1)
        qthi = sb("qthi", [P, KD, D], F32R, st1)
        qtlo = sb("qtlo", [P, KD, D], F32R, st1)
        qzhi = sb("qzhi", [P, HI, P], F32R, st1)
        qzlo = sb("qzlo", [P, HI, P], F32R, st1)
        vh = sb("vh", [P, S2 // P, HI, VW], BF16, st1)
        vrest = sb("vrest", [P, 2, 512], F32, st1)
        sm = sb("sm", [P, 2, S2], F32, st1)
        pthi = sb("pthi", [P, PTR, 4, P], F16, st1)
        ptlo = sb("ptlo", [P, PTR, 4, P], F16, st1)
        mbias = sb("mbias", [P, S2], BF16, st1)
        xnT_hi = khi[:, 0, :].rearrange("p (k t) -> p k t", k=KD)
        xnT_lo = klo[:, 0, :].rearrange("p (k t) -> p k t", k=KD)
        xn0 = sm[:, 0, :].rearrange("p (b d) -> p b d", b=B)
        mraw = sm[:, 1, :].bitcast(I32)
        st1.close()

        st2 = ExitStack()
        raw = sb("raw", [P, 2, KD, 512], F32, st2)
        Whi = sb("Whi", [P, 3, KD, 512], F32R, st2)
        Wlo = sb("Wlo", [P, 3, KD, 512], F32R, st2)
        aThi = sb("aThi", [P, KD, D], F32R, st2)
        aTlo = sb("aTlo", [P, KD, D], F32R, st2)
        tok = sb("tok", [P, B, D], F32, st2)
        g32 = sb("g32", [P, KD, D], F32, st2)
        dq_scale = sb("dq_scale", [P, KD, 512], F32, st2)
        dq_w = sb("dq_w", [P, KD, 512], F32, st2)
        lora_raw = sb("lora_raw", [P, 2, D], F32, st2)
        lora_hi = sb("lora_hi", [P, 2, D], F32R, st2)
        lora_st = sb("lora_st", [P, 2, 2, D], F32R, st2)
        st3 = ExitStack()
        qz2 = sb("qz2", [P, KD, 4, D], F32, st3)
        kT2 = sb("kT2", [P, KD, D], F32, st3)
        vh2 = sb("vh2", [P, B, H, VW], BF16, st3)
        vrest2 = tok
        sm2 = sb("sm2", [P, 2, 4, P], F32, st3)
        pthi2 = bo_bc[:].bitcast(F16).rearrange("p (s j q) -> p s j q", s=2, j=4)
        ptlo2 = sb("ptlo2", [P, 2, 4, P], F16, st3)
        st3.close()
        st4 = ExitStack()
        h_tok = sb("h_tok", [P, B, D], F32, st4)
        f_bc = sb("f_bc", [P, 2 * NBLK, D], F32, st4)
        st4.close()
        st2.close()

        s_x, s_m, s_wq, s_cst = sem("x_loaded"), sem("mask_loaded"), sem("wq_loaded"), sem("bias_loaded")
        s_id = sem("identity_ready")
        s_vec = sem("vector_chain")
        s_xn = sem("xn_ready")
        s_t0 = sem("xn_transposed")
        s_t0h = sem("xnT_hi_ready")
        s_t0l = sem("xnT_lo_ready")
        s_wq_hi, s_wq_lo = sem("wq_hi_ready"), sem("wq_lo_ready")
        s_q = sem("q_mm_done")
        s_qh, s_ql = sem("q_hi_ready"), sem("q_lo_ready")
        s_w = sem("kv_weights_loaded")
        s_w_hi, s_w_lo = sem("kv_weights_hi"), sem("kv_weights_lo")
        s_c = [sem("ctx_loaded0"), sem("ctx_loaded1")]
        s_c_hi, s_c_lo = sem("ctx_hi"), sem("ctx_lo")
        kv_mm = sem("kv_mm_done")
        kv_hi = sem("kv_hi_ready")
        kv_lo = sem("kv_lo_ready")
        v_mid = sem("v_mid_ready")
        v_all = sem("v_parts_ready")
        q_slots = sem("q_slots_ready")
        scores = sem("scores_done")
        masked = sem("scores_masked")
        nbias = sem("neg_max_ready")
        exps = sem("exp_done")
        tps = sem("weights_transposed")
        pt_hi, pt_lo = sem("weights_hi_ready"), sem("weights_lo_ready")
        pv = sem("pv_done")
        o_ready = sem("attn_out_ready")
        bk_now = sem("k_bias_in_place")
        passed_sp, passed_dve = sem("passed_sp"), sem("passed_dve")
        s_raw = [sem("raw_loaded0"), sem("raw_loaded1")]
        s_Whi, s_Wlo = sem("W_hi_ready"), sem("W_lo_ready")
        s_lin = sem("linear_done")
        s_T = sem("act_transposed")
        s_g = sem("act_full_ready")
        s_ah, s_al = sem("act_hi_ready"), sem("act_lo_ready")
        s_res = sem("residual_ready")
        s_tok = sem("tokens_ready")
        s_xb = sem("residual_bias_added")
        s_k2 = sem("self_k_ready")
        s_q2 = sem("self_q_ready")
        s_v1, s_vr, s_v2, s_v3 = sem("self_v_hi"), sem("self_v_rest"), sem("self_v_mid"), sem("self_v_low")
        u_s, u_m, u_nb, u_e = sem("self_scores"), sem("self_masked"), sem("self_neg_max"), sem("self_exp")
        u_t, u_h, u_l, u_pv, u_o = (sem("self_transposed"), sem("self_w_hi"), sem("self_w_lo"),
                                    sem("self_pv"), sem("self_out"))
        u_sum = sem("self_out_summed")
        s_pre, s_ffn = sem("vector_steps"), sem("vector_ffn_steps")
        s_ones2, s_h, s_fadd = sem("self_v_ones"), sem("h_ready"), sem("lora_added")
        passed_act, passed_pool = sem("passed_act"), sem("passed_pool")
        s_fq = [sem("ffn_levels0"), sem("ffn_levels1")]
        s_fs, s_fl, s_fb = sem("ffn_scale_loaded"), sem("ffn_lora_loaded"), sem("ffn_bias_loaded")
        s_dq1, s_dq2 = sem("dequant_levels"), sem("dequant_scaled")
        s_lora, s_fw = sem("lora_product"), sem("ffn_weight_lo")
        s_fhi = sem("ffn_weight_hi")
        s_lh, s_ls = sem("lora_hi"), sem("lora_stacked")
        s_tab = sem("gelu_table_input")
        s_hb = sem("h_bias_added")
        s_out, s_fin = sem("out_stored"), sem("out_ready")

        block = ctx.enter_context(nc.Block())

        ctxT_v = ctxT.rearrange("(k p) t -> p k t", p=P)

        def wview(w):
            return w.rearrange("(k p) o -> p k o", p=P)

        @block.sync
        def _(sp):
            sp.dma_start(x_sb[:], x.rearrange("(b p) d -> p b d", p=P)).then_inc(s_x, 16)
            sp.dma_start(mraw, mask).then_inc(s_m, 16)
            sp.dma_start(craw[:, 1], wview(wqT)).then_inc(s_wq, 16)
            sp.dma_start(craw[:, 0], ctxT_v[:, :, 0:512]).then_inc(s_c[0], 16)

            def load_kv_weights(p):
                wait(sp, s_w_lo, p)
                sp.dma_start(wraw[:, 0], wview(wkT)[:, :, 256 * p:256 * p + 256]).then_inc(s_w, 16)
                sp.dma_start(wraw[:, 1], wview(wvT)[:, :, 256 * p:256 * p + 256]).then_inc(s_w, 16)

            load_kv_weights(0)
            sp.wait_ge(s_wq_lo, 1)
            sp.dma_start(craw[:, 1], ctxT_v[:, :, 512:1024]).then_inc(s_c[1], 16)

            def ctx_load(i, kc):
                wait_apart(sp, s_c_lo, i * 4 + (kc - 1), passed_sp)
                sp.dma_start(craw[:, kc % 2], ctxT_v[:, :, bass.ds((i & 3) * S2 + kc * 512, 512)]
                             ).then_inc(s_c[kc % 2], 16)

            ctx_load(0, 2)
            ctx_load(0, 3)
            load_kv_weights(1)
            with sp.Fori(1, NI) as i:
                for kc in range(NKC):
                    ctx_load(i, kc)
            for n, w in enumerate((woT, aqT, akT, avT, aoT)):
                if n < 2:
                    sp.wait_ge(s_c_lo, NKC * NI)
                else:
                    sp.wait_ge(s_Wlo, n - 1)
                sp.dma_start(raw[:, n % 2], wview(w)).then_inc(s_raw[n % 2], 16)

            def ffn_levels(blk, a):
                if not isinstance(blk, int):
                    wait_apart(sp, s_dq1, KD * (2 * blk + (a - 1)), passed_sp)
                sp.dma_start(raw[:, 1 - a].bitcast(I32),
                             fqT[bass.ds(2 * blk + a, 1)].rearrange("one (k p) o -> p (one k) o", p=P)
                             ).then_inc(s_fq[a], 16)

            def ffn_scales(blk, a):
                if a == 1 or not isinstance(blk, int):
                    wait_apart(sp, s_dq2, KD * (2 * blk + a), passed_sp)
                sp.dma_start(dq_scale[:], fsT[bass.ds(2 * blk + a, 1)].rearrange("one (k p) o -> p (one k) o", p=P)
                             ).then_inc(s_fs, 16)

            def ffn_lora(blk, a):
                if a == 1 or not isinstance(blk, int):
                    wait_apart(sp, s_ls, 2 * (2 * blk + a), passed_sp)
                f = bass.ds(2 * blk + a, 1)
                for t, src in enumerate((f_la, f_lbT)):
                    for quad in range(4):
                        sp.dma_start(lora_raw[32 * quad:32 * quad + 32, t],
                                     src[f].rearrange("one r d -> r (one d)")).then_inc(s_fl, 16)

            sp.wait_ge(s_Wlo, 4)
            ffn_levels(0, 0)
            sp.wait_ge(o_ready, 6 * NI)
            ffn_scales(0, 0)
            ffn_lora(0, 0)
            ffn_lora(0, 1)
            sp.wait_ge(s_Wlo, 5)
            ffn_levels(0, 1)
            ffn_scales(0, 1)
            sp.wait_ge(u_s, NU)
            sp.dma_start(f_bc[:].rearrange("p f d -> p (f d)"),
                         f_bias.rearrange("f d -> (f d)").partition_broadcast(P)).then_inc(s_fb, 16)
            with sp.Fori(1, NBLK) as blk:
                for a in range(2):
                    ffn_lora(blk, a)
                    ffn_levels(blk, a)
                    ffn_scales(blk, a)
            out_v = out.rearrange("(b p) d -> p b d", p=P)
            for b in range(B):
                sp.wait_ge(s_fin, b + 1)
                sp.dma_start(out_v[:, b], h_tok[:, b]).then_inc(s_out, 16)
            sp.wait_ge(s_out, 16 * B)

        @block.gpsimd
        def _(pool):
            nc.gpsimd.memset(ident[:], 0.0).then_inc(s_id, 1)
            nc.gpsimd.memset(causal[:], 0.0).then_inc(s_id, 1)
            nc.gpsimd.memset(rowmask[:], 1.0).then_inc(s_id, 1)
            nc.gpsimd.memset(gelu_tab[:], 0.0).then_inc(s_tab, 1)
            nc.gpsimd.memset(is_low[:], 0.0).then_inc(s_tab, 1)
            for n, (quad, t) in enumerate(((1, 0), (3, 0), (2, 1), (3, 1))):
                pool.wait_ge(s_tab, n + 2)
                nc.gpsimd.memset(is_low[32 * quad:32 * quad + 32, t:t + 1], -1.0).then_inc(s_tab, 1)
            pool.wait_ge(s_tab, 6)
            nc.gpsimd.memset(vh[:, :, :, 3 * HD:VW], 1.0).then_inc(s_id, 1)
            nc.gpsimd.memset(qzhi[:].bitcast(F32), 0.0).then_inc(s_id, 1)
            nc.gpsimd.memset(qzlo[:].bitcast(F32), 0.0).then_inc(s_id, 1)
            pool.wait_ge(s_id, 6)
            nc.gpsimd.affine_select(out=ident[:], in_=ident[:], compare_op=ALU.not_equal, fill=1.0, base=0,
                                    pattern=[[-1, P]], channel_multiplier=1).then_inc(s_id, 1)
            nc.gpsimd.affine_select(out=causal[:], in_=causal[:], compare_op=ALU.is_ge, fill=NEG, base=0,
                                    pattern=[[-1, P]], channel_multiplier=1).then_inc(s_id, 1)
            nc.gpsimd.affine_select(out=rowmask[:], in_=rowmask[:], compare_op=ALU.is_ge, fill=0.0, base=0,
                                    pattern=[[-HD, 4]], channel_multiplier=1).then_inc(s_id, 1)
            pool.wait_ge(s_id, 9)
            nc.gpsimd.affine_select(out=rowmask[:], in_=rowmask[:], compare_op=ALU.is_ge, fill=0.0, base=HD - 1,
                                    pattern=[[HD, 4]], channel_multiplier=-1).then_inc(s_id, 1)
            pool.dma_start(b_q[:], bq).then_inc(s_cst, 16)
            pool.dma_start(b_k[:, :, 0:2], bk.rearrange("p (a m) -> p a m", a=2)).then_inc(s_cst, 16)
            pool.dma_start(b_v[:], bv).then_inc(s_cst, 16)
            pool.dma_start(g_a[:], a_gamma).then_inc(s_cst, 16)
            pool.dma_start(be_a[:], a_beta).then_inc(s_cst, 16)
            pool.dma_start(g_f[:], f_gamma).then_inc(s_cst, 16)
            pool.dma_start(be_f[:], f_beta).then_inc(s_cst, 16)
            pool.dma_start(bo_bc[:], bo.partition_broadcast(P)).then_inc(s_cst, 16)

            pool.wait_ge(s_wq_hi, 1)
            nc.gpsimd.tensor_tensor(clo[:, 1], craw[:, 1], chi[:, 1].bitcast(F32), ALU.subtract).then_inc(s_wq_lo, 1)

            def kv_weights_lo(p):
                pool.wait_ge(s_w_hi, p + 1)
                nc.gpsimd.tensor_tensor(wlo[:], wraw[:], whi[:].bitcast(F32), ALU.subtract).then_inc(s_w_lo, 1)

            def ctx_lo(i, kc):
                pool.wait_ge(s_c_hi, KD * (4 * i + (kc + 1)))
                nc.gpsimd.tensor_tensor(clo[:, kc % 2], craw[:, kc % 2], chi[:, kc % 2].bitcast(F32),
                                        ALU.subtract).then_inc(s_c_lo, 1)

            def v_low(i, n):
                pool.wait_ge(v_mid, 8 * i + (n + 1))
                v = vh[:, 2 * n:2 * n + 2]
                nc.gpsimd.tensor_tensor(v[:, :, :, 2 * HD:3 * HD],
                                        vrest[:, n % 2].rearrange("p (a h c) -> p a h c", a=2, c=HD),
                                        v[:, :, :, HD:2 * HD], ALU.subtract).then_inc(v_all, 1)

            def iteration(i, prefetch, weights=None):
                for kc in range(NKC):
                    if kc + 2 < NKC:
                        ctx_lo(i, kc + 2)
                    v_low(i, 2 * kc)
                    v_low(i, 2 * kc + 1)
                if weights is not None:
                    kv_weights_lo(weights)
                if prefetch:
                    ctx_lo(i + 1, 0)
                    ctx_lo(i + 1, 1)

            kv_weights_lo(0)
            ctx_lo(0, 0)
            ctx_lo(0, 1)
            pool.wait_ge(s_cst, 16 * 8)
            pool.wait_ge(s_x, 16)
            pool.wait_ge(s_xn, 1)
            for b in range(B):
                nc.gpsimd.tensor_tensor(x_sb[:, b], x_sb[:, b], bo_bc[:], ALU.add).then_inc(s_xb, 1)
            with pool.Fori(0, 3) as i:
                iteration(i, True)
            iteration(3, True, weights=1)
            with pool.Fori(4, NI - 1) as i:
                iteration(i, True)
            iteration(NI - 1, False)

            def weight_lo(n):
                pool.wait_ge(s_Whi, n + 1)
                nc.gpsimd.tensor_tensor(Wlo[:, SLOT[n]], raw[:, n % 2], Whi[:, SLOT[n]].bitcast(F32),
                                        ALU.subtract).then_inc(s_Wlo, 1)

            def dequantise(blk, a, ks=range(KD)):
                f = 2 * blk + a
                for k in ks:
                    if not (isinstance(f, int) and f == 0):
                        wait_apart(pool, s_fw, KD * (f - 1) + (k + 1), passed_pool)
                    if k == 0:
                        wait_apart(pool, s_fq[a], 16 * (blk + 1), passed_pool)
                    nc.gpsimd.tensor_scalar(dq_w[:, k], raw[:, 1 - a, k].bitcast(I32), DEQ, -1.0,
                                            ALU.mult, ALU.add).then_inc(s_dq1, 1)
                for k in ks:
                    if k == 0:
                        pool.wait_ge(s_fs, 16 * (f + 1))
                    pool.wait_ge(s_dq1, KD * f + (k + 1))
                    nc.gpsimd.tensor_tensor(dq_w[:, k], dq_w[:, k], dq_scale[:, k], ALU.mult).then_inc(s_dq2, 1)

            def ffn_weight_lo(f, slot):
                for k in range(KD):
                    pool.wait_ge(s_fhi, KD * f + (k + 1))
                    nc.gpsimd.tensor_tensor(Wlo[:, slot, k], dq_w[:, k], Whi[:, slot, k].bitcast(F32),
                                            ALU.subtract).then_inc(s_fw, 1)

            for n in (WXO, WQ, WK):
                weight_lo(n)
            pool.wait_ge(o_ready, 6 * NI)
            nc.gpsimd.memset(vh2[:, :, :, 3 * HD:VW], 1.0).then_inc(s_ones2, 1)
            weight_lo(WV)
            weight_lo(WAO)
            for b in range(B):
                pool.wait_ge(s_v2, b + 1)
                nc.gpsimd.tensor_tensor(vh2[:, b, :, 2 * HD:3 * HD],
                                        vrest2[:, b % 2].rearrange("p (h c) -> p h c", c=HD),
                                        vh2[:, b, :, HD:2 * HD], ALU.subtract).then_inc(s_v3, 1)
            for u in range(NU):
                if u in (4, 8):
                    dequantise(0, 0, (0, 1) if u == 4 else (2, 3))
                pool.wait_ge(u_sum, 2 * (u + 1))
                nc.gpsimd.tensor_tensor(o_tok[:, u // 4, P * (u % 4):P * (u % 4) + P].rearrange("p (h c) -> p h c", c=HD),
                                        osum2[:, u % 2], rc2[:, u % 2].unsqueeze(2).broadcast_to([P, 4, HD]),
                                        ALU.mult).then_inc(u_o, 1)
            ffn_weight_lo(0, SLOT0)
            dequantise(0, 1)

            def ffn_block(blk, last):
                ffn_weight_lo(2 * blk + 1, SLOT1)
                for b in range(B):
                    wait_apart(pool, s_T, 12 + 8 * blk + (b + 1), passed_pool)
                    nc.gpsimd.tensor_tensor(h_tok[:, b], h_tok[:, b],
                                            f_bc[:, bass.ds(2 * blk + 1, 1)].rearrange("p one d -> p (one d)"),
                                            ALU.add).then_inc(s_hb, 1)
                if last:
                    for b in range(B):
                        pool.wait_ge(s_hb, 4 * blk + b + 1)
                        nc.gpsimd.tensor_tensor(h_tok[:, b], h_tok[:, b], x_sb[:, b], ALU.add).then_inc(s_hb, 1)
                else:
                    dequantise(blk + 1, 0)
                    ffn_weight_lo(2 * blk + 2, SLOT0)
                    dequantise(blk + 1, 1)

            pool.wait_ge(s_fb, 16)
            with pool.Fori(0, NBLK - 1) as blk:
                ffn_block(blk, False)
            ffn_block(NBLK - 1, True)

        def split_product(out_ap, pairs, last_sem=None):
            n = len(pairs)
            for k, (lh, ll, rh, rl) in enumerate(pairs):
                nc.tensor.matmul(out_ap, lh, rh, start=(k == 0), stop=False)
                nc.tensor.matmul(out_ap, lh, rl, start=False, stop=False)
                mm = nc.tensor.matmul(out_ap, ll, rh, start=False, stop=(k == n - 1))
            if last_sem is not None:
                mm.then_inc(last_sem, 1)

        def ksl(m):
            return slice(P * m, P * m + P)

        @block.tensor
        def _(pe):
            pe.wait_ge(s_id, 7)
            pe.wait_ge(s_xn, 1)
            for k in range(KD):
                for b in range(B):
                    mm = nc.tensor.transpose(ps[:, k, ksl(b)], xn0[:, b, ksl(k)], ident[:])
                mm.then_inc(s_t0, 1)
            pe.wait_ge(s_wq_lo, 1)
            pe.wait_ge(s_t0l, KD)
            for m in range(KD):
                split_product(ps[:, 4 + m], [(chi[:, 1, k, ksl(m)], clo[:, 1, k, ksl(m)], xnT_hi[:, k], xnT_lo[:, k])
                                             for k in range(KD)], s_q)
            pe.wait_ge(s_ql, KD)

            with pe.Fori(0, NI) as i:
                pe.wait_ge(s_w_lo, (i >> 2) + 1)
                for kc in range(NKC):
                    pe.wait_ge(s_c_lo, 4 * i + (kc + 1))
                    c = kc % 2
                    for t in range(4):
                        n = 4 * kc + t
                        if n >= 4:
                            pe.wait_ge(kv_lo, 16 * i + (n - 3))
                        if t < 2:
                            split_product(ps[:, t], [(whi[:, 0, k, ksl(t)], wlo[:, 0, k, ksl(t)], chi[:, c, k], clo[:, c, k])
                                                     for k in range(KD)], kv_mm)
                        else:
                            for a in range(2):
                                q = 2 * (t - 2) + a
                                split_product(ps[:, t, 256 * a:256 * a + 256],
                                              [(chi[:, c, k, ksl(q)], clo[:, c, k, ksl(q)], whi[:, 1, k], wlo[:, 1, k])
                                               for k in range(KD)], kv_mm if a else None)
                pe.wait_ge(kv_lo, 16 * (i + 1))
                pe.wait_ge(q_slots, i + 1)

                def score(m):
                    h, c = m // NKC, m % NKC
                    if m >= 4 and c % 2 == 0:
                        pe.wait_ge(masked, 16 * i + (2 * (h - 1) + c // 2 + 1))
                    ks = slice(512 * c, 512 * c + 512)
                    split_product(ps[:, c], [(qzhi[:, h], qzlo[:, h], khi[:, h // 4, ks], klo[:, h // 4, ks])],
                                  scores if c % 2 else None)

                def transposes(n):
                    h, t = n // NKC, n % NKC
                    if t % 2 == 0:
                        pe.wait_ge(exps, 16 * i + (2 * h + t // 2 + 1))
                    if n >= TB:
                        pe.wait_ge(pt_lo, 32 * i + (n - TB + 1))
                    for y in range(4):
                        mm = nc.tensor.transpose(ps[:, 4 + n % TB, ksl(y)], sm[:, h % 2, ksl(4 * t + y)], ident[:])
                    mm.then_inc(tps, 1)

                def weighted(n):
                    h, t = n // NKC, n % NKC
                    pe.wait_ge(pt_lo, 32 * i + (n + 1))
                    if n == 0:
                        pe.wait_ge(v_all, 8 * (i + 1))
                    acc = ps[:, 6 + h // 4, VW * (h % 4):VW * (h % 4) + VW]
                    for y in range(4):
                        v = vh[:, 4 * t + y, h, :]
                        nc.tensor.matmul(acc, pthi[:, n % PTR, y], v, start=(t == 0 and y == 0), stop=False)
                        mm = nc.tensor.matmul(acc, ptlo[:, n % PTR, y], v, start=False, stop=(t == 3 and y == 3))
                    mm.then_inc(pv, 1)

                for n in range(-LEAD, NG + LAG):
                    if 0 <= n + LEAD < NG:
                        score(n + LEAD)
                    if 0 <= n < NG:
                        transposes(n)
                    if 0 <= n - LAG < NG:
                        weighted(n - LAG)
            def transpose_tile(src, b, base):
                wait(pe, s_al, base + (b - 1))
                for k in range(KD):
                    mm = nc.tensor.transpose(ps[:, b % 2, ksl(k)], src[:, b, ksl(k)], ident[:])
                mm.then_inc(s_T, 1)

            def lora_product(f, k, slot):
                if k == 0:
                    pe.wait_ge(s_ls, 2 * (f + 1))
                wait(pe, s_fadd, 4 * f + (k - 1))
                nc.tensor.matmul(ps[:, 2 + k % 2], lora_st[:, slot, 0, ksl(k)], lora_st[:, slot, 1],
                                 start=True, stop=True).then_inc(s_lora, 1)

            def linear_tile(b, slot, base, weight=None):
                pe.wait_ge(s_al, base + (b + 1))
                for k in range(KD):
                    if weight is not None and b == 0:
                        pe.wait_ge(s_fw, KD * weight + (k + 1))
                    lh, ll = aThi[:, k, ksl(b)], aTlo[:, k, ksl(b)]
                    nc.tensor.matmul(ps[:, 4 + b], lh, Whi[:, slot, k], start=(k == 0), stop=False)
                    nc.tensor.matmul(ps[:, 4 + b], lh, Wlo[:, slot, k], start=False, stop=False)
                    mm = nc.tensor.matmul(ps[:, 4 + b], ll, Whi[:, slot, k], start=False, stop=(k == KD - 1))
                mm.then_inc(s_lin, 1)

            def token_linear(transposed, slot, base, weight=None, build=None, build_slot=0, begun=False, ahead=None):
                if not begun:
                    transposed(0)
                    transposed(1)
                for b in range(B):
                    if build is not None and b == 0:
                        lora_product(build, 0, build_slot)
                        lora_product(build, 1, build_slot)
                    if b == B - 1 and ahead is not None:
                        ahead(0)
                        ahead(1)
                    linear_tile(b, slot, base, weight)
                    if b < 2:
                        transposed(b + 2)
                        if build is not None:
                            lora_product(build, b + 2, build_slot)

            def feature_linear(slot, free_sem):
                for m in range(KD):
                    if free_sem is not None:
                        pe.wait_ge(free_sem, m + 1)
                    split_product(ps[:, 4 + m], [(Whi[:, slot, k, ksl(m)], Wlo[:, slot, k, ksl(m)], aThi[:, k], aTlo[:, k])
                                                 for k in range(KD)], s_lin)

            def attention_out_tile(b):
                pe.wait_ge(o_ready, 6 * (HI // 2 + b + 1))
                if b == 0:
                    pe.wait_ge(masked, 16 * NI)
                transpose_tile(o_tok, b, 0)

            pe.wait_ge(s_Wlo, 1)
            token_linear(attention_out_tile, SLOT[WXO], 0)

            for b in range(B):
                pe.wait_ge(s_tok, b + 1)
                transpose_tile(tok, b, 4)
            pe.wait_ge(s_Wlo, 2)
            pe.wait_ge(s_al, 8)
            feature_linear(SLOT[WQ], None)
            pe.wait_ge(s_Wlo, 3)
            feature_linear(SLOT[WK], s_q2)
            pe.wait_ge(s_Wlo, 4)
            for b in range(B):
                pe.wait_ge(s_k2, b + 1)
                split_product(ps[:, 4 + b], [(aThi[:, k, ksl(b)], aTlo[:, k, ksl(b)], Whi[:, SLOT[WV], k], Wlo[:, SLOT[WV], k])
                                             for k in range(KD)], s_lin)
            pe.wait_ge(s_v3, B)
            pe.wait_ge(s_ones2, 1)
            for n in range(NU + 3):
                if n < NU:
                    b, g = n // 4, n % 4
                    wait(pe, u_m, n - 1)
                    for j in range(4):
                        mm = nc.tensor.matmul(ps[:, 2 + n % 2, ksl(j)], qz2[:, g, j, ksl(b)], kT2[:, g, ksl(b)],
                                              start=True, stop=True)
                    mm.then_inc(u_s, 1)
                if 0 <= n - 2 < NU:
                    u = n - 2
                    pe.wait_ge(u_e, u + 1)
                    wait(pe, u_l, u - 1)
                    for j in range(4):
                        mm = nc.tensor.transpose(ps[:, u % 2, ksl(j)], sm2[:, u % 2, j], ident[:])
                    mm.then_inc(u_t, 1)
                if 0 <= n - 3 < NU:
                    u = n - 3
                    b, g = u // 4, u % 4
                    pe.wait_ge(u_l, u + 1)
                    wait(pe, u_sum, 2 * (u - 1))
                    for j in range(4):
                        acc = ps[:, 6 + u % 2, VW * j:VW * j + VW]
                        nc.tensor.matmul(acc, pthi2[:, u % 2, j], vh2[:, b, 4 * g + j], start=True, stop=False)
                        mm = nc.tensor.matmul(acc, ptlo2[:, u % 2, j], vh2[:, b, 4 * g + j], start=False, stop=True)
                    mm.then_inc(u_pv, 1)
            def self_out_tile(b):
                pe.wait_ge(s_tok, 4 + b + 1)
                transpose_tile(tok, b, 8)

            def h_tile(blk, b):
                pe.wait_ge(s_h, 4 * blk + (b + 1))
                transpose_tile(h_tok, b, 12 + 8 * blk)

            pe.wait_ge(s_Wlo, 5)
            token_linear(self_out_tile, SLOT[WAO], 8, build=0)
            h_tile(0, 0)
            h_tile(0, 1)

            def ffn_block(blk, last):
                def normed_tile(b):
                    pe.wait_ge(s_tok, 8 + 4 * blk + (b + 1))
                    transpose_tile(tok, b, 16 + 8 * blk)

                token_linear(lambda b: h_tile(blk, b), SLOT0, 12 + 8 * blk, weight=2 * blk, build=2 * blk + 1, build_slot=1,
                             begun=True)
                token_linear(normed_tile, SLOT1, 16 + 8 * blk, weight=2 * blk + 1,
                             build=None if last else 2 * blk + 2,
                             ahead=None if last else (lambda b: h_tile(blk + 1, b)))

            with pe.Fori(0, NBLK - 1) as blk:
                ffn_block(blk, False)
            ffn_block(NBLK - 1, True)

        @block.scalar
        def _(act):
            def ident_bias(out_ap, in_ap, bias_ap):
                return nc.scalar.activation(out_ap, in_ap, ACT.Identity, bias=bias_ap)

            for k in range(KD):
                act.wait_ge(s_t0, k + 1)
                nc.scalar.copy(xnT_hi[:, k], ps[:, k]).then_inc(s_t0h, 1)
            act.wait_ge(s_cst, 16 * 8)
            for m in range(KD):
                act.wait_ge(s_q, m + 1)
                ident_bias(qthi[:, m], ps[:, 4 + m], b_q[:, m:m + 1]).then_inc(s_qh, 1)

            def ctx_hi_piece(i, kc, k):
                if k == 0:
                    act.wait_ge(s_c[kc], 32 * i + 16)
                nc.scalar.copy(chi[:, kc, k], craw[:, kc, k]).then_inc(s_c_hi, 1)

            def iteration(i, prefetch):
                def v_mid_part(n):
                    act.wait_ge(kv_lo, 16 * i + (4 * (n // 2) + 2 + n % 2 + 1))
                    nc.scalar.copy(vh[:, 2 * n:2 * n + 2, :, HD:2 * HD],
                                   vrest[:, n % 2].rearrange("p (a h c) -> p a h c", a=2, c=HD)).then_inc(v_mid, 1)

                act.wait_ge(bk_now, i + 1)
                for n in range(16):
                    kc, t = n // 4, n % 4
                    act.wait_ge(kv_mm, 16 * i + (n + 1))
                    if t < 2:
                        ident_bias(khi[:, t, 512 * kc:512 * kc + 512], ps[:, t],
                                   b_kn[:, t:t + 1]).then_inc(kv_hi, 1)
                    else:
                        v = 2 * kc + t - 2
                        nc.scalar.copy(vh[:, 2 * v:2 * v + 2, :, 0:HD],
                                       ps[:, t].rearrange("p (a h c) -> p a h c", a=2, c=HD)).then_inc(kv_hi, 1)
                        if v >= 1:
                            v_mid_part(v - 1)
                v_mid_part(7)

                def exp_half(h, half):
                    act.wait_ge(nbias, 8 * i + (h + 1))
                    s = sm[:, h % 2, 1024 * half:1024 * half + 1024]
                    nc.scalar.activation(s, s, ACT.Exp, bias=nb[:, h % 2, 0:1], scale=SCALE).then_inc(exps, 1)

                def weights_hi(n):
                    act.wait_ge(tps, 32 * i + (n + 1))
                    if n >= PTR:
                        act.wait_ge(pv, 32 * i + (n - PTR + 1))
                    nc.scalar.copy(pthi[:, n % PTR], ps[:, 4 + n % TB].rearrange("p (y q) -> p y q", y=4)).then_inc(pt_hi, 1)

                for n in range(-2, NG):
                    h, t = (n + 2) // NKC, (n + 2) % NKC
                    if h < HI and t % 2 == 0:
                        exp_half(h, t // 2)
                    if n >= 0:
                        weights_hi(n)
                    if 6 <= n < 6 + 2 * 2 * KD and n % 2 and prefetch:
                        ctx_hi_piece(i + 1, (n - 6) // (2 * KD), (n - 6) // 2 % KD)

            with act.Fori(0, NI - 1) as i:
                iteration(i, True)
            iteration(NI - 1, False)
            def head_view(ap):
                return ap.rearrange("p (h c) -> p h c", c=HD)

            def tile_view(ap, b):
                return ap[:, :, P * b:P * b + P]

            def bank_view(b):
                return ps[:, b % 2].rearrange("p (k t) -> p k t", k=KD)

            def high_tile(b, base):
                act.wait_ge(s_T, base + (b + 1))
                nc.scalar.copy(tile_view(aThi, b), bank_view(b)).then_inc(s_ah, 1)

            for b in range(B):
                act.wait_ge(s_T, b + 1)
                for k in range(KD):
                    ins = ident_bias(aThi[:, k, P * b:P * b + P], bank_view(b)[:, k], b_v[:, k:k + 1])
                ins.then_inc(s_ah, 1)
            for b in range(B):
                high_tile(b, 4)
            for m in range(KD):
                act.wait_ge(s_lin, 4 + m + 1)
                for j in range(4):
                    ins = nc.scalar.activation(qz2[:, m, j], ps[:, 4 + m], ACT.Copy, scale=rowmask[:, j:j + 1])
                ins.then_inc(s_q2, 1)
            for b in range(B + 1):
                if b < B:
                    act.wait_ge(s_lin, 12 + b + 1)
                    nc.scalar.copy(vh2[:, b, :, 0:HD], head_view(ps[:, 4 + b])).then_inc(s_v1, 1)
                if b >= 1:
                    act.wait_ge(s_vr, b)
                    nc.scalar.copy(vh2[:, b - 1, :, HD:2 * HD], head_view(vrest2[:, (b - 1) % 2])).then_inc(s_v2, 1)
            def lora_high(f):
                act.wait_ge(s_fl, 16 * 8 * (f + 1))
                wait(act, s_ls, 2 * f)
                nc.scalar.copy(lora_hi[:], lora_raw[:]).then_inc(s_lh, 1)

            lora_high(0)
            for n in range(NU + 2):
                if n >= 2:
                    u = n - 2
                    act.wait_ge(u_t, u + 1)
                    wait(act, u_pv, u - 1)
                    nc.scalar.copy(pthi2[:, u % 2], ps[:, u % 2].rearrange("p (j q) -> p j q", j=4)).then_inc(u_h, 1)
                if n < NU:
                    act.wait_ge(u_nb, n + 1)
                    for j in range(4):
                        ins = nc.scalar.activation(sm2[:, n % 2, j], sm2[:, n % 2, j], ACT.Exp, bias=nb[:, n % 2, j:j + 1])
                    ins.then_inc(u_e, 1)
            def ffn_weight_hi(f, slot, ks):
                for k in ks:
                    act.wait_ge(s_fadd, KD * f + (k + 1))
                    nc.scalar.copy(Whi[:, slot, k], dq_w[:, k]).then_inc(s_fhi, 1)

            lora_high(1)
            for b in range(B):
                act.wait_ge(s_T, 8 + b + 1)
                for k in range(KD):
                    ins = nc.scalar.activation(g32[:, k, P * b:P * b + P], bank_view(b)[:, k], ACT.Identity,
                                               scale=g_a[:, k:k + 1], bias=be_a[:, k:k + 1])
                ins.then_inc(s_g, 1)
            ffn_weight_hi(0, SLOT0, range(KD))

            g_ff = g_f[:].rearrange("p f k -> p (f k)")
            be_ff = be_f[:].rearrange("p f k -> p (f k)")

            def ffn_block(blk, last):
                if not last:
                    lora_high(2 * blk + 2)
                nc.scalar.activation(gelu_tab[:], gelu_tab[:], ACT.Gelu)
                high_tile(2, 12 + 8 * blk)
                ffn_weight_hi(2 * blk + 1, SLOT1, (0, 1))
                high_tile(3, 12 + 8 * blk)
                ffn_weight_hi(2 * blk + 1, SLOT1, (2, 3))
                if not last:
                    lora_high(2 * blk + 3)
                for b in range(B):
                    wait_apart(act, s_T, 16 + 8 * blk + (b + 1), passed_act)
                    for k in range(KD):
                        ins = nc.scalar.activation(g32[:, k, P * b:P * b + P], bank_view(b)[:, k], ACT.Gelu,
                                                   scale=g_ff[:, bass.ds(4 * blk + k, 1)],
                                                   bias=be_ff[:, bass.ds(4 * blk + k, 1)])
                    ins.then_inc(s_g, 1)
                if not last:
                    ffn_weight_hi(2 * blk + 2, SLOT0, range(KD))
                    high_tile(0, 20 + 8 * blk)
                    high_tile(1, 20 + 8 * blk)

            high_tile(0, 12)
            high_tile(1, 12)
            with act.Fori(0, NBLK - 1) as blk:
                ffn_block(blk, False)
            ffn_block(NBLK - 1, True)

        @block.vector
        def _(dve):
            chain = [0]

            def mark(ins):
                chain[0] += 1
                ins.then_inc(s_vec, 1)
                return chain[0]

            def link(ins):
                dve.wait_ge(s_vec, mark(ins))

            def kv_weights_hi(p):
                dve.wait_ge(s_w, 32 * (p + 1))
                wait(dve, kv_mm, 16 * 4 * p)
                nc.vector.tensor_copy(whi[:], wraw[:]).then_inc(s_w_hi, 1)

            def ctx_hi(i, kc, pieces=range(KD)):
                if 0 in pieces:
                    dve.wait_ge(s_c[kc % 2], 32 * i + 16 * (kc // 2 + 1))
                    wait(dve, kv_mm, 16 * i + 4 * (kc - 1))
                s = slice(pieces[0], pieces[-1] + 1)
                nc.vector.tensor_copy(chi[:, kc % 2, s], craw[:, kc % 2, s]).then_inc(s_c_hi, len(pieces))

            def rstd(mark, need, tiles):
                cols = [slice(b, b + 1) for b in tiles]
                for c, b in zip(cols, tiles):
                    mark(nc.vector.tensor_scalar(ve[:, c], mv[:, b, 1:2], LN_EPS, None, ALU.add))
                last = [mark(nc.vector.tensor_scalar(nh[:, c], mv[:, b, 1:2], LN_EPS, -0.5, ALU.add, ALU.mult))
                        for c, b in zip(cols, tiles)]

                def step(make):
                    for n, c in enumerate(cols):
                        need(last[n])
                        last[n] = mark(make(c))

                step(lambda c: nc.vector.tensor_scalar(rs[:, c].bitcast(I32), ve[:, c].bitcast(I32), -0.5,
                                                       float(0x5F3759DF), ALU.mult, ALU.add))
                for _ in range(3):
                    step(lambda c: nc.vector.scalar_tensor_tensor(out=rt[:, c], in0=rs[:, c], scalar=nh[:, c],
                                                                  in1=rs[:, c], op0=ALU.mult, op1=ALU.mult))
                    step(lambda c: nc.vector.scalar_tensor_tensor(out=rs[:, c], in0=rt[:, c], scalar=1.5,
                                                                  in1=rs[:, c], op0=ALU.add, op1=ALU.mult))
                need(last[-1])

            def weight_hi(n):
                dve.wait_ge(s_raw[n % 2], 16 * (n // 2 + 1))
                if n <= WK:
                    dve.wait_ge(kv_mm, 16 * NI)
                else:
                    dve.wait_ge(s_lin, 4 if n == WV else 8)
                nc.vector.tensor_copy(Whi[:, SLOT[n]], raw[:, n % 2]).then_inc(s_Whi, 1)

            dve.wait_ge(s_wq, 16)
            nc.vector.tensor_copy(chi[:, 1], craw[:, 1]).then_inc(s_wq_hi, 1)
            dve.wait_ge(s_x, 16)
            for b in range(B):
                link(nc.vector.bn_stats(stats[:, b], x_sb[:, b]))
                link(nc.vector.bn_aggr(mv[:, b], stats[:, b]))
            rstd(mark, lambda value: dve.wait_ge(s_vec, value), range(B))
            for b in range(B):
                ins = nc.vector.tensor_scalar(xn0[:, b], x_sb[:, b], mv[:, b, 0:1], rs[:, b:b + 1],
                                              ALU.subtract, ALU.mult)
            ins.then_inc(s_xn, 1)
            kv_weights_hi(0)
            ctx_hi(0, 0)
            for k in range(KD):
                dve.wait_ge(s_t0h, k + 1)
                nc.vector.tensor_tensor(xnT_lo[:, k], ps[:, k], xnT_hi[:, k].bitcast(F32), ALU.subtract).then_inc(s_t0l, 1)
            dve.wait_ge(s_m, 16)
            link(nc.vector.tensor_scalar(mbias[:], mraw, 0.0, NEG, ALU.is_equal, ALU.mult))
            link(nc.vector.tensor_reduce(nanfix[:, 0:1], mbias[:], AX.X, ALU.max))
            link(nc.vector.tensor_scalar(nanfix[:, 1:2], nanfix[:, 0:1], 0.1 * NEG, None, ALU.is_gt))
            link(nc.vector.reciprocal(nanfix[:, 2:3], nanfix[:, 1:2]))
            link(nc.vector.tensor_tensor(nanfix[:, 3:4], nanfix[:, 1:2], nanfix[:, 2:3], ALU.mult))
            for m in range(KD):
                dve.wait_ge(s_qh, m + 1)
                nc.vector.scalar_tensor_tensor(out=qtlo[:, m], in0=ps[:, 4 + m], scalar=b_q[:, m:m + 1],
                                               in1=qthi[:, m].bitcast(F32), op0=ALU.add, op1=ALU.subtract).then_inc(s_ql, 1)
            dve.wait_ge(s_q, KD)
            dve.wait_ge(s_ql, KD)
            ctx_hi(0, 1)
            pool_init = 6
            dve.wait_ge(s_id, pool_init)

            def iteration(i, prefetch, weights=None):
                def kv_rest(n):
                    kc, t = n // 4, n % 4
                    dve.wait_ge(kv_hi, 16 * i + (n + 1))
                    if t < 2:
                        ks = slice(512 * kc, 512 * kc + 512)
                        nc.vector.scalar_tensor_tensor(out=klo[:, t, ks], in0=ps[:, t],
                                                       scalar=b_kn[:, t:t + 1],
                                                       in1=khi[:, t, ks].bitcast(F32), op0=ALU.add,
                                                       op1=ALU.subtract).then_inc(kv_lo, 1)
                    else:
                        v = 2 * kc + t - 2
                        if v >= 2:
                            dve.wait_ge(v_all, 8 * i + (v - 1))
                        nc.vector.tensor_tensor(vrest[:, v % 2].rearrange("p (a h c) -> p a h c", a=2, c=HD),
                                                ps[:, t].rearrange("p (a h c) -> p a h c", a=2, c=HD),
                                                vh[:, 2 * v:2 * v + 2, :, 0:HD], ALU.subtract).then_inc(kv_lo, 1)

                nc.vector.tensor_copy(b_kn[:], b_kf[:, bass.ds(i & 4, 2)]).then_inc(bk_now, 1)
                for j in range(4):
                    rows = slice(32 * j, 32 * j + 32)
                    for dst, src in ((qzhi, qthi), (qzlo, qtlo)):
                        s = src[rows].rearrange("p m t -> p (m t)")
                        for g in range(2):
                            ins = nc.vector.tensor_copy(dst[rows, 4 * g + j],
                                                        s[:, bass.ds((i & 4) * 256 + (i & 3) * P + 512 * g, P)])
                ins.then_inc(q_slots, 1)
                dve.wait_ge(bk_now, i + 1)
                for n in range(16):
                    kv_rest(n)
                    if n in (4, 8):
                        ctx_hi(i, 2 + n // 8)

                def mask_half(h, half):
                    if h >= 2:
                        dve.wait_ge(tps, 32 * i + (4 * (h - 2) + 2 * half + 2))
                    if half:
                        dve.wait_ge(masked, 16 * i + (2 * h + 1))
                    wait_apart(dve, scores, 16 * i + (2 * h + half + 1), passed_dve)
                    s = slice(1024 * half, 1024 * half + 1024)
                    nc.vector.tensor_tensor_reduce(
                        sm[:, h % 2, s], ps[:, 2 * half:2 * half + 2].rearrange("p c t -> p (c t)"), mbias[:, s],
                        1.0, mx[:, h % 2, 0:1] if half else 3.0 * NEG, ALU.add, ALU.max,
                        mx[:, h % 2, half:half + 1]).then_inc(masked, 1)
                    if half:
                        dve.wait_ge(masked, 16 * i + (2 * h + 2))
                        nc.vector.tensor_scalar(nb[:, h % 2, 0:1], mx[:, h % 2, 1:2], -SCALE, PSHIFT,
                                                ALU.mult, ALU.add).then_inc(nbias, 1)

                def weights_lo(n):
                    dve.wait_ge(pt_hi, 32 * i + (n + 1))
                    nc.vector.tensor_tensor(ptlo[:, n % PTR], ps[:, 4 + n % TB].rearrange("p (y q) -> p y q", y=4),
                                            pthi[:, n % PTR], ALU.subtract).then_inc(pt_lo, 1)

                def normalise(g):
                    dve.wait_ge(pv, 32 * i + 16 * (g + 1))
                    acc = ps[:, 6 + g, 0:4 * VW].rearrange("p (h w) -> p h w", h=4)
                    nc.vector.reciprocal(rc[:], acc[:, :, 3 * HD]).then_inc(o_ready, 1)
                    nc.vector.tensor_reduce(osum[:], acc[:, :, 0:3 * HD].rearrange("p h (s c) -> p h c s", s=3),
                                            AX.X, ALU.add).then_inc(o_ready, 1)
                    dve.wait_ge(o_ready, 6 * i + (3 * g + 2))
                    dst = o_tok[:].rearrange("p b d -> p (b d)")[:, bass.ds((i & 3) * D + (i & 4) * 64 + P * g, P)]
                    nc.vector.scalar_tensor_tensor(out=dst, in0=osum[:].rearrange("p h c -> p (h c)"),
                                                   scalar=nanfix[:, 3:4],
                                                   in1=rc[:].unsqueeze(2).broadcast_to([P, 4, HD]),
                                                   op0=ALU.mult, op1=ALU.mult).then_inc(o_ready, 1)

                for n in range(1 - LEAD, NG):
                    m = n + LEAD
                    if m % 2 == 1 and m < NG:
                        mask_half(m // NKC, (m % NKC) // 2)
                    if n == NG // 2 + LAG:
                        normalise(0)
                    if n == 4 and weights is not None:
                        kv_weights_hi(weights)
                    if n in (8, 16, 24) and not prefetch:
                        weight_hi(n // 8 - 1)
                    if n >= 0:
                        weights_lo(n)
                normalise(1)

            with dve.Fori(0, 3) as i:
                iteration(i, True)
            iteration(3, True, weights=1)
            with dve.Fori(4, NI - 1) as i:
                iteration(i, True)
            iteration(NI - 1, False)
            def tile_view(ap, b):
                return ap[:, :, P * b:P * b + P]

            def low_tile(b, base, bias=None):
                dve.wait_ge(s_ah, base + (b + 1))
                bank = ps[:, b % 2].rearrange("p (k t) -> p k t", k=KD)
                if bias is None:
                    ins = nc.vector.tensor_tensor(tile_view(aTlo, b), bank, tile_view(aThi, b).bitcast(F32), ALU.subtract)
                else:
                    for k in range(KD):
                        t = slice(P * b, P * b + P)
                        ins = nc.vector.scalar_tensor_tensor(out=aTlo[:, k, t], in0=bank[:, k], scalar=bias[:, k:k + 1],
                                                             in1=aThi[:, k, t].bitcast(F32), op0=ALU.add, op1=ALU.subtract)
                ins.then_inc(s_al, 1)

            def both_parts(steps, b, base):
                dve.wait_ge(s_g, base + (b + 1))
                steps.need(steps.mark(nc.vector.tensor_copy(tile_view(aThi, b), tile_view(g32, b))))
                nc.vector.tensor_tensor(tile_view(aTlo, b), tile_view(g32, b), tile_view(aThi, b).bitcast(F32),
                                        ALU.subtract).then_inc(s_al, 1)

            def lora_add(f, k):
                dve.wait_ge(s_lora, KD * f + (k + 1))
                dve.wait_ge(s_dq2, KD * f + (k + 1))
                nc.vector.tensor_tensor(dq_w[:, k], dq_w[:, k], ps[:, 2 + k % 2], ALU.add).then_inc(s_fadd, 1)

            def lora_stack(f, slot):
                dve.wait_ge(s_lh, f + 1)
                for t in range(2):
                    nc.vector.scalar_tensor_tensor(out=lora_st[:, slot, t], in0=lora_hi[:, t].bitcast(F32),
                                                   scalar=is_low[:, t:t + 1], in1=lora_raw[:, t],
                                                   op0=ALU.mult, op1=ALU.add).then_inc(s_ls, 1)

            class Norm:

                def __init__(self, steps, src, dst, done):
                    self.steps, self.src, self.dst, self.done, self.seen = steps, src, dst, done, {}

                def stats(self, b, made=None):
                    if made is not None:
                        self.steps.need(made)
                    self.seen[b] = self.steps.mark(nc.vector.bn_stats(stats[:, b], self.src[:, b]))

                def finish(self, tiles):
                    s = self.steps
                    for b in tiles:
                        wait_apart(dve, s.sem, self.seen[b], passed_dve)
                        last = s.mark(nc.vector.bn_aggr(mv[:, b], stats[:, b]))
                    s.need(last)
                    rstd(s.mark, s.need, tiles)
                    for b in tiles:
                        nc.vector.tensor_scalar(self.dst[:, b], self.src[:, b], mv[:, b, 0:1], rs[:, b:b + 1],
                                                ALU.subtract, ALU.mult).then_inc(self.done, 1)

            def token_stage(steps, parts, produce, norm=None, build=None, stack=None, begun=False, ahead=None):
                if not begun:
                    parts(0)
                    parts(1)
                made = {}

                def tile(b):
                    made[b] = steps.mark(produce(b)) if norm is not None else produce(b)

                if stack is not None:
                    lora_stack(*stack)
                if build is not None:
                    lora_add(build, 0)
                    lora_add(build, 1)
                for b in range(2):
                    parts(b + 2)
                    tile(b)
                    if build is not None:
                        lora_add(build, b + 2)
                    if norm is not None:
                        norm.stats(b, made[b])
                if norm is not None:
                    norm.finish((0, 1))
                tile(2)
                if norm is not None:
                    norm.stats(2, made[2])
                    tile(3)
                if ahead is not None:
                    ahead(0)
                if norm is not None:
                    norm.stats(3, made[3])
                if ahead is not None:
                    ahead(1)
                if norm is not None:
                    norm.finish((2, 3))
                else:
                    tile(3)

            def residual_tile(base, need_bias=False):
                def produce(b):
                    if need_bias:
                        dve.wait_ge(s_xb, b + 1)
                    dve.wait_ge(s_lin, base + b + 1)
                    return nc.vector.tensor_tensor(x_sb[:, b], ps[:, 4 + b], x_sb[:, b], ALU.add)
                return produce

            steps = Steps(dve, s_pre, 0)
            norm = Norm(steps, x_sb, tok, s_tok)
            token_stage(steps, lambda b: low_tile(b, 0, b_v), residual_tile(0, True), norm,
                        ahead=lambda b: low_tile(b, 4))
            low_tile(2, 4)
            low_tile(3, 4)
            weight_hi(WV)
            for m in range(KD):
                dve.wait_ge(s_lin, 8 + m + 1)
                nc.vector.tensor_scalar(kT2[:, m], ps[:, 4 + m], SCALE, None, ALU.mult).then_inc(s_k2, 1)
                if m == 0:
                    weight_hi(WAO)
            for b in range(B):
                dve.wait_ge(s_v1, b + 1)
                if b >= 2:
                    dve.wait_ge(s_v3, b - 1)
                nc.vector.tensor_tensor(vrest2[:, b % 2].rearrange("p (h c) -> p h c", c=HD),
                                        ps[:, 4 + b].rearrange("p (h c) -> p h c", c=HD),
                                        vh2[:, b, :, 0:HD], ALU.subtract).then_inc(s_vr, 1)
            dve.wait_ge(s_tab, 6)
            lora_stack(0, 0)
            for n in range(NU + 4):
                if n < NU:
                    dve.wait_ge(u_s, n + 1)
                    wait(dve, u_t, n - 1)
                    wait(dve, u_nb, n - 1)
                    for j in range(4):
                        ins = nc.vector.tensor_tensor_reduce(sm2[:, n % 2, j], ps[:, 2 + n % 2, P * j:P * j + P],
                                                             causal[:], 1.0, 3.0 * NEG, ALU.add, ALU.max,
                                                             mx2[:, n % 2, j:j + 1])
                    ins.then_inc(u_m, 1)
                    dve.wait_ge(u_m, n + 1)
                    nc.vector.tensor_scalar(nb[:, n % 2], mx2[:, n % 2], -1.0, PSHIFT, ALU.mult, ALU.add).then_inc(u_nb, 1)
                if 0 <= n - 2 < NU:
                    u = n - 2
                    dve.wait_ge(u_h, u + 1)
                    nc.vector.tensor_tensor(ptlo2[:, u % 2], ps[:, u % 2].rearrange("p (j q) -> p j q", j=4),
                                            pthi2[:, u % 2], ALU.subtract).then_inc(u_l, 1)
                if 0 <= n - 4 < NU:
                    u = n - 4
                    dve.wait_ge(u_pv, u + 1)
                    wait(dve, u_o, u - 1)
                    acc = ps[:, 6 + u % 2, 0:4 * VW].rearrange("p (h w) -> p h w", h=4)
                    nc.vector.reciprocal(rc2[:, u % 2], acc[:, :, 3 * HD]).then_inc(u_sum, 1)
                    nc.vector.tensor_reduce(osum2[:, u % 2], acc[:, :, 0:3 * HD].rearrange("p h (s c) -> p h c s", s=3),
                                            AX.X, ALU.add).then_inc(u_sum, 1)
            norm = Norm(steps, o_tok, tok, s_tok)
            dve.wait_ge(u_o, NU)
            for pair in ((0, 1), (2, 3)):
                for b in pair:
                    norm.stats(b)
                norm.finish(pair)
            norm = Norm(steps, x_sb, h_tok, s_h)
            token_stage(steps, lambda b: both_parts(steps, b, 0), residual_tile(16), norm, build=0, stack=(1, 1),
                        ahead=lambda b: low_tile(b, 8))

            def ffn_block(blk, last):
                steps = Steps(dve, s_ffn, FFN_STEPS * blk)

                def first(b):
                    dve.wait_ge(s_lin, 20 + 8 * blk + (b + 1))
                    return nc.vector.tensor_tensor(tok[:, b], ps[:, 4 + b],
                                                   f_bc[:, bass.ds(2 * blk, 1)].rearrange("p one d -> p (one d)"), ALU.add)

                def second(b):
                    dve.wait_ge(s_hb, 4 * blk + (b + 1) + (B if last else 0))
                    dve.wait_ge(s_lin, 24 + 8 * blk + (b + 1))
                    ins = nc.vector.tensor_tensor(h_tok[:, b], ps[:, 4 + b], h_tok[:, b], ALU.add)
                    return ins.then_inc(s_fin if last else s_h, 1)

                norm = Norm(steps, tok, tok, s_tok)
                token_stage(steps, lambda b: low_tile(b, 8 + 4 * blk), first, norm, build=2 * blk + 1,
                            stack=None if last else (2 * blk + 2, 0), begun=True,
                            ahead=lambda b: both_parts(steps, b, 4 + 4 * blk))
                token_stage(steps, lambda b: both_parts(steps, b, 4 + 4 * blk), second, None,
                            build=None if last else 2 * blk + 2, stack=None if last else (2 * blk + 3, 1), begun=True,
                            ahead=None if last else (lambda b: low_tile(b, 12 + 4 * blk)))
                if not last:
                    assert steps.n == FFN_STEPS, steps.n

            dve.wait_ge(s_fb, 16)
            with dve.Fori(0, NBLK - 1) as blk:
                ffn_block(blk, False)
            ffn_block(NBLK - 1, True)


def kernel(**inputs):
    import concourse.bacc as bacc
    from concourse.bass_utils import run_bass_kernel_spmd

    nc = bacc.Bacc("TRN2", target_bir_lowering=False, num_devices=1)
    g = {k: np.asarray(v) for k, v in inputs.items()}

    def cols(v):
        return v.reshape(KD, P).T

    av = g["L0_attn_Wv"].reshape(HD, H, D).transpose(1, 0, 2).reshape(D, D)
    fq = g["L0_ffn_qweights"]
    data = {
        "x": g["x"].reshape(B * P, D),
        "ctxT": g["ctx_1024"].reshape(B * S2, D).T,
        "mask": g["mask_1x1xSxS2_ik0"].reshape(P, S2),
        "wqT": g["L0_xattn_Wq"].T, "wkT": g["L0_xattn_Wk"].T, "wvT": g["L0_xattn_Wv"].T, "woT": g["L0_xattn_Wo"].T,
        "bq": cols(g["L0_xattn_bq"]), "bk": cols(g["L0_xattn_bk"]), "bv": cols(g["L0_xattn_bv"]),
        "bo": g["L0_xattn_bo"],
        "aqT": g["L0_attn_Wq"].T, "akT": g["L0_attn_Wk"].T, "avT": av.T, "aoT": g["L0_attn_Wo"].T,
        "a_gamma": cols(g["L0_attn_gamma"]), "a_beta": cols(g["L0_attn_beta"]),
        "fqT": fq.transpose(0, 2, 1), "fsT": np.repeat(g["L0_ffn_scales"].transpose(0, 2, 1), 16, axis=1),
        "f_bias": g["L0_ffn_biases"],
        "f_la": g["L0_ffn_lora_a"], "f_lbT": g["L0_ffn_lora_b"].transpose(0, 2, 1),
        "f_gamma": g["L0_ffn_ln_gamma"].reshape(NBLK, KD, P).transpose(2, 0, 1),
        "f_beta": g["L0_ffn_ln_beta"].reshape(NBLK, KD, P).transpose(2, 0, 1),
    }
    arrays, args = {}, {}
    for name, a in data.items():
        a = np.ascontiguousarray(a)
        arrays["in_" + name] = a
        args[name] = nc.dram_tensor("in_" + name, a.shape, mybir.dt.from_np(a.dtype), kind="ExternalInput").ap()
    args["out"] = nc.dram_tensor("out", (B * P, D), F32, kind="ExternalOutput").ap()
    build(nc, **args)
    r = run_bass_kernel_spmd(nc, [arrays], core_ids=[0])
    return r.results[0]["out"].reshape(B, P, D)
```

```python
from contextlib import ExitStack
import math

import numpy as np

import concourse.bass as bass
from concourse import mybir

ALU = mybir.AluOpType
ACT = mybir.ActivationFunctionType
AX = mybir.AxisListType
F32 = mybir.dt.float32
F32R = mybir.dt.float32r
F16 = mybir.dt.float16
BF16 = mybir.dt.bfloat16
I32 = mybir.dt.int32

P = 128
B = 4
D = 512
KD = D // P
H = 16
HD = D // H
S2 = 2048
NKC = S2 // 512
NI = 2 * B
HI = H // 2
KEY_STACK = (0, 1, 2, 0)
QUERY_STACK = ((0, 0, 0, 1), (2, 1, 1))
NQ = 4 * sum(len(q) for q in QUERY_STACK)
KSLOTS = 4
VW = 3 * HD + 2
SCALE = HD ** -0.5
NEG = -1.0e30
LN_EPS = 1e-5
PSHIFT = math.log(4096.0)
LEAD = 7
LAG = 3
NG = HI * NKC
PTR = 4
TB = 2
NBLK = 3
NU = B * H // 4
FFN_STEPS = 52
DEQ = 1.0 / 7.5
WXO, WQ, WK, WV, WAO = range(5)
SLOT = [0, 1, 2, 0, 1]
SLOT0, SLOT1 = 2, 0


def wait(eng, sem, value):
    if not (isinstance(value, int) and value <= 0):
        eng.wait_ge(sem, value)


def wait_apart(eng, sem, value, passed):
    if not (isinstance(value, int) and value <= 0):
        eng.wait_ge(sem, value)
        eng.sem_inc(passed, 1)


class Steps:

    def __init__(self, eng, sem, base):
        self.eng, self.sem, self.base, self.n = eng, sem, base, 0

    def mark(self, ins):
        self.n += 1
        ins.then_inc(self.sem, 1)
        return self.base + self.n

    def need(self, value):
        self.eng.wait_ge(self.sem, value)


def build(nc, x, ctxT, mask, wqT, wkT, wvT, woT, bq, bk, bv, bo,
          aqT, akT, avT, aoT, a_gamma, a_beta, fqT, fsT, f_bias, f_la, f_lbT, f_gamma, f_beta, out):
    ctx = ExitStack()
    with ctx:
        def sb(name, shape, dt, st=ctx):
            return st.enter_context(nc.sbuf_tensor(name, shape, dt))

        def sem(name):
            return ctx.enter_context(nc.semaphore(name))

        ps = ctx.enter_context(nc.psum_tensor("ps", [P, 8, 512], F32))

        ident = sb("ident", [P, P], F32)
        causal = sb("causal", [P, P], F32)
        rowmask = sb("rowmask", [P, 4], F32)
        x_sb = sb("x_sb", [P, B, D], F32)
        o_tok = sb("o_tok", [P, B, D], F32)
        b_q = sb("b_q", [P, KD], F32)
        b_k = sb("b_k", [P, 2, KD], F32)
        b_kf = b_k[:].rearrange("p a m -> p (a m)")
        b_kn = sb("b_kn", [P, 2], F32)
        b_v = sb("b_v", [P, KD], F32)
        g_a = sb("g_a", [P, KD], F32)
        be_a = sb("be_a", [P, KD], F32)
        g_f = sb("g_f", [P, NBLK, KD], F32)
        be_f = sb("be_f", [P, NBLK, KD], F32)
        stats = sb("stats", [P, B, 6], F32)
        mv = sb("mv", [P, B, 2], F32)
        ve = sb("ve", [P, B], F32)
        rs = sb("rs", [P, B], F32)
        rt = sb("rt", [P, B], F32)
        nh = sb("nh", [P, B], F32)
        nanfix = sb("nanfix", [P, 4], F32)
        mx = sb("mx", [P, 2, 2], F32)
        nb = sb("nb", [P, 2, 4], F32)
        rc = sb("rc", [P, 4], F32)
        osum = sb("osum", [P, 4, HD], F32)
        mx2 = sb("mx2", [P, 2, 4], F32)
        rc2 = sb("rc2", [P, 2, 4], F32)
        osum2 = sb("osum2", [P, 2, 4, HD], F32)
        is_low = sb("is_low", [P, 2], F32)
        gelu_tab = sb("gelu_tab", [P, 1], F32)

        st1 = ExitStack()
        craw = sb("craw", [P, 2, KD, 512], F32, st1)
        chi = sb("chi", [P, 2, KD, 512], F32R, st1)
        clo = sb("clo", [P, 2, KD, 512], F32R, st1)
        wraw = sb("wraw", [P, 2, KD, 256], F32, st1)
        whi = sb("whi", [P, 2, KD, 256], F32R, st1)
        wlo = sb("wlo", [P, 2, KD, 256], F32R, st1)
        st0 = ExitStack()
        xnT_hi = sb("xnT_hi", [P, KD, D], F32R, st0)
        xnT_lo = sb("xnT_lo", [P, KD, D], F32R, st0)
        st0.close()
        kparts = sb("kparts", [P, 3, 2, S2], BF16, st1)
        kst = sb("kst", [P, KSLOTS, S2], BF16, st1)
        qparts = sb("qparts", [P, 3, 2, B, 2, P], BF16, st1)
        qst = sb("qst", [P, 2, 2, 4, P], BF16, st1)
        vh = sb("vh", [P, S2 // P, HI, VW], BF16, st1)
        rest = sb("rest", [P, 4, 512], F32, st1)
        sm = sb("sm", [P, 2, S2], F32, st1)
        pthi = sb("pthi", [P, PTR, 4, P], F16, st1)
        ptlo = sb("ptlo", [P, PTR, 4, P], F16, st1)
        mbias = sb("mbias", [P, S2], BF16, st1)
        qparts_flat = qparts[:].rearrange("p s a b g t -> p s (a b g t)")
        xn0 = sm[:, 0, :].rearrange("p (b d) -> p b d", b=B)
        bo_bc = kst[:, KSLOTS - 1, 0:2 * D].bitcast(F32)
        mraw = sm[:, 1, :].bitcast(I32)
        st1.close()

        st2 = ExitStack()
        raw = sb("raw", [P, 2, KD, 512], F32, st2)
        Whi = sb("Whi", [P, 3, KD, 512], F32R, st2)
        Wlo = sb("Wlo", [P, 3, KD, 512], F32R, st2)
        aThi = sb("aThi", [P, KD, D], F32R, st2)
        aTlo = sb("aTlo", [P, KD, D], F32R, st2)
        tok = sb("tok", [P, B, D], F32, st2)
        g32 = sb("g32", [P, KD, D], F32, st2)
        dq_scale = sb("dq_scale", [P, KD, 512], F32, st2)
        dq_w = sb("dq_w", [P, KD, 512], F32, st2)
        lora_raw = sb("lora_raw", [P, 2, D], F32, st2)
        lora_hi = sb("lora_hi", [P, 2, D], F32R, st2)
        lora_st = sb("lora_st", [P, 2, 2, D], F32R, st2)
        st3 = ExitStack()
        qz2 = sb("qz2", [P, KD, 4, D], F32, st3)
        kT2 = sb("kT2", [P, KD, D], F32, st3)
        vh2 = sb("vh2", [P, B, H, VW], BF16, st3)
        vrest2 = tok
        sm2 = sb("sm2", [P, 2, 4, P], F32, st3)
        pthi2 = sb("pthi2", [P, 2, 4, P], F16, st3)
        ptlo2 = sb("ptlo2", [P, 2, 4, P], F16, st3)
        st3.close()
        st4 = ExitStack()
        h_tok = sb("h_tok", [P, B, D], F32, st4)
        f_bc = sb("f_bc", [P, 2 * NBLK, D], F32, st4)
        st4.close()
        st2.close()

        s_x, s_m, s_wq, s_cst = sem("x_loaded"), sem("mask_loaded"), sem("wq_loaded"), sem("bias_loaded")
        s_id = sem("identity_ready")
        s_vec = sem("vector_chain")
        s_xn = sem("xn_ready")
        s_t0 = sem("xn_transposed")
        s_t0h = sem("xnT_hi_ready")
        s_t0l = sem("xnT_lo_ready")
        s_wq_hi, s_wq_lo = sem("wq_hi_ready"), sem("wq_lo_ready")
        s_q = sem("q_mm_done")
        s_qh, s_ql = sem("q_hi_ready"), sem("q_lo_ready")
        s_w = sem("kv_weights_loaded")
        s_w_hi, s_w_lo = sem("kv_weights_hi"), sem("kv_weights_lo")
        s_c = [sem("ctx_loaded0"), sem("ctx_loaded1")]
        s_c_hi, s_c_lo = sem("ctx_hi"), sem("ctx_lo")
        kv_mm = sem("kv_mm_done")
        kv_hi = sem("kv_hi_ready")
        kv_lo = sem("kv_lo_ready")
        v_mid = sem("v_mid_ready")
        v_all = sem("v_parts_ready")
        q_stack = sem("q_stack_loaded")
        s_qm, s_ql3 = sem("q_mid_ready"), sem("q_low_ready")
        k_stack = [sem("k_stack_loaded%d" % n) for n in range(KSLOTS)]
        scores = sem("scores_done")
        masked = sem("scores_masked")
        nbias = sem("neg_max_ready")
        exps = sem("exp_done")
        tps = sem("weights_transposed")
        pt_hi, pt_lo = sem("weights_hi_ready"), sem("weights_lo_ready")
        pv = sem("pv_done")
        o_ready = sem("attn_out_ready")
        bk_now = sem("k_bias_in_place")
        passed_sp, passed_dve = sem("passed_sp"), sem("passed_dve")
        s_raw = [sem("raw_loaded0"), sem("raw_loaded1")]
        s_Whi, s_Wlo = sem("W_hi_ready"), sem("W_lo_ready")
        s_lin = sem("linear_done")
        s_T = sem("act_transposed")
        s_g = sem("act_full_ready")
        s_ah, s_al = sem("act_hi_ready"), sem("act_lo_ready")
        s_res = sem("residual_ready")
        s_tok = sem("tokens_ready")
        s_xb = sem("residual_bias_added")
        s_k2 = sem("self_k_ready")
        s_q2 = sem("self_q_ready")
        s_v1, s_vr, s_v2, s_v3 = sem("self_v_hi"), sem("self_v_rest"), sem("self_v_mid"), sem("self_v_low")
        u_s, u_m, u_nb, u_e = sem("self_scores"), sem("self_masked"), sem("self_neg_max"), sem("self_exp")
        u_t, u_h, u_l, u_pv, u_o = (sem("self_transposed"), sem("self_w_hi"), sem("self_w_lo"),
                                    sem("self_pv"), sem("self_out"))
        u_sum = sem("self_out_summed")
        s_pre, s_ffn = sem("vector_steps"), sem("vector_ffn_steps")
        s_ones2, s_h, s_fadd = sem("self_v_ones"), sem("h_ready"), sem("lora_added")
        passed_act, passed_pool = sem("passed_act"), sem("passed_pool")
        s_fq = [sem("ffn_levels0"), sem("ffn_levels1")]
        s_fs, s_fl, s_fb = sem("ffn_scale_loaded"), sem("ffn_lora_loaded"), sem("ffn_bias_loaded")
        s_dq1, s_dq2 = sem("dequant_levels"), sem("dequant_scaled")
        s_lora, s_fw = sem("lora_product"), sem("ffn_weight_lo")
        s_fhi = sem("ffn_weight_hi")
        s_lh, s_ls = sem("lora_hi"), sem("lora_stacked")
        s_tab = sem("gelu_table_input")
        s_hb = sem("h_bias_added")
        s_out, s_fin = sem("out_stored"), sem("out_ready")

        block = ctx.enter_context(nc.Block())

        ctxT_v = ctxT.rearrange("(k p) t -> p k t", p=P)

        def wview(w):
            return w.rearrange("(k p) o -> p k o", p=P)

        @block.sync
        def _(sp):
            sp.dma_start(x_sb[:], x.rearrange("(b p) d -> p b d", p=P)).then_inc(s_x, 16)
            sp.dma_start(craw[:, 1], wview(wqT)).then_inc(s_wq, 16)
            sp.dma_start(b_q[:], bq).then_inc(s_cst, 16)
            sp.dma_start(craw[:, 0], ctxT_v[:, :, 0:512]).then_inc(s_c[0], 16)

            def load_kv_weights(p):
                wait(sp, s_w_lo, p)
                sp.dma_start(wraw[:, 0], wview(wkT)[:, :, 256 * p:256 * p + 256]).then_inc(s_w, 16)
                sp.dma_start(wraw[:, 1], wview(wvT)[:, :, 256 * p:256 * p + 256]).then_inc(s_w, 16)

            load_kv_weights(0)
            sp.dma_start(b_k[:, :, 0:2], bk.rearrange("p (a m) -> p a m", a=2)).then_inc(s_cst, 16)
            sp.dma_start(b_v[:], bv).then_inc(s_cst, 16)
            sp.dma_start(g_a[:], a_gamma).then_inc(s_cst, 16)
            sp.dma_start(be_a[:], a_beta).then_inc(s_cst, 16)
            sp.dma_start(g_f[:], f_gamma).then_inc(s_cst, 16)
            sp.dma_start(be_f[:], f_beta).then_inc(s_cst, 16)
            sp.dma_start(bo_bc, bo.partition_broadcast(P)).then_inc(s_cst, 16)
            sp.dma_start(mraw, mask).then_inc(s_m, 16)
            sp.wait_ge(s_wq_lo, 1)
            sp.dma_start(craw[:, 1], ctxT_v[:, :, 512:1024]).then_inc(s_c[1], 16)

            def ctx_load(i, kc):
                wait_apart(sp, s_c_lo, i * 4 + (kc - 1), passed_sp)
                sp.dma_start(craw[:, kc % 2], ctxT_v[:, :, bass.ds((i & 3) * S2 + kc * 512, 512)]
                             ).then_inc(s_c[kc % 2], 16)

            ctx_load(0, 2)
            ctx_load(0, 3)
            load_kv_weights(1)
            def stack_queries(i):
                for j in range(4):
                    for turn, parts in enumerate(QUERY_STACK):
                        for quad, part in enumerate(parts):
                            sp.dma_start(qst[HD * quad:HD * quad + HD, turn, :, j],
                                         qparts_flat[HD * j:HD * j + HD, part, bass.ds(i * 256, 256)
                                                     ].rearrange("p (g t) -> p g t", g=2)).then_inc(q_stack, 16)

            def stack_keys(i, h):
                if h in (0, 4):
                    wait_apart(sp, v_all, 16 * i + (4 * (NKC - 1) + h // 4 + 1), passed_sp)
                if h >= KSLOTS:
                    wait_apart(sp, scores, 16 * i + 2 * (h - KSLOTS + 1), passed_sp)
                j = h % 4
                for quad, part in enumerate(KEY_STACK):
                    sp.dma_start(kst[HD * quad:HD * quad + HD, h % KSLOTS], kparts[HD * j:HD * j + HD, part, h // 4]
                                 ).then_inc(k_stack[h % KSLOTS], 16)

            def iteration(i, prefetch):
                stack_queries(i)
                if prefetch:
                    ctx_load(i + 1, 0)
                    ctx_load(i + 1, 1)
                for h in range(HI):
                    if h == KSLOTS and not prefetch:
                        sp.wait_ge(s_c_lo, NKC * NI)
                        load_raw(0)
                        load_raw(1)
                    stack_keys(i, h)
                if prefetch:
                    ctx_load(i + 1, 2)
                    ctx_load(i + 1, 3)

            def load_raw(n):
                if n >= 2:
                    sp.wait_ge(s_Wlo, n - 1)
                sp.dma_start(raw[:, n % 2], wview((woT, aqT, akT, avT, aoT)[n])).then_inc(s_raw[n % 2], 16)

            sp.wait_ge(s_id, 5)
            sp.wait_ge(s_ql3, KD)
            iteration(0, True)
            with sp.Fori(1, NI - 1) as i:
                wait_apart(sp, scores, 16 * i, passed_sp)
                iteration(i, True)
            sp.wait_ge(scores, 16 * (NI - 1))
            iteration(NI - 1, False)
            for n in (WK, WV, WAO):
                load_raw(n)

            def ffn_levels(blk, a):
                if not isinstance(blk, int):
                    wait_apart(sp, s_dq1, KD * (2 * blk + (a - 1)), passed_sp)
                sp.dma_start(raw[:, 1 - a].bitcast(I32),
                             fqT[bass.ds(2 * blk + a, 1)].rearrange("one (k p) o -> p (one k) o", p=P)
                             ).then_inc(s_fq[a], 16)

            def ffn_scales(blk, a):
                if a == 1 or not isinstance(blk, int):
                    wait_apart(sp, s_dq2, KD * (2 * blk + a), passed_sp)
                sp.dma_start(dq_scale[:], fsT[bass.ds(2 * blk + a, 1)].rearrange("one (k p) o -> p (one k) o", p=P)
                             ).then_inc(s_fs, 16)

            def ffn_lora(blk, a):
                if a == 1 or not isinstance(blk, int):
                    wait_apart(sp, s_ls, 2 * (2 * blk + a), passed_sp)
                f = bass.ds(2 * blk + a, 1)
                for t, src in enumerate((f_la, f_lbT)):
                    for quad in range(4):
                        sp.dma_start(lora_raw[32 * quad:32 * quad + 32, t],
                                     src[f].rearrange("one r d -> r (one d)")).then_inc(s_fl, 16)

            sp.wait_ge(s_Wlo, 4)
            ffn_levels(0, 0)
            sp.wait_ge(o_ready, 6 * NI)
            ffn_scales(0, 0)
            ffn_lora(0, 0)
            ffn_lora(0, 1)
            sp.wait_ge(s_Wlo, 5)
            ffn_levels(0, 1)
            ffn_scales(0, 1)
            sp.wait_ge(u_s, NU)
            sp.dma_start(f_bc[:].rearrange("p f d -> p (f d)"),
                         f_bias.rearrange("f d -> (f d)").partition_broadcast(P)).then_inc(s_fb, 16)
            with sp.Fori(1, NBLK) as blk:
                for a in range(2):
                    ffn_lora(blk, a)
                    ffn_levels(blk, a)
                    ffn_scales(blk, a)
            out_v = out.rearrange("(b p) d -> p b d", p=P)
            for b in range(B):
                sp.wait_ge(s_fin, b + 1)
                sp.dma_start(out_v[:, b], h_tok[:, b]).then_inc(s_out, 16)
            sp.wait_ge(s_out, 16 * B)

        @block.gpsimd
        def _(pool):
            nc.gpsimd.memset(ident[:], 0.0).then_inc(s_id, 1)
            nc.gpsimd.memset(causal[:], 0.0).then_inc(s_id, 1)
            nc.gpsimd.memset(rowmask[:], 1.0).then_inc(s_id, 1)
            nc.gpsimd.memset(gelu_tab[:], 0.0).then_inc(s_tab, 1)
            nc.gpsimd.memset(is_low[:], 0.0).then_inc(s_tab, 1)
            for n, (quad, t) in enumerate(((1, 0), (3, 0), (2, 1), (3, 1))):
                pool.wait_ge(s_tab, n + 2)
                nc.gpsimd.memset(is_low[32 * quad:32 * quad + 32, t:t + 1], -1.0).then_inc(s_tab, 1)
            pool.wait_ge(s_tab, 6)
            nc.gpsimd.memset(vh[:, :, :, 3 * HD:VW], 1.0).then_inc(s_id, 1)
            nc.gpsimd.memset(qst[:, 1], 0.0).then_inc(s_id, 1)
            pool.wait_ge(s_id, 5)
            nc.gpsimd.affine_select(out=ident[:], in_=ident[:], compare_op=ALU.not_equal, fill=1.0, base=0,
                                    pattern=[[-1, P]], channel_multiplier=1).then_inc(s_id, 1)
            nc.gpsimd.affine_select(out=causal[:], in_=causal[:], compare_op=ALU.is_ge, fill=NEG, base=0,
                                    pattern=[[-1, P]], channel_multiplier=1).then_inc(s_id, 1)
            nc.gpsimd.affine_select(out=rowmask[:], in_=rowmask[:], compare_op=ALU.is_ge, fill=0.0, base=0,
                                    pattern=[[-HD, 4]], channel_multiplier=1).then_inc(s_id, 1)
            pool.wait_ge(s_id, 8)
            nc.gpsimd.affine_select(out=rowmask[:], in_=rowmask[:], compare_op=ALU.is_ge, fill=0.0, base=HD - 1,
                                    pattern=[[HD, 4]], channel_multiplier=-1).then_inc(s_id, 1)
            pool.wait_ge(s_wq_hi, 1)
            nc.gpsimd.tensor_tensor(clo[:, 1], craw[:, 1], chi[:, 1].bitcast(F32), ALU.subtract).then_inc(s_wq_lo, 1)

            def kv_weights_lo(p):
                pool.wait_ge(s_w_hi, p + 1)
                nc.gpsimd.tensor_tensor(wlo[:], wraw[:], whi[:].bitcast(F32), ALU.subtract).then_inc(s_w_lo, 1)

            def ctx_lo(i, kc):
                pool.wait_ge(s_c_hi, KD * (4 * i + (kc + 1)))
                nc.gpsimd.tensor_tensor(clo[:, kc % 2], craw[:, kc % 2], chi[:, kc % 2].bitcast(F32),
                                        ALU.subtract).then_inc(s_c_lo, 1)

            def low_part(i, n):
                pool.wait_ge(v_mid, 16 * i + (n + 1))
                kc, t = n // 4, n % 4
                if t < 2:
                    ks = slice(512 * kc, 512 * kc + 512)
                    ins = nc.gpsimd.tensor_tensor(kparts[:, 2, t, ks], rest[:, n % 4], kparts[:, 1, t, ks], ALU.subtract)
                else:
                    v = 2 * kc + t - 2
                    v = vh[:, 2 * v:2 * v + 2]
                    ins = nc.gpsimd.tensor_tensor(v[:, :, :, 2 * HD:3 * HD],
                                                  rest[:, n % 4].rearrange("p (a h c) -> p a h c", a=2, c=HD),
                                                  v[:, :, :, HD:2 * HD], ALU.subtract)
                ins.then_inc(v_all, 1)

            def iteration(i, prefetch, weights=None):
                for n in range(16):
                    low_part(i, n)
                    if n in (3, 7):
                        ctx_lo(i, 2 + n // 4)
                if weights is not None:
                    kv_weights_lo(weights)
                if prefetch:
                    ctx_lo(i + 1, 0)
                    ctx_lo(i + 1, 1)

            kv_weights_lo(0)
            ctx_lo(0, 0)
            ctx_lo(0, 1)
            pool.wait_ge(s_cst, 16 * 8)
            pool.wait_ge(s_x, 16)
            pool.wait_ge(s_xn, 1)
            for b in range(B):
                nc.gpsimd.tensor_tensor(x_sb[:, b], x_sb[:, b], bo_bc, ALU.add).then_inc(s_xb, 1)
            with pool.Fori(0, 3) as i:
                iteration(i, True)
            iteration(3, True, weights=1)
            with pool.Fori(4, NI - 1) as i:
                iteration(i, True)
            iteration(NI - 1, False)

            def weight_lo(n):
                pool.wait_ge(s_Whi, n + 1)
                nc.gpsimd.tensor_tensor(Wlo[:, SLOT[n]], raw[:, n % 2], Whi[:, SLOT[n]].bitcast(F32),
                                        ALU.subtract).then_inc(s_Wlo, 1)

            def dequantise(blk, a, ks=range(KD)):
                f = 2 * blk + a
                for k in ks:
                    if not (isinstance(f, int) and f == 0):
                        wait_apart(pool, s_fw, KD * (f - 1) + (k + 1), passed_pool)
                    if k == 0:
                        wait_apart(pool, s_fq[a], 16 * (blk + 1), passed_pool)
                    nc.gpsimd.tensor_scalar(dq_w[:, k], raw[:, 1 - a, k].bitcast(I32), DEQ, -1.0,
                                            ALU.mult, ALU.add).then_inc(s_dq1, 1)
                for k in ks:
                    if k == 0:
                        pool.wait_ge(s_fs, 16 * (f + 1))
                    pool.wait_ge(s_dq1, KD * f + (k + 1))
                    nc.gpsimd.tensor_tensor(dq_w[:, k], dq_w[:, k], dq_scale[:, k], ALU.mult).then_inc(s_dq2, 1)

            def ffn_weight_lo(f, slot):
                for k in range(KD):
                    pool.wait_ge(s_fhi, KD * f + (k + 1))
                    nc.gpsimd.tensor_tensor(Wlo[:, slot, k], dq_w[:, k], Whi[:, slot, k].bitcast(F32),
                                            ALU.subtract).then_inc(s_fw, 1)

            for n in (WXO, WQ, WK):
                weight_lo(n)
            pool.wait_ge(o_ready, 6 * NI)
            nc.gpsimd.memset(vh2[:, :, :, 3 * HD:VW], 1.0).then_inc(s_ones2, 1)
            weight_lo(WV)
            weight_lo(WAO)
            for b in range(B):
                pool.wait_ge(s_v2, b + 1)
                nc.gpsimd.tensor_tensor(vh2[:, b, :, 2 * HD:3 * HD],
                                        vrest2[:, b % 2].rearrange("p (h c) -> p h c", c=HD),
                                        vh2[:, b, :, HD:2 * HD], ALU.subtract).then_inc(s_v3, 1)
            for u in range(NU):
                if u in (4, 8):
                    dequantise(0, 0, (0, 1) if u == 4 else (2, 3))
                pool.wait_ge(u_sum, 2 * (u + 1))
                nc.gpsimd.tensor_tensor(o_tok[:, u // 4, P * (u % 4):P * (u % 4) + P].rearrange("p (h c) -> p h c", c=HD),
                                        osum2[:, u % 2], rc2[:, u % 2].unsqueeze(2).broadcast_to([P, 4, HD]),
                                        ALU.mult).then_inc(u_o, 1)
            ffn_weight_lo(0, SLOT0)
            dequantise(0, 1)

            def ffn_block(blk, last):
                ffn_weight_lo(2 * blk + 1, SLOT1)
                for b in range(B):
                    wait_apart(pool, s_T, 12 + 8 * blk + (b + 1), passed_pool)
                    nc.gpsimd.tensor_tensor(h_tok[:, b], h_tok[:, b],
                                            f_bc[:, bass.ds(2 * blk + 1, 1)].rearrange("p one d -> p (one d)"),
                                            ALU.add).then_inc(s_hb, 1)
                if last:
                    for b in range(B):
                        pool.wait_ge(s_hb, 4 * blk + b + 1)
                        nc.gpsimd.tensor_tensor(h_tok[:, b], h_tok[:, b], x_sb[:, b], ALU.add).then_inc(s_hb, 1)
                else:
                    dequantise(blk + 1, 0)
                    ffn_weight_lo(2 * blk + 2, SLOT0)
                    dequantise(blk + 1, 1)

            pool.wait_ge(s_fb, 16)
            with pool.Fori(0, NBLK - 1) as blk:
                ffn_block(blk, False)
            ffn_block(NBLK - 1, True)

        def split_product(out_ap, pairs, last_sem=None):
            n = len(pairs)
            for k, (lh, ll, rh, rl) in enumerate(pairs):
                nc.tensor.matmul(out_ap, lh, rh, start=(k == 0), stop=False)
                nc.tensor.matmul(out_ap, lh, rl, start=False, stop=False)
                mm = nc.tensor.matmul(out_ap, ll, rh, start=False, stop=(k == n - 1))
            if last_sem is not None:
                mm.then_inc(last_sem, 1)

        def ksl(m):
            return slice(P * m, P * m + P)

        @block.tensor
        def _(pe):
            pe.wait_ge(s_id, 6)
            pe.wait_ge(s_xn, 1)
            for k in range(KD):
                for b in range(B):
                    mm = nc.tensor.transpose(ps[:, k, ksl(b)], xn0[:, b, ksl(k)], ident[:])
                mm.then_inc(s_t0, 1)
            pe.wait_ge(s_wq_lo, 1)
            pe.wait_ge(s_t0l, KD)
            for m in range(KD):
                split_product(ps[:, 4 + m], [(chi[:, 1, k, ksl(m)], clo[:, 1, k, ksl(m)], xnT_hi[:, k], xnT_lo[:, k])
                                             for k in range(KD)], s_q)

            def kv_part(i, n, k):
                kc, t = n // 4, n % 4
                c = kc % 2
                if t == 0 and k == 0:
                    if kc == 0:
                        pe.wait_ge(s_w_lo, (i >> 2) + 1)
                    pe.wait_ge(s_c_lo, 4 * i + (kc + 1))
                if n >= 4 and k == 0:
                    pe.wait_ge(kv_lo, 16 * i + (n - 3))
                if t < 2:
                    out_ap, first, last = ps[:, t], k == 0, k == KD - 1
                    triples = [(whi[:, 0, k, ksl(t)], wlo[:, 0, k, ksl(t)], chi[:, c, k], clo[:, c, k])]
                else:
                    a = k // 2
                    out_ap, first, last = ps[:, t, 256 * a:256 * a + 256], k % 2 == 0, k % 2 == 1
                    q = 2 * (t - 2) + a
                    triples = [(chi[:, c, kk, ksl(q)], clo[:, c, kk, ksl(q)], whi[:, 1, kk], wlo[:, 1, kk])
                               for kk in (2 * (k % 2), 2 * (k % 2) + 1)]
                for m, (lh, ll, rh, rl) in enumerate(triples):
                    nc.tensor.matmul(out_ap, lh, rh, start=(first and m == 0), stop=False)
                    nc.tensor.matmul(out_ap, lh, rl, start=False, stop=False)
                    mm = nc.tensor.matmul(out_ap, ll, rh, start=False, stop=(last and m == len(triples) - 1))
                if k == KD - 1:
                    mm.then_inc(kv_mm, 1)

            for n in range(4):
                for k in range(KD):
                    kv_part(0, n, k)

            def iteration(i, ahead):
                for n in range(4, 16):
                    for k in range(KD):
                        kv_part(i, n, k)
                pe.wait_ge(q_stack, 16 * NQ * (i + 1))

                def score(m):
                    h, c = m // NKC, m % NKC
                    if m < 4:
                        pe.wait_ge(kv_lo, 16 * i + (m + 13))
                    elif c % 2 == 0:
                        pe.wait_ge(masked, 16 * i + (2 * (h - 1) + c // 2 + 1))
                    if c == 0:
                        pe.wait_ge(k_stack[h % KSLOTS], 16 * 4 * (HI // KSLOTS) * i + 16 * 4 * (h // KSLOTS + 1))
                    for turn in range(2):
                        mm = nc.tensor.matmul(ps[:, c], qst[:, turn, h // 4, h % 4],
                                              kst[:, h % KSLOTS, 512 * c:512 * c + 512], start=(turn == 0), stop=(turn == 1))
                    if c % 2:
                        mm.then_inc(scores, 1)

                def transposes(n):
                    h, t = n // NKC, n % NKC
                    if t % 2 == 0:
                        pe.wait_ge(exps, 16 * i + (2 * h + t // 2 + 1))
                    if n >= TB:
                        pe.wait_ge(pt_lo, 32 * i + (n - TB + 1))
                    for y in range(4):
                        mm = nc.tensor.transpose(ps[:, 4 + n % TB, ksl(y)], sm[:, h % 2, ksl(4 * t + y)], ident[:])
                    mm.then_inc(tps, 1)

                def weighted(n):
                    h, t = n // NKC, n % NKC
                    pe.wait_ge(pt_lo, 32 * i + (n + 1))
                    if n == 0:
                        pe.wait_ge(v_all, 16 * (i + 1))
                    acc = ps[:, 6 + h // 4, VW * (h % 4):VW * (h % 4) + VW]
                    for y in range(4):
                        v = vh[:, 4 * t + y, h, :]
                        nc.tensor.matmul(acc, pthi[:, n % PTR, y], v, start=(t == 0 and y == 0), stop=False)
                        mm = nc.tensor.matmul(acc, ptlo[:, n % PTR, y], v, start=False, stop=(t == 3 and y == 3))
                    mm.then_inc(pv, 1)

                for n in range(-LEAD, NG + LAG):
                    if 0 <= n + LEAD < NG:
                        score(n + LEAD)
                    if 0 <= n < NG:
                        transposes(n)
                    if 0 <= n - LAG < NG:
                        weighted(n - LAG)
                    if ahead and NG - LEAD + 2 <= n:
                        part = 2 * (n - (NG - LEAD + 2))
                        if part % 8 == 0:
                            pe.wait_ge(masked, 16 * i + (15 + part // 8))
                        kv_part(i + 1, part // KD, part % KD)
                        kv_part(i + 1, (part + 1) // KD, (part + 1) % KD)
                assert NG + LAG - (NG - LEAD + 2) == 8

            with pe.Fori(0, NI - 1) as i:
                iteration(i, True)
            iteration(NI - 1, False)
            def transpose_tile(src, b, base):
                wait(pe, s_al, base + (b - 1))
                for k in range(KD):
                    mm = nc.tensor.transpose(ps[:, b % 2, ksl(k)], src[:, b, ksl(k)], ident[:])
                mm.then_inc(s_T, 1)

            def lora_product(f, k, slot):
                if k == 0:
                    pe.wait_ge(s_ls, 2 * (f + 1))
                wait(pe, s_fadd, 4 * f + (k - 1))
                nc.tensor.matmul(ps[:, 2 + k % 2], lora_st[:, slot, 0, ksl(k)], lora_st[:, slot, 1],
                                 start=True, stop=True).then_inc(s_lora, 1)

            def linear_tile(b, slot, base, weight=None):
                pe.wait_ge(s_al, base + (b + 1))
                for k in range(KD):
                    if weight is not None and b == 0:
                        pe.wait_ge(s_fw, KD * weight + (k + 1))
                    lh, ll = aThi[:, k, ksl(b)], aTlo[:, k, ksl(b)]
                    nc.tensor.matmul(ps[:, 4 + b], lh, Whi[:, slot, k], start=(k == 0), stop=False)
                    nc.tensor.matmul(ps[:, 4 + b], lh, Wlo[:, slot, k], start=False, stop=False)
                    mm = nc.tensor.matmul(ps[:, 4 + b], ll, Whi[:, slot, k], start=False, stop=(k == KD - 1))
                mm.then_inc(s_lin, 1)

            def token_linear(transposed, slot, base, weight=None, build=None, build_slot=0, begun=False, ahead=None,
                             late=False):
                if not begun:
                    transposed(0)
                    transposed(1)
                for b in range(B):
                    if build is not None and b == 0:
                        lora_product(build, 0, build_slot)
                        lora_product(build, 1, build_slot)
                    if b == B - 1 and ahead is not None:
                        ahead(0)
                        ahead(1)
                    if b < 2 and not late:
                        transposed(b + 2)
                    linear_tile(b, slot, base, weight)
                    if b < 2 and late:
                        transposed(b + 2)
                    if b < 2 and build is not None:
                        lora_product(build, b + 2, build_slot)

            def feature_linear(slot, free_sem):
                for m in range(KD):
                    if free_sem is not None:
                        pe.wait_ge(free_sem, m + 1)
                    split_product(ps[:, 4 + m], [(Whi[:, slot, k, ksl(m)], Wlo[:, slot, k, ksl(m)], aThi[:, k], aTlo[:, k])
                                                 for k in range(KD)], s_lin)

            def attention_out_tile(b):
                pe.wait_ge(o_ready, 6 * (HI // 2 + b + 1))
                if b == 0:
                    pe.wait_ge(masked, 16 * NI)
                transpose_tile(o_tok, b, 0)

            pe.wait_ge(s_Wlo, 1)
            token_linear(attention_out_tile, SLOT[WXO], 0)

            for b in range(B):
                pe.wait_ge(s_tok, b + 1)
                transpose_tile(tok, b, 4)
            pe.wait_ge(s_Wlo, 2)
            pe.wait_ge(s_al, 8)
            feature_linear(SLOT[WQ], None)
            pe.wait_ge(s_Wlo, 3)
            feature_linear(SLOT[WK], s_q2)
            pe.wait_ge(s_Wlo, 4)
            for b in range(B):
                pe.wait_ge(s_k2, b + 1)
                split_product(ps[:, 4 + b], [(aThi[:, k, ksl(b)], aTlo[:, k, ksl(b)], Whi[:, SLOT[WV], k], Wlo[:, SLOT[WV], k])
                                             for k in range(KD)], s_lin)
            for n in range(NU + 3):
                if n < NU:
                    b, g = n // 4, n % 4
                    wait(pe, u_m, n - 1)
                    for j in range(4):
                        mm = nc.tensor.matmul(ps[:, 2 + n % 2, ksl(j)], qz2[:, g, j, ksl(b)], kT2[:, g, ksl(b)],
                                              start=True, stop=True)
                    mm.then_inc(u_s, 1)
                if 0 <= n - 2 < NU:
                    u = n - 2
                    pe.wait_ge(u_e, u + 1)
                    wait(pe, u_l, u - 1)
                    for j in range(4):
                        mm = nc.tensor.transpose(ps[:, u % 2, ksl(j)], sm2[:, u % 2, j], ident[:])
                    mm.then_inc(u_t, 1)
                if 0 <= n - 3 < NU:
                    u = n - 3
                    b, g = u // 4, u % 4
                    if u == 0:
                        pe.wait_ge(s_v3, B)
                        pe.wait_ge(s_ones2, 1)
                    pe.wait_ge(u_l, u + 1)
                    wait(pe, u_sum, 2 * (u - 1))
                    for j in range(4):
                        acc = ps[:, 6 + u % 2, VW * j:VW * j + VW]
                        nc.tensor.matmul(acc, pthi2[:, u % 2, j], vh2[:, b, 4 * g + j], start=True, stop=False)
                        mm = nc.tensor.matmul(acc, ptlo2[:, u % 2, j], vh2[:, b, 4 * g + j], start=False, stop=True)
                    mm.then_inc(u_pv, 1)
            def self_out_tile(b):
                pe.wait_ge(s_tok, 4 + b + 1)
                transpose_tile(tok, b, 8)

            def h_tile(blk, b):
                pe.wait_ge(s_h, 4 * blk + (b + 1))
                transpose_tile(h_tok, b, 12 + 8 * blk)

            pe.wait_ge(s_Wlo, 5)
            token_linear(self_out_tile, SLOT[WAO], 8, build=0)
            h_tile(0, 0)
            h_tile(0, 1)

            def ffn_block(blk, last):
                def normed_tile(b):
                    pe.wait_ge(s_tok, 8 + 4 * blk + (b + 1))
                    transpose_tile(tok, b, 16 + 8 * blk)

                token_linear(lambda b: h_tile(blk, b), SLOT0, 12 + 8 * blk, weight=2 * blk, build=2 * blk + 1, build_slot=1,
                             begun=True)
                token_linear(normed_tile, SLOT1, 16 + 8 * blk, weight=2 * blk + 1,
                             build=None if last else 2 * blk + 2,
                             ahead=None if last else (lambda b: h_tile(blk + 1, b)), late=True)

            with pe.Fori(0, NBLK - 1) as blk:
                ffn_block(blk, False)
            ffn_block(NBLK - 1, True)

        @block.scalar
        def _(act):
            def ident_bias(out_ap, in_ap, bias_ap):
                return nc.scalar.activation(out_ap, in_ap, ACT.Identity, bias=bias_ap)

            act.wait_ge(s_wq, 16)
            nc.scalar.copy(chi[:, 1], craw[:, 1]).then_inc(s_wq_hi, 1)
            for k in range(KD):
                act.wait_ge(s_t0, k + 1)
                nc.scalar.copy(xnT_hi[:, k], ps[:, k]).then_inc(s_t0h, 1)
            act.wait_ge(s_cst, 16 * 8)
            for m in range(KD + 1):
                if m < KD:
                    act.wait_ge(s_q, m + 1)
                    ident_bias(qparts[:, 0, m // 2, :, m % 2], ps[:, 4 + m].rearrange("p (b t) -> p b t", b=B),
                               b_q[:, m:m + 1]).then_inc(s_qh, 1)
                if m >= 1:
                    act.wait_ge(s_ql, m)
                    nc.scalar.copy(qparts[:, 1, (m - 1) // 2, :, (m - 1) % 2],
                                   rest[:, m - 1].rearrange("p (b t) -> p b t", b=B)).then_inc(s_qm, 1)

            def ctx_hi_piece(i, kc, k):
                if k == 0:
                    act.wait_ge(s_c[kc], 32 * i + 16)
                nc.scalar.copy(chi[:, kc, k], craw[:, kc, k]).then_inc(s_c_hi, 1)

            def mid_part(i, n):
                act.wait_ge(kv_lo, 16 * i + (n + 1))
                kc, t = n // 4, n % 4
                if t < 2:
                    ins = nc.scalar.copy(kparts[:, 1, t, 512 * kc:512 * kc + 512], rest[:, n % 4])
                else:
                    v = 2 * kc + t - 2
                    ins = nc.scalar.copy(vh[:, 2 * v:2 * v + 2, :, HD:2 * HD],
                                         rest[:, n % 4].rearrange("p (a h c) -> p a h c", a=2, c=HD))
                ins.then_inc(v_mid, 1)

            def large_parts(i, n):
                kc, t = n // 4, n % 4
                act.wait_ge(kv_mm, 16 * i + (n + 1))
                if t < 2:
                    ident_bias(kparts[:, 0, t, 512 * kc:512 * kc + 512], ps[:, t],
                               b_kn[:, t:t + 1]).then_inc(kv_hi, 1)
                else:
                    v = 2 * kc + t - 2
                    nc.scalar.copy(vh[:, 2 * v:2 * v + 2, :, 0:HD],
                                   ps[:, t].rearrange("p (a h c) -> p a h c", a=2, c=HD)).then_inc(kv_hi, 1)
                mid_part(i, n)

            def first_tiles(i):
                act.wait_ge(bk_now, i + 1)
                large_parts(i, 0)
                large_parts(i, 1)

            first_tiles(0)

            def iteration(i, prefetch):
                for n in range(2, 16):
                    large_parts(i, n)

                def exp_half(h, half):
                    act.wait_ge(nbias, 8 * i + (h + 1))
                    s = sm[:, h % 2, 1024 * half:1024 * half + 1024]
                    nc.scalar.activation(s, s, ACT.Exp, bias=nb[:, h % 2, 0:1], scale=SCALE).then_inc(exps, 1)

                def weights_hi(n):
                    act.wait_ge(tps, 32 * i + (n + 1))
                    if n >= PTR:
                        act.wait_ge(pv, 32 * i + (n - PTR + 1))
                    nc.scalar.copy(pthi[:, n % PTR], ps[:, 4 + n % TB].rearrange("p (y q) -> p y q", y=4)).then_inc(pt_hi, 1)

                for n in range(-2, NG):
                    h, t = (n + 2) // NKC, (n + 2) % NKC
                    if h < HI and t % 2 == 0:
                        exp_half(h, t // 2)
                    if n >= 0:
                        weights_hi(n)
                    if 6 <= n < 6 + 2 * 2 * KD and n % 2 and prefetch:
                        ctx_hi_piece(i + 1, (n - 6) // (2 * KD), (n - 6) // 2 % KD)
                if prefetch:
                    first_tiles(i + 1)

            with act.Fori(0, NI - 1) as i:
                iteration(i, True)
            iteration(NI - 1, False)
            def head_view(ap):
                return ap.rearrange("p (h c) -> p h c", c=HD)

            def tile_view(ap, b):
                return ap[:, :, P * b:P * b + P]

            def bank_view(b):
                return ps[:, b % 2].rearrange("p (k t) -> p k t", k=KD)

            def high_tile(b, base):
                act.wait_ge(s_T, base + (b + 1))
                nc.scalar.copy(tile_view(aThi, b), bank_view(b)).then_inc(s_ah, 1)

            for b in range(B):
                act.wait_ge(s_T, b + 1)
                for k in range(KD):
                    ins = ident_bias(aThi[:, k, P * b:P * b + P], bank_view(b)[:, k], b_v[:, k:k + 1])
                ins.then_inc(s_ah, 1)
            for b in range(B):
                high_tile(b, 4)
            for m in range(KD):
                act.wait_ge(s_lin, 4 + m + 1)
                for j in range(4):
                    ins = nc.scalar.activation(qz2[:, m, j], ps[:, 4 + m], ACT.Copy, scale=rowmask[:, j:j + 1])
                ins.then_inc(s_q2, 1)
            def lora_high(f):
                act.wait_ge(s_fl, 16 * 8 * (f + 1))
                wait(act, s_ls, 2 * f)
                nc.scalar.copy(lora_hi[:], lora_raw[:]).then_inc(s_lh, 1)

            lora_high(0)
            for b in range(B + 1):
                if b < B:
                    act.wait_ge(s_lin, 12 + b + 1)
                    nc.scalar.copy(vh2[:, b, :, 0:HD], head_view(ps[:, 4 + b])).then_inc(s_v1, 1)
                if b >= 1:
                    act.wait_ge(s_vr, b)
                    nc.scalar.copy(vh2[:, b - 1, :, HD:2 * HD], head_view(vrest2[:, (b - 1) % 2])).then_inc(s_v2, 1)
            for n in range(NU + 2):
                if n >= 2:
                    u = n - 2
                    act.wait_ge(u_t, u + 1)
                    wait(act, u_pv, u - 1)
                    nc.scalar.copy(pthi2[:, u % 2], ps[:, u % 2].rearrange("p (j q) -> p j q", j=4)).then_inc(u_h, 1)
                if n < NU:
                    act.wait_ge(u_nb, n + 1)
                    for j in range(4):
                        ins = nc.scalar.activation(sm2[:, n % 2, j], sm2[:, n % 2, j], ACT.Exp, bias=nb[:, n % 2, j:j + 1])
                    ins.then_inc(u_e, 1)
            def ffn_weight_hi(f, slot, ks):
                for k in ks:
                    act.wait_ge(s_fadd, KD * f + (k + 1))
                    nc.scalar.copy(Whi[:, slot, k], dq_w[:, k]).then_inc(s_fhi, 1)

            lora_high(1)
            for b in range(B):
                act.wait_ge(s_T, 8 + b + 1)
                for k in range(KD):
                    ins = nc.scalar.activation(g32[:, k, P * b:P * b + P], bank_view(b)[:, k], ACT.Identity,
                                               scale=g_a[:, k:k + 1], bias=be_a[:, k:k + 1])
                ins.then_inc(s_g, 1)
            ffn_weight_hi(0, SLOT0, range(KD))

            g_ff = g_f[:].rearrange("p f k -> p (f k)")
            be_ff = be_f[:].rearrange("p f k -> p (f k)")

            def ffn_block(blk, last):
                if not last:
                    lora_high(2 * blk + 2)
                nc.scalar.activation(gelu_tab[:], gelu_tab[:], ACT.Gelu)
                high_tile(2, 12 + 8 * blk)
                ffn_weight_hi(2 * blk + 1, SLOT1, (0, 1))
                high_tile(3, 12 + 8 * blk)
                ffn_weight_hi(2 * blk + 1, SLOT1, (2, 3))
                if not last:
                    lora_high(2 * blk + 3)
                for b in range(B):
                    wait_apart(act, s_T, 16 + 8 * blk + (b + 1), passed_act)
                    for k in range(KD):
                        ins = nc.scalar.activation(g32[:, k, P * b:P * b + P], bank_view(b)[:, k], ACT.Gelu,
                                                   scale=g_ff[:, bass.ds(4 * blk + k, 1)],
                                                   bias=be_ff[:, bass.ds(4 * blk + k, 1)])
                    ins.then_inc(s_g, 1)
                if not last:
                    ffn_weight_hi(2 * blk + 2, SLOT0, range(KD))
                    high_tile(0, 20 + 8 * blk)
                    high_tile(1, 20 + 8 * blk)

            high_tile(0, 12)
            high_tile(1, 12)
            with act.Fori(0, NBLK - 1) as blk:
                ffn_block(blk, False)
            ffn_block(NBLK - 1, True)

        @block.vector
        def _(dve):
            chain = [0]

            def mark(ins):
                chain[0] += 1
                ins.then_inc(s_vec, 1)
                return chain[0]

            def link(ins):
                dve.wait_ge(s_vec, mark(ins))

            def kv_weights_hi(p):
                dve.wait_ge(s_w, 32 * (p + 1))
                wait(dve, kv_mm, 16 * 4 * p)
                nc.vector.tensor_copy(whi[:], wraw[:]).then_inc(s_w_hi, 1)

            def ctx_hi(i, kc, pieces=range(KD)):
                if 0 in pieces:
                    dve.wait_ge(s_c[kc % 2], 32 * i + 16 * (kc // 2 + 1))
                    wait(dve, kv_mm, 16 * i + 4 * (kc - 1))
                s = slice(pieces[0], pieces[-1] + 1)
                nc.vector.tensor_copy(chi[:, kc % 2, s], craw[:, kc % 2, s]).then_inc(s_c_hi, len(pieces))

            def rstd(mark, need, tiles):
                cols = [slice(b, b + 1) for b in tiles]
                for c, b in zip(cols, tiles):
                    mark(nc.vector.tensor_scalar(ve[:, c], mv[:, b, 1:2], LN_EPS, None, ALU.add))
                last = [mark(nc.vector.tensor_scalar(nh[:, c], mv[:, b, 1:2], LN_EPS, -0.5, ALU.add, ALU.mult))
                        for c, b in zip(cols, tiles)]

                def step(make):
                    for n, c in enumerate(cols):
                        need(last[n])
                        last[n] = mark(make(c))

                step(lambda c: nc.vector.tensor_scalar(rs[:, c].bitcast(I32), ve[:, c].bitcast(I32), -0.5,
                                                       float(0x5F3759DF), ALU.mult, ALU.add))
                for _ in range(3):
                    step(lambda c: nc.vector.scalar_tensor_tensor(out=rt[:, c], in0=rs[:, c], scalar=nh[:, c],
                                                                  in1=rs[:, c], op0=ALU.mult, op1=ALU.mult))
                    step(lambda c: nc.vector.scalar_tensor_tensor(out=rs[:, c], in0=rt[:, c], scalar=1.5,
                                                                  in1=rs[:, c], op0=ALU.add, op1=ALU.mult))
                need(last[-1])

            def weight_hi(n):
                dve.wait_ge(s_raw[n % 2], 16 * (n // 2 + 1))
                if n <= WK:
                    dve.wait_ge(kv_mm, 16 * NI)
                else:
                    dve.wait_ge(s_lin, 4 if n == WV else 8)
                nc.vector.tensor_copy(Whi[:, SLOT[n]], raw[:, n % 2]).then_inc(s_Whi, 1)

            dve.wait_ge(s_x, 16)
            for b in range(B):
                link(nc.vector.bn_stats(stats[:, b], x_sb[:, b]))
                link(nc.vector.bn_aggr(mv[:, b], stats[:, b]))
            rstd(mark, lambda value: dve.wait_ge(s_vec, value), range(B))
            for b in range(B):
                ins = nc.vector.tensor_scalar(xn0[:, b], x_sb[:, b], mv[:, b, 0:1], rs[:, b:b + 1],
                                              ALU.subtract, ALU.mult)
            ins.then_inc(s_xn, 1)
            kv_weights_hi(0)
            ctx_hi(0, 0)
            for k in range(KD):
                dve.wait_ge(s_t0h, k + 1)
                nc.vector.tensor_tensor(xnT_lo[:, k], ps[:, k], xnT_hi[:, k].bitcast(F32), ALU.subtract).then_inc(s_t0l, 1)
            dve.wait_ge(s_m, 16)
            link(nc.vector.tensor_scalar(mbias[:], mraw, 0.0, NEG, ALU.is_equal, ALU.mult))
            link(nc.vector.tensor_reduce(nanfix[:, 0:1], mbias[:], AX.X, ALU.max))
            link(nc.vector.tensor_scalar(nanfix[:, 1:2], nanfix[:, 0:1], 0.1 * NEG, None, ALU.is_gt))
            link(nc.vector.reciprocal(nanfix[:, 2:3], nanfix[:, 1:2]))
            link(nc.vector.tensor_tensor(nanfix[:, 3:4], nanfix[:, 1:2], nanfix[:, 2:3], ALU.mult))
            for m in range(KD):
                dve.wait_ge(s_qh, m + 1)
                nc.vector.scalar_tensor_tensor(out=rest[:, m].rearrange("p (b t) -> p b t", b=B),
                                               in0=ps[:, 4 + m].rearrange("p (b t) -> p b t", b=B),
                                               scalar=b_q[:, m:m + 1], in1=qparts[:, 0, m // 2, :, m % 2],
                                               op0=ALU.add, op1=ALU.subtract).then_inc(s_ql, 1)
            for m in range(KD):
                dve.wait_ge(s_qm, m + 1)
                nc.vector.tensor_tensor(qparts[:, 2, m // 2, :, m % 2], rest[:, m].rearrange("p (b t) -> p b t", b=B),
                                        qparts[:, 1, m // 2, :, m % 2], ALU.subtract).then_inc(s_ql3, 1)
            dve.wait_ge(s_q, KD)
            ctx_hi(0, 1)
            pool_init = 5
            dve.wait_ge(s_id, pool_init)

            def kv_rest(i, n):
                kc, t = n // 4, n % 4
                dve.wait_ge(kv_hi, 16 * i + (n + 1))
                if n >= 4:
                    dve.wait_ge(v_all, 16 * i + (n - 3))
                if t < 2:
                    ks = slice(512 * kc, 512 * kc + 512)
                    nc.vector.scalar_tensor_tensor(out=rest[:, n % 4], in0=ps[:, t], scalar=b_kn[:, t:t + 1],
                                                   in1=kparts[:, 0, t, ks], op0=ALU.add,
                                                   op1=ALU.subtract).then_inc(kv_lo, 1)
                else:
                    v = 2 * kc + t - 2
                    nc.vector.tensor_tensor(rest[:, n % 4].rearrange("p (a h c) -> p a h c", a=2, c=HD),
                                            ps[:, t].rearrange("p (a h c) -> p a h c", a=2, c=HD),
                                            vh[:, 2 * v:2 * v + 2, :, 0:HD], ALU.subtract).then_inc(kv_lo, 1)

            def first_tiles(i):
                nc.vector.tensor_copy(b_kn[:], b_kf[:, bass.ds(i & 4, 2)]).then_inc(bk_now, 1)
                dve.wait_ge(bk_now, i + 1)
                kv_rest(i, 0)
                kv_rest(i, 1)

            first_tiles(0)

            def iteration(i, prefetch, weights=None):
                for n in range(2, 16):
                    kv_rest(i, n)
                    if n in (3, 7):
                        ctx_hi(i, 2 + n // 4)

                def mask_half(h, half):
                    if h >= 2:
                        dve.wait_ge(tps, 32 * i + (4 * (h - 2) + 2 * half + 2))
                    if half:
                        dve.wait_ge(masked, 16 * i + (2 * h + 1))
                    wait_apart(dve, scores, 16 * i + (2 * h + half + 1), passed_dve)
                    s = slice(1024 * half, 1024 * half + 1024)
                    nc.vector.tensor_tensor_reduce(
                        sm[:, h % 2, s], ps[:, 2 * half:2 * half + 2].rearrange("p c t -> p (c t)"), mbias[:, s],
                        1.0, mx[:, h % 2, 0:1] if half else 3.0 * NEG, ALU.add, ALU.max,
                        mx[:, h % 2, half:half + 1]).then_inc(masked, 1)
                    if half:
                        dve.wait_ge(masked, 16 * i + (2 * h + 2))
                        nc.vector.tensor_scalar(nb[:, h % 2, 0:1], mx[:, h % 2, 1:2], -SCALE, PSHIFT,
                                                ALU.mult, ALU.add).then_inc(nbias, 1)

                def weights_lo(n):
                    dve.wait_ge(pt_hi, 32 * i + (n + 1))
                    nc.vector.tensor_tensor(ptlo[:, n % PTR], ps[:, 4 + n % TB].rearrange("p (y q) -> p y q", y=4),
                                            pthi[:, n % PTR], ALU.subtract).then_inc(pt_lo, 1)

                def normalise(g):
                    dve.wait_ge(pv, 32 * i + 16 * (g + 1))
                    acc = ps[:, 6 + g, 0:4 * VW].rearrange("p (h w) -> p h w", h=4)
                    nc.vector.reciprocal(rc[:], acc[:, :, 3 * HD]).then_inc(o_ready, 1)
                    nc.vector.tensor_reduce(osum[:], acc[:, :, 0:3 * HD].rearrange("p h (s c) -> p h c s", s=3),
                                            AX.X, ALU.add).then_inc(o_ready, 1)
                    dve.wait_ge(o_ready, 6 * i + (3 * g + 2))
                    dst = o_tok[:].rearrange("p b d -> p (b d)")[:, bass.ds((i & 3) * D + (i & 4) * 64 + P * g, P)]
                    nc.vector.scalar_tensor_tensor(out=dst, in0=osum[:].rearrange("p h c -> p (h c)"),
                                                   scalar=nanfix[:, 3:4],
                                                   in1=rc[:].unsqueeze(2).broadcast_to([P, 4, HD]),
                                                   op0=ALU.mult, op1=ALU.mult).then_inc(o_ready, 1)

                for n in range(1 - LEAD, NG):
                    m = n + LEAD
                    if m % 2 == 1 and m < NG:
                        mask_half(m // NKC, (m % NKC) // 2)
                    if n == NG // 2 + LAG:
                        normalise(0)
                    if n == 4 and weights is not None:
                        kv_weights_hi(weights)
                    if n in (8, 16, 24) and not prefetch:
                        weight_hi(n // 8 - 1)
                    if n >= 0:
                        weights_lo(n)
                if prefetch:
                    first_tiles(i + 1)
                normalise(1)

            with dve.Fori(0, 3) as i:
                iteration(i, True)
            iteration(3, True, weights=1)
            with dve.Fori(4, NI - 1) as i:
                iteration(i, True)
            iteration(NI - 1, False)
            def tile_view(ap, b):
                return ap[:, :, P * b:P * b + P]

            def low_tile(b, base, bias=None):
                dve.wait_ge(s_ah, base + (b + 1))
                bank = ps[:, b % 2].rearrange("p (k t) -> p k t", k=KD)
                if bias is None:
                    ins = nc.vector.tensor_tensor(tile_view(aTlo, b), bank, tile_view(aThi, b).bitcast(F32), ALU.subtract)
                else:
                    for k in range(KD):
                        t = slice(P * b, P * b + P)
                        ins = nc.vector.scalar_tensor_tensor(out=aTlo[:, k, t], in0=bank[:, k], scalar=bias[:, k:k + 1],
                                                             in1=aThi[:, k, t].bitcast(F32), op0=ALU.add, op1=ALU.subtract)
                ins.then_inc(s_al, 1)

            def both_parts(steps, b, base):
                dve.wait_ge(s_g, base + (b + 1))
                steps.need(steps.mark(nc.vector.tensor_copy(tile_view(aThi, b), tile_view(g32, b))))
                nc.vector.tensor_tensor(tile_view(aTlo, b), tile_view(g32, b), tile_view(aThi, b).bitcast(F32),
                                        ALU.subtract).then_inc(s_al, 1)

            def lora_add(f, k):
                dve.wait_ge(s_lora, KD * f + (k + 1))
                dve.wait_ge(s_dq2, KD * f + (k + 1))
                nc.vector.tensor_tensor(dq_w[:, k], dq_w[:, k], ps[:, 2 + k % 2], ALU.add).then_inc(s_fadd, 1)

            def lora_stack(f, slot):
                dve.wait_ge(s_lh, f + 1)
                for t in range(2):
                    nc.vector.scalar_tensor_tensor(out=lora_st[:, slot, t], in0=lora_hi[:, t].bitcast(F32),
                                                   scalar=is_low[:, t:t + 1], in1=lora_raw[:, t],
                                                   op0=ALU.mult, op1=ALU.add).then_inc(s_ls, 1)

            class Norm:

                def __init__(self, steps, src, dst, done):
                    self.steps, self.src, self.dst, self.done, self.seen = steps, src, dst, done, {}

                def stats(self, b, made=None):
                    if made is not None:
                        self.steps.need(made)
                    self.seen[b] = self.steps.mark(nc.vector.bn_stats(stats[:, b], self.src[:, b]))

                def finish(self, tiles):
                    s = self.steps
                    for b in tiles:
                        wait_apart(dve, s.sem, self.seen[b], passed_dve)
                        last = s.mark(nc.vector.bn_aggr(mv[:, b], stats[:, b]))
                    s.need(last)
                    rstd(s.mark, s.need, tiles)
                    for b in tiles:
                        nc.vector.tensor_scalar(self.dst[:, b], self.src[:, b], mv[:, b, 0:1], rs[:, b:b + 1],
                                                ALU.subtract, ALU.mult).then_inc(self.done, 1)

            def token_stage(steps, parts, produce, norm=None, build=None, stack=None, begun=False, ahead=None):
                if not begun:
                    parts(0)
                    parts(1)
                made = {}

                def tile(b):
                    made[b] = steps.mark(produce(b)) if norm is not None else produce(b)

                if stack is not None:
                    lora_stack(*stack)
                if build is not None:
                    lora_add(build, 0)
                    lora_add(build, 1)
                for b in range(2):
                    parts(b + 2)
                    tile(b)
                    if build is not None:
                        lora_add(build, b + 2)
                    if norm is not None:
                        norm.stats(b, made[b])
                if norm is not None:
                    norm.finish((0, 1))
                tile(2)
                if norm is not None:
                    norm.stats(2, made[2])
                    tile(3)
                if ahead is not None:
                    ahead(0)
                if norm is not None:
                    norm.stats(3, made[3])
                if ahead is not None:
                    ahead(1)
                if norm is not None:
                    norm.finish((2, 3))
                else:
                    tile(3)

            def residual_tile(base, need_bias=False):
                def produce(b):
                    if need_bias:
                        dve.wait_ge(s_xb, b + 1)
                    dve.wait_ge(s_lin, base + b + 1)
                    return nc.vector.tensor_tensor(x_sb[:, b], ps[:, 4 + b], x_sb[:, b], ALU.add)
                return produce

            steps = Steps(dve, s_pre, 0)
            norm = Norm(steps, x_sb, tok, s_tok)
            token_stage(steps, lambda b: low_tile(b, 0, b_v), residual_tile(0, True), norm,
                        ahead=lambda b: low_tile(b, 4))
            low_tile(2, 4)
            low_tile(3, 4)
            weight_hi(WV)
            for m in range(KD):
                dve.wait_ge(s_lin, 8 + m + 1)
                nc.vector.tensor_scalar(kT2[:, m], ps[:, 4 + m], SCALE, None, ALU.mult).then_inc(s_k2, 1)
                if m == 0:
                    weight_hi(WAO)
            dve.wait_ge(s_tab, 6)
            lora_stack(0, 0)
            for b in range(B):
                dve.wait_ge(s_v1, b + 1)
                if b >= 2:
                    dve.wait_ge(s_v3, b - 1)
                nc.vector.tensor_tensor(vrest2[:, b % 2].rearrange("p (h c) -> p h c", c=HD),
                                        ps[:, 4 + b].rearrange("p (h c) -> p h c", c=HD),
                                        vh2[:, b, :, 0:HD], ALU.subtract).then_inc(s_vr, 1)
            for n in range(NU + 4):
                if n < NU:
                    dve.wait_ge(u_s, n + 1)
                    wait(dve, u_t, n - 1)
                    wait(dve, u_nb, n - 1)
                    for j in range(4):
                        ins = nc.vector.tensor_tensor_reduce(sm2[:, n % 2, j], ps[:, 2 + n % 2, P * j:P * j + P],
                                                             causal[:], 1.0, 3.0 * NEG, ALU.add, ALU.max,
                                                             mx2[:, n % 2, j:j + 1])
                    ins.then_inc(u_m, 1)
                    dve.wait_ge(u_m, n + 1)
                    nc.vector.tensor_scalar(nb[:, n % 2], mx2[:, n % 2], -1.0, PSHIFT, ALU.mult, ALU.add).then_inc(u_nb, 1)
                if 0 <= n - 2 < NU:
                    u = n - 2
                    dve.wait_ge(u_h, u + 1)
                    nc.vector.tensor_tensor(ptlo2[:, u % 2], ps[:, u % 2].rearrange("p (j q) -> p j q", j=4),
                                            pthi2[:, u % 2], ALU.subtract).then_inc(u_l, 1)
                if 0 <= n - 4 < NU:
                    u = n - 4
                    dve.wait_ge(u_pv, u + 1)
                    wait(dve, u_o, u - 1)
                    acc = ps[:, 6 + u % 2, 0:4 * VW].rearrange("p (h w) -> p h w", h=4)
                    nc.vector.reciprocal(rc2[:, u % 2], acc[:, :, 3 * HD]).then_inc(u_sum, 1)
                    nc.vector.tensor_reduce(osum2[:, u % 2], acc[:, :, 0:3 * HD].rearrange("p h (s c) -> p h c s", s=3),
                                            AX.X, ALU.add).then_inc(u_sum, 1)
            norm = Norm(steps, o_tok, tok, s_tok)
            dve.wait_ge(u_o, NU)
            for pair in ((0, 1), (2, 3)):
                for b in pair:
                    norm.stats(b)
                norm.finish(pair)
            norm = Norm(steps, x_sb, h_tok, s_h)
            token_stage(steps, lambda b: both_parts(steps, b, 0), residual_tile(16), norm, build=0, stack=(1, 1),
                        ahead=lambda b: low_tile(b, 8))

            def ffn_block(blk, last):
                steps = Steps(dve, s_ffn, FFN_STEPS * blk)

                def first(b):
                    dve.wait_ge(s_lin, 20 + 8 * blk + (b + 1))
                    return nc.vector.tensor_tensor(tok[:, b], ps[:, 4 + b],
                                                   f_bc[:, bass.ds(2 * blk, 1)].rearrange("p one d -> p (one d)"), ALU.add)

                def second(b):
                    dve.wait_ge(s_hb, 4 * blk + (b + 1) + (B if last else 0))
                    dve.wait_ge(s_lin, 24 + 8 * blk + (b + 1))
                    ins = nc.vector.tensor_tensor(h_tok[:, b], ps[:, 4 + b], h_tok[:, b], ALU.add)
                    return ins.then_inc(s_fin if last else s_h, 1)

                norm = Norm(steps, tok, tok, s_tok)
                token_stage(steps, lambda b: low_tile(b, 8 + 4 * blk), first, norm, build=2 * blk + 1,
                            stack=None if last else (2 * blk + 2, 0), begun=True,
                            ahead=lambda b: both_parts(steps, b, 4 + 4 * blk))
                token_stage(steps, lambda b: both_parts(steps, b, 4 + 4 * blk), second, None,
                            build=None if last else 2 * blk + 2, stack=None if last else (2 * blk + 3, 1), begun=True,
                            ahead=None if last else (lambda b: low_tile(b, 12 + 4 * blk)))
                if not last:
                    assert steps.n == FFN_STEPS, steps.n

            dve.wait_ge(s_fb, 16)
            with dve.Fori(0, NBLK - 1) as blk:
                ffn_block(blk, False)
            ffn_block(NBLK - 1, True)


def kernel(**inputs):
    import concourse.bacc as bacc
    from concourse.bass_utils import run_bass_kernel_spmd

    nc = bacc.Bacc("TRN2", target_bir_lowering=False, num_devices=1)
    g = {k: np.asarray(v) for k, v in inputs.items()}

    def cols(v):
        return v.reshape(KD, P).T

    av = g["L0_attn_Wv"].reshape(HD, H, D).transpose(1, 0, 2).reshape(D, D)
    fq = g["L0_ffn_qweights"]
    data = {
        "x": g["x"].reshape(B * P, D),
        "ctxT": g["ctx_1024"].reshape(B * S2, D).T,
        "mask": g["mask_1x1xSxS2_ik0"].reshape(P, S2),
        "wqT": g["L0_xattn_Wq"].T, "wkT": g["L0_xattn_Wk"].T, "wvT": g["L0_xattn_Wv"].T, "woT": g["L0_xattn_Wo"].T,
        "bq": cols(g["L0_xattn_bq"]), "bk": cols(g["L0_xattn_bk"]), "bv": cols(g["L0_xattn_bv"]),
        "bo": g["L0_xattn_bo"],
        "aqT": g["L0_attn_Wq"].T, "akT": g["L0_attn_Wk"].T, "avT": av.T, "aoT": g["L0_attn_Wo"].T,
        "a_gamma": cols(g["L0_attn_gamma"]), "a_beta": cols(g["L0_attn_beta"]),
        "fqT": fq.transpose(0, 2, 1), "fsT": np.repeat(g["L0_ffn_scales"].transpose(0, 2, 1), 16, axis=1),
        "f_bias": g["L0_ffn_biases"],
        "f_la": g["L0_ffn_lora_a"], "f_lbT": g["L0_ffn_lora_b"].transpose(0, 2, 1),
        "f_gamma": g["L0_ffn_ln_gamma"].reshape(NBLK, KD, P).transpose(2, 0, 1),
        "f_beta": g["L0_ffn_ln_beta"].reshape(NBLK, KD, P).transpose(2, 0, 1),
    }
    arrays, args = {}, {}
    for name, a in data.items():
        a = np.ascontiguousarray(a)
        arrays["in_" + name] = a
        args[name] = nc.dram_tensor("in_" + name, a.shape, mybir.dt.from_np(a.dtype), kind="ExternalInput").ap()
    args["out"] = nc.dram_tensor("out", (B * P, D), F32, kind="ExternalOutput").ap()
    build(nc, **args)
    r = run_bass_kernel_spmd(nc, [arrays], core_ids=[0])
    return r.results[0]["out"].reshape(B, P, D)
```
